# Optimizing a Trainium2 kernel written in Bass

```python
import numpy as np
import jax
import jax.numpy as jnp

def _softmax(x, axis=-1):
    return jax.nn.softmax(x, axis=axis)

def _gelu(x):
    return jax.nn.gelu(x, approximate=True)

def _silu(x):
    return jax.nn.silu(x)

def _sigmoid(x):
    return jax.nn.sigmoid(x)

def _layernorm(x, axis=-1, eps=1e-05):
    m = jnp.mean(x, axis=axis, keepdims=True)
    v = jnp.var(x, axis=axis, keepdims=True)
    return (x - m) / jnp.sqrt(v + eps)

def _scatter_add(tgt, idx, src, axis=0):
    return tgt.at[idx].add(src)

def _segment_sum(src, seg, n):
    return jax.ops.segment_sum(src, seg, n)
kernel_name = 'mk_decoder_preln_d2_seqx_r8_c8678b'

def setup_inputs(seed: int=0):
    np.random.seed(seed)
    _w = jnp.asarray

    def _rec_inputs():
        import jax
        import jax.numpy as jnp
        _rk = jax.random.key(seed)
        x = 0.0001212 + 1 * jax.random.normal(jax.random.fold_in(_rk, 1), (64, 64, 256), jnp.float32)
        _lenS = 64 - jax.random.randint(jax.random.fold_in(_rk, 7), (64,), 0, max(1, 64 // 4) + 1, jnp.int32)
        _lenS2 = 64 - jax.random.randint(jax.random.fold_in(_rk, 8), (64,), 0, max(1, 64 // 4) + 1, jnp.int32)
        _ctx_2048P = jax.random.normal(jax.random.fold_in(_rk, 11), (64, 16, 256), jnp.float32)
        _ctx_2048c = jax.random.dirichlet(jax.random.fold_in(_rk, 511), 0.3 * jnp.ones((16,), jnp.float32), (64, 64))
        _ctx_2048t = jnp.einsum('bsk,bkd->bsd', _ctx_2048c, _ctx_2048P)
        _ctx_2048t = _ctx_2048t * jax.lax.rsqrt(jnp.mean(jnp.square(_ctx_2048t)) + 1e-12) * 0.953939
        ctx_2048 = 0.000173663 + 1.0001 * (_ctx_2048t + 0.3 * jax.random.normal(jax.random.fold_in(_rk, 611), (64, 64, 256), jnp.float32))
        return (x, ctx_2048)
    x, ctx_2048 = _rec_inputs()

    def _L0_attn_setup():
        import jax, jax.numpy as jnp
        import numpy as np
        from jax import lax
        B, L, D = (2, 256, 256)
        H, DK, DV, K = (16, 128, 128, 4)
        Q_DIM = H * DK
        V_DIM = H * DV

        def silu(x):
            return x * jax.nn.sigmoid(x)

        def causal_dwconv(x, w, b):
            Kk = w.shape[1]
            xp = jnp.pad(x, ((0, 0), (Kk - 1, 0), (0, 0)))
            kern = w.T[:, None, :]
            y = lax.conv_general_dilated(xp, kern, window_strides=(1,), padding='VALID', dimension_numbers=('NWC', 'WIO', 'NWC'), feature_group_count=w.shape[0])
            return y + b

        def layernorm(x, w, b, eps=1e-05):
            m = jnp.mean(x, axis=-1, keepdims=True)
            var = jnp.mean((x - m) ** 2, axis=-1, keepdims=True)
            return (x - m) * lax.rsqrt(var + eps) * w + b
        key = jax.random.key(seed)
        ks = jax.random.split(key, 16)
        s = 0.02
        f32 = jnp.float32
        return {'hidden_states': jax.random.normal(ks[0], (B, L, D), f32), 'Wq': jax.random.normal(ks[1], (D, Q_DIM), f32) * s, 'Wk': jax.random.normal(ks[2], (D, Q_DIM), f32) * s, 'Wv': jax.random.normal(ks[3], (D, V_DIM), f32) * s, 'Wb': jax.random.normal(ks[4], (D, H), f32) * s, 'bb': jnp.full((H,), -2.0, f32), 'Wg': jax.random.normal(ks[5], (D, V_DIM), f32) * s, 'Wo': jax.random.normal(ks[6], (V_DIM, D), f32) * s, 'qconv_w': jax.random.normal(ks[7], (Q_DIM, K), f32) * 0.5, 'qconv_b': jnp.zeros((Q_DIM,), f32), 'kconv_w': jax.random.normal(ks[8], (Q_DIM, K), f32) * 0.5, 'kconv_b': jnp.zeros((Q_DIM,), f32), 'qn_w': jnp.ones((DK,), f32), 'qn_b': jnp.zeros((DK,), f32), 'kn_w': jnp.ones((DK,), f32), 'kn_b': jnp.zeros((DK,), f32)}
    _L0_attn_all = _L0_attn_setup()
    _L0_attn_in = {k: v for k, v in _L0_attn_all.items() if k in ('Wq', 'Wk', 'Wv', 'Wb', 'bb', 'Wg', 'Wo', 'qconv_w', 'qconv_b', 'kconv_w', 'kconv_b', 'qn_w', 'qn_b', 'kn_w', 'kn_b')}
    del _L0_attn_all

    def _L0_xattn_setup():
        import jax, jax.numpy as jnp
        import numpy as np
        B_DIM, T_DIM, C_DIM = (16, 128, 256)

        def _wkv(w, u, k, v):
            Bn, Tn, Cn = k.shape
            NEG_INF = jnp.float32(-1e+38)

            def step(carry, kv_t):
                p, q, o = carry
                kt, vt = kv_t
                no = jnp.maximum(o, u + kt)
                A = jnp.exp(o - no)
                E = jnp.exp(u + kt - no)
                y = (A * p + E * vt) / (A * q + E)
                no2 = jnp.maximum(w + o, kt)
                A2 = jnp.exp(w + o - no2)
                E2 = jnp.exp(kt - no2)
                return ((A2 * p + E2 * vt, A2 * q + E2, no2), y)
            init = (jnp.zeros((Bn, Cn), k.dtype), jnp.zeros((Bn, Cn), k.dtype), jnp.full((Bn, Cn), NEG_INF, k.dtype))
            kT = jnp.moveaxis(k, 1, 0)
            vT = jnp.moveaxis(v, 1, 0)
            _, yT = jax.lax.scan(step, init, (kT, vT))
            return jnp.moveaxis(yT, 0, 1)
        key = jax.random.key(seed)
        k1, k2, k3, k4 = jax.random.split(key, 4)
        w = -jnp.exp(jax.random.normal(k1, (C_DIM,), jnp.float32))
        u = jax.random.normal(k2, (C_DIM,), jnp.float32)
        k = jax.random.normal(k3, (B_DIM, T_DIM, C_DIM), jnp.float32)
        v = jax.random.normal(k4, (B_DIM, T_DIM, C_DIM), jnp.float32)
        return {'B': B_DIM, 'T': T_DIM, 'C': C_DIM, 'w': w, 'u': u, 'k': k, 'v': v}
    _L0_xattn_all = _L0_xattn_setup()
    _L0_xattn_in = {k: v for k, v in _L0_xattn_all.items() if k in ('w', 'u')}
    del _L0_xattn_all

    def _L0_ffn_setup():
        import jax, jax.numpy as jnp
        import numpy as np
        ALPHA = 1.702
        LIMIT = 7.0
        TOP_K = 2
        E, H, I = (8, 256, 256)
        B, S = (2, 256)
        key = jax.random.key(seed)
        ks = jax.random.split(key, 7)
        return {'hidden_states': jax.random.normal(ks[0], (B, S, H), dtype=jnp.float32), 'router_weight': jax.random.normal(ks[1], (E, H), dtype=jnp.float32) * 0.02, 'router_bias': jax.random.normal(ks[2], (E,), dtype=jnp.float32) * 0.02, 'gate_up_proj': jax.random.normal(ks[3], (E, H, 2 * I), dtype=jnp.float32) * 0.02, 'gate_up_proj_bias': jax.random.normal(ks[4], (E, 2 * I), dtype=jnp.float32) * 0.02, 'down_proj': jax.random.normal(ks[5], (E, I, H), dtype=jnp.float32) * 0.02, 'down_proj_bias': jax.random.normal(ks[6], (E, H), dtype=jnp.float32) * 0.02}
    _L0_ffn_all = _L0_ffn_setup()
    _L0_ffn_in = {k: v for k, v in _L0_ffn_all.items() if k in ('router_weight', 'router_bias', 'gate_up_proj', 'gate_up_proj_bias', 'down_proj', 'down_proj_bias')}
    del _L0_ffn_all

    def _L1_attn_setup():
        import jax, jax.numpy as jnp
        import numpy as np
        N_HEADS = 16
        N_KV_HEADS = 4
        WINDOW = 128
        THETA = 10000.0

        def _rope_cos_sin(T, half):
            inv = 1.0 / THETA ** (jnp.arange(half, dtype=jnp.float32) / half)
            f = jnp.arange(T, dtype=jnp.float32)[:, None] * inv[None, :]
            return (jnp.cos(f), jnp.sin(f))

        def _apply_rope(x, cos, sin):
            xr, xi = (x[..., 0::2], x[..., 1::2])
            out_r = xr * cos - xi * sin
            out_i = xr * sin + xi * cos
            return jnp.stack([out_r, out_i], axis=-1).reshape(x.shape)
        key = jax.random.key(seed)
        ks = jax.random.split(key, 6)
        B, T, C = (1, 512, 256)
        kvC = C // N_HEADS * N_KV_HEADS
        return {'x': jax.random.normal(ks[0], (B, T, C), dtype=jnp.float32), 'wq': jax.random.normal(ks[1], (C, C), dtype=jnp.float32) * 0.02, 'wk': jax.random.normal(ks[2], (C, kvC), dtype=jnp.float32) * 0.02, 'wv': jax.random.normal(ks[3], (C, kvC), dtype=jnp.float32) * 0.02, 'wo': jax.random.normal(ks[4], (C, C), dtype=jnp.float32) * 0.02, 'sink': jnp.zeros((1, N_HEADS, 1, 1), dtype=jnp.float32)}
    _L1_attn_all = _L1_attn_setup()
    _L1_attn_in = {k: v for k, v in _L1_attn_all.items() if k in ('wq', 'wk', 'wv', 'wo', 'sink')}
    del _L1_attn_all

    def _L1_xattn_setup():
        import jax, jax.numpy as jnp
        import numpy as np
        B, S, D, H = (4, 512, 256, 16)
        HD = D // H
        key = jax.random.key(seed)
        ks = jax.random.split(key, 12)
        sc = 1.0 / np.sqrt(D)
        inp = {'q': jax.random.normal(ks[0], (B, S, D), jnp.float32), 'k': jax.random.normal(ks[1], (B, S, D), jnp.float32), 'v': jax.random.normal(ks[2], (B, S, D), jnp.float32), 'Wq': jax.random.normal(ks[3], (D, D), jnp.float32) * sc, 'bq': jnp.zeros((D,), jnp.float32), 'Wk': jax.random.normal(ks[4], (D, D), jnp.float32) * sc, 'bk': jnp.zeros((D,), jnp.float32), 'Wv': jax.random.normal(ks[5], (D, D), jnp.float32) * sc, 'bv': jnp.zeros((D,), jnp.float32), 'Wo': jax.random.normal(ks[6], (D, D), jnp.float32) * sc, 'bo': jnp.zeros((D,), jnp.float32)}
        return inp
    _L1_xattn_all = _L1_xattn_setup()
    _L1_xattn_in = {k: v for k, v in _L1_xattn_all.items() if k in ('Wq', 'bq', 'Wk', 'bk', 'Wv', 'bv', 'Wo', 'bo')}
    del _L1_xattn_all

    def _L1_ffn_setup():
        import jax, jax.numpy as jnp
        import numpy as np
        B_, S, D = (2, 256, 256)
        F_ = 1024
        R = 16
        H = 16
        HD = D // H
        MOD_SCALE = 0.1
        EPS = 1e-06

        def _rmsnorm(x, w):
            v = jnp.mean(x * x, axis=-1, keepdims=True)
            return x * jax.lax.rsqrt(v + EPS) * w

        def _attention(x, Wq, Wk, Wv, Wo):
            b, s, d = x.shape
            q = (x @ Wq.T).reshape(b, s, H, HD)
            k = (x @ Wk.T).reshape(b, s, H, HD)
            v = (x @ Wv.T).reshape(b, s, H, HD)
            scores = jnp.einsum('bqhd,bkhd->bhqk', q, k) / np.sqrt(HD).astype(np.float32)
            causal = jnp.tril(jnp.ones((s, s), bool))
            scores = jnp.where(causal, scores, jnp.finfo(scores.dtype).min)
            probs = jax.nn.softmax(scores, axis=-1)
            out = jnp.einsum('bhqk,bkhd->bqhd', probs, v).reshape(b, s, d)
            return out @ Wo.T
        key = jax.random.key(seed)
        ks = jax.random.split(key, 12)
        sd = 0.02
        return {'hidden_states': jax.random.normal(ks[0], (B_, S, D), jnp.float32), 'ln1_w': jnp.ones((D,), jnp.float32), 'ln2_w': jnp.ones((D,), jnp.float32), 'Wq': jax.random.normal(ks[1], (D, D), jnp.float32) * sd, 'Wk': jax.random.normal(ks[2], (D, D), jnp.float32) * sd, 'Wv': jax.random.normal(ks[3], (D, D), jnp.float32) * sd, 'Wo': jax.random.normal(ks[4], (D, D), jnp.float32) * sd, 'A': jax.random.normal(ks[5], (D, R), jnp.float32) * (0.01 / np.sqrt(D)), 'B': jax.random.normal(ks[6], (R, F_), jnp.float32) * (0.01 / np.sqrt(R)), 'W_in_base': jax.random.normal(ks[7], (F_, D), jnp.float32) * sd, 'W_up_base': jax.random.normal(ks[8], (F_, D), jnp.float32) * sd, 'W_down': jax.random.normal(ks[9], (D, F_), jnp.float32) * sd}
    _L1_ffn_all = _L1_ffn_setup()
    _L1_ffn_in = {k: v for k, v in _L1_ffn_all.items() if k in ('ln1_w', 'ln2_w', 'Wq', 'Wk', 'Wv', 'Wo', 'A', 'B', 'W_in_base', 'W_up_base', 'W_down')}
    del _L1_ffn_all
    return {'x': x, 'ctx_2048': ctx_2048, 'L0_attn_Wq': _L0_attn_in['Wq'], 'L0_attn_Wk': _L0_attn_in['Wk'], 'L0_attn_Wv': _L0_attn_in['Wv'], 'L0_attn_Wb': _L0_attn_in['Wb'], 'L0_attn_bb': _L0_attn_in['bb'], 'L0_attn_Wg': _L0_attn_in['Wg'], 'L0_attn_Wo': _L0_attn_in['Wo'], 'L0_attn_qconv_w': _L0_attn_in['qconv_w'], 'L0_attn_qconv_b': _L0_attn_in['qconv_b'], 'L0_attn_kconv_w': _L0_attn_in['kconv_w'], 'L0_attn_kconv_b': _L0_attn_in['kconv_b'], 'L0_attn_qn_w': _L0_attn_in['qn_w'], 'L0_attn_qn_b': _L0_attn_in['qn_b'], 'L0_attn_kn_w': _L0_attn_in['kn_w'], 'L0_attn_kn_b': _L0_attn_in['kn_b'], 'L0_xattn_w': _L0_xattn_in['w'], 'L0_xattn_u': _L0_xattn_in['u'], 'L0_ffn_router_weight': _L0_ffn_in['router_weight'], 'L0_ffn_router_bias': _L0_ffn_in['router_bias'], 'L0_ffn_gate_up_proj': _L0_ffn_in['gate_up_proj'], 'L0_ffn_gate_up_proj_bias': _L0_ffn_in['gate_up_proj_bias'], 'L0_ffn_down_proj': _L0_ffn_in['down_proj'], 'L0_ffn_down_proj_bias': _L0_ffn_in['down_proj_bias'], 'L1_attn_wq': _L1_attn_in['wq'], 'L1_attn_wk': _L1_attn_in['wk'], 'L1_attn_wv': _L1_attn_in['wv'], 'L1_attn_wo': _L1_attn_in['wo'], 'L1_attn_sink': _L1_attn_in['sink'], 'L1_xattn_Wq': _L1_xattn_in['Wq'], 'L1_xattn_bq': _L1_xattn_in['bq'], 'L1_xattn_Wk': _L1_xattn_in['Wk'], 'L1_xattn_bk': _L1_xattn_in['bk'], 'L1_xattn_Wv': _L1_xattn_in['Wv'], 'L1_xattn_bv': _L1_xattn_in['bv'], 'L1_xattn_Wo': _L1_xattn_in['Wo'], 'L1_xattn_bo': _L1_xattn_in['bo'], 'L1_ffn_ln1_w': _L1_ffn_in['ln1_w'], 'L1_ffn_ln2_w': _L1_ffn_in['ln2_w'], 'L1_ffn_Wq': _L1_ffn_in['Wq'], 'L1_ffn_Wk': _L1_ffn_in['Wk'], 'L1_ffn_Wv': _L1_ffn_in['Wv'], 'L1_ffn_Wo': _L1_ffn_in['Wo'], 'L1_ffn_A': _L1_ffn_in['A'], 'L1_ffn_B': _L1_ffn_in['B'], 'L1_ffn_W_in_base': _L1_ffn_in['W_in_base'], 'L1_ffn_W_up_base': _L1_ffn_in['W_up_base'], 'L1_ffn_W_down': _L1_ffn_in['W_down']}

def reference(x, ctx_2048, L0_attn_Wq, L0_attn_Wk, L0_attn_Wv, L0_attn_Wb, L0_attn_bb, L0_attn_Wg, L0_attn_Wo, L0_attn_qconv_w, L0_attn_qconv_b, L0_attn_kconv_w, L0_attn_kconv_b, L0_attn_qn_w, L0_attn_qn_b, L0_attn_kn_w, L0_attn_kn_b, L0_xattn_w, L0_xattn_u, L0_ffn_router_weight, L0_ffn_router_bias, L0_ffn_gate_up_proj, L0_ffn_gate_up_proj_bias, L0_ffn_down_proj, L0_ffn_down_proj_bias, L1_attn_wq, L1_attn_wk, L1_attn_wv, L1_attn_wo, L1_attn_sink, L1_xattn_Wq, L1_xattn_bq, L1_xattn_Wk, L1_xattn_bk, L1_xattn_Wv, L1_xattn_bv, L1_xattn_Wo, L1_xattn_bo, L1_ffn_ln1_w, L1_ffn_ln2_w, L1_ffn_Wq, L1_ffn_Wk, L1_ffn_Wv, L1_ffn_Wo, L1_ffn_A, L1_ffn_B, L1_ffn_W_in_base, L1_ffn_W_up_base, L1_ffn_W_down):
    import jax
    import jax.numpy as jnp

    def _L0_attn_ref(hidden_states, Wq, Wk, Wv, Wb, bb, Wg, Wo, qconv_w, qconv_b, kconv_w, kconv_b, qn_w, qn_b, kn_w, kn_b):
        import jax, jax.numpy as jnp
        import numpy as np
        from jax import lax
        B, L, D = (2, 256, 256)
        H, DK, DV, K = (16, 128, 128, 4)
        Q_DIM = H * DK
        V_DIM = H * DV

        def silu(x):
            return x * jax.nn.sigmoid(x)

        def causal_dwconv(x, w, b):
            Kk = w.shape[1]
            xp = jnp.pad(x, ((0, 0), (Kk - 1, 0), (0, 0)))
            kern = w.T[:, None, :]
            y = lax.conv_general_dilated(xp, kern, window_strides=(1,), padding='VALID', dimension_numbers=('NWC', 'WIO', 'NWC'), feature_group_count=w.shape[0])
            return y + b

        def layernorm(x, w, b, eps=1e-05):
            m = jnp.mean(x, axis=-1, keepdims=True)
            var = jnp.mean((x - m) ** 2, axis=-1, keepdims=True)
            return (x - m) * lax.rsqrt(var + eps) * w + b
        Bs, Ls, Ds = hidden_states.shape
        q = hidden_states @ Wq
        k = hidden_states @ Wk
        v = hidden_states @ Wv
        beta = jax.nn.sigmoid(hidden_states @ Wb + bb)
        gate = silu(hidden_states @ Wg)
        q = silu(causal_dwconv(q, qconv_w, qconv_b))
        k = silu(causal_dwconv(k, kconv_w, kconv_b))
        q = layernorm(q.reshape(Bs, Ls, H, DK), qn_w, qn_b)
        k = layernorm(k.reshape(Bs, Ls, H, DK), kn_w, kn_b)
        v = v.reshape(Bs, Ls, H, DV)
        qs = q.transpose(1, 0, 2, 3)
        ks_ = k.transpose(1, 0, 2, 3)
        vs = v.transpose(1, 0, 2, 3)
        bs = beta.transpose(1, 0, 2)
        S0 = jnp.zeros((Bs, H, DV, DK), hidden_states.dtype)

        def step(S, inp):
            q_t, k_t, v_t, b_t = inp
            b = b_t[..., None, None]
            S = (1.0 - b) * S + b * (v_t[..., :, None] * k_t[..., None, :])
            o_t = jnp.einsum('bhvk,bhk->bhv', S, q_t)
            return (S, o_t)
        _, os = lax.scan(step, S0, (qs, ks_, vs, bs))
        o = os.transpose(1, 0, 2, 3).reshape(Bs, Ls, H * DV)
        o = o * gate
        return o @ Wo

    def _L0_xattn_ref(B, T, C, w, u, k, v):
        import jax, jax.numpy as jnp
        import numpy as np
        B_DIM, T_DIM, C_DIM = (16, 128, 256)

        def _wkv(w, u, k, v):
            Bn, Tn, Cn = k.shape
            NEG_INF = jnp.float32(-1e+38)

            def step(carry, kv_t):
                p, q, o = carry
                kt, vt = kv_t
                no = jnp.maximum(o, u + kt)
                A = jnp.exp(o - no)
                E = jnp.exp(u + kt - no)
                y = (A * p + E * vt) / (A * q + E)
                no2 = jnp.maximum(w + o, kt)
                A2 = jnp.exp(w + o - no2)
                E2 = jnp.exp(kt - no2)
                return ((A2 * p + E2 * vt, A2 * q + E2, no2), y)
            init = (jnp.zeros((Bn, Cn), k.dtype), jnp.zeros((Bn, Cn), k.dtype), jnp.full((Bn, Cn), NEG_INF, k.dtype))
            kT = jnp.moveaxis(k, 1, 0)
            vT = jnp.moveaxis(v, 1, 0)
            _, yT = jax.lax.scan(step, init, (kT, vT))
            return jnp.moveaxis(yT, 0, 1)
        return _wkv(w, u, k, v)

    def _L0_ffn_ref(hidden_states, router_weight, router_bias, gate_up_proj, gate_up_proj_bias, down_proj, down_proj_bias):
        import jax, jax.numpy as jnp
        import numpy as np
        ALPHA = 1.702
        LIMIT = 7.0
        TOP_K = 2
        E, H, I = (8, 256, 256)
        B, S = (2, 256)
        bsz, seq_len, hidden = hidden_states.shape
        h = hidden_states.reshape(-1, hidden)
        T = h.shape[0]
        logits = h @ router_weight.T + router_bias
        top_vals, top_idx = jax.lax.top_k(logits, TOP_K)
        top_w = jax.nn.softmax(top_vals, axis=-1)
        scores = jnp.zeros_like(logits).at[jnp.arange(T)[:, None], top_idx].set(top_w)
        gate_up = jnp.einsum('th,ehj->etj', h, gate_up_proj) + gate_up_proj_bias[:, None, :]
        gate = gate_up[..., ::2]
        up = gate_up[..., 1::2]
        gate = jnp.minimum(gate, LIMIT)
        up = jnp.clip(up, -LIMIT, LIMIT)
        glu = gate * jax.nn.sigmoid(gate * ALPHA)
        act = (up + 1.0) * glu
        expert_out = jnp.einsum('eti,eih->eth', act, down_proj) + down_proj_bias[:, None, :]
        out = jnp.einsum('te,eth->th', scores, expert_out)
        return out.reshape(bsz, seq_len, hidden)

    def _L1_attn_ref(x, wq, wk, wv, wo, sink):
        import jax, jax.numpy as jnp
        import numpy as np
        N_HEADS = 16
        N_KV_HEADS = 4
        WINDOW = 128
        THETA = 10000.0

        def _rope_cos_sin(T, half):
            inv = 1.0 / THETA ** (jnp.arange(half, dtype=jnp.float32) / half)
            f = jnp.arange(T, dtype=jnp.float32)[:, None] * inv[None, :]
            return (jnp.cos(f), jnp.sin(f))

        def _apply_rope(x, cos, sin):
            xr, xi = (x[..., 0::2], x[..., 1::2])
            out_r = xr * cos - xi * sin
            out_i = xr * sin + xi * cos
            return jnp.stack([out_r, out_i], axis=-1).reshape(x.shape)
        B, T, C = x.shape
        hd = C // N_HEADS
        n_rep = N_HEADS // N_KV_HEADS
        q = (x @ wq).reshape(B, T, N_HEADS, hd).transpose(0, 2, 1, 3)
        k = (x @ wk).reshape(B, T, N_KV_HEADS, hd).transpose(0, 2, 1, 3)
        v = (x @ wv).reshape(B, T, N_KV_HEADS, hd).transpose(0, 2, 1, 3)
        cos, sin = _rope_cos_sin(T, hd // 2)
        q = _apply_rope(q, cos, sin)
        k = _apply_rope(k, cos, sin)
        k = jnp.repeat(k, n_rep, axis=1)
        v = jnp.repeat(v, n_rep, axis=1)
        att = jnp.einsum('bhqd,bhkd->bhqk', q, k) * hd ** (-0.5) + sink
        idx = jnp.arange(T)
        band = jnp.abs(idx[:, None] - idx[None, :]) <= WINDOW // 2
        att = jnp.where(band[None, None, :, :], att, -jnp.inf)
        att = jax.nn.softmax(att, axis=-1)
        att = jnp.where(jnp.isnan(att), 1.0 / T, att)
        out = jnp.einsum('bhqk,bhkd->bqhd', att, v).reshape(B, T, C)
        return out @ wo

    def _L1_xattn_ref(q, k, v, Wq, bq, Wk, bk, Wv, bv, Wo, bo):
        import jax, jax.numpy as jnp
        import numpy as np
        B, S, D, H = (4, 512, 256, 16)
        HD = D // H
        bs, sl, nf = q.shape
        Q = (q @ Wq.T + bq).reshape(bs, sl, H, HD)
        K = (k @ Wk.T + bk).reshape(bs, sl, H, HD)
        V = (v @ Wv.T + bv).reshape(bs, sl, H, HD)
        score = jnp.einsum('bshd,bsgd->bshg', Q, K)
        weight = jax.nn.softmax(score, axis=-1)
        attn = jnp.einsum('bshg,bsgd->bshd', weight, V).reshape(bs, sl, nf)
        return attn @ Wo.T + bo

    def _L1_ffn_ref(hidden_states, ln1_w, ln2_w, Wq, Wk, Wv, Wo, A, B, W_in_base, W_up_base, W_down):
        import jax, jax.numpy as jnp
        import numpy as np
        B_, S, D = (2, 256, 256)
        F_ = 1024
        R = 16
        H = 16
        HD = D // H
        MOD_SCALE = 0.1
        EPS = 1e-06

        def _rmsnorm(x, w):
            v = jnp.mean(x * x, axis=-1, keepdims=True)
            return x * jax.lax.rsqrt(v + EPS) * w

        def _attention(x, Wq, Wk, Wv, Wo):
            b, s, d = x.shape
            q = (x @ Wq.T).reshape(b, s, H, HD)
            k = (x @ Wk.T).reshape(b, s, H, HD)
            v = (x @ Wv.T).reshape(b, s, H, HD)
            scores = jnp.einsum('bqhd,bkhd->bhqk', q, k) / np.sqrt(HD).astype(np.float32)
            causal = jnp.tril(jnp.ones((s, s), bool))
            scores = jnp.where(causal, scores, jnp.finfo(scores.dtype).min)
            probs = jax.nn.softmax(scores, axis=-1)
            out = jnp.einsum('bhqk,bkhd->bqhd', probs, v).reshape(b, s, d)
            return out @ Wo.T
        residual = hidden_states
        x = _rmsnorm(hidden_states, ln1_w)
        attn = _attention(x, Wq, Wk, Wv, Wo)
        mod = MOD_SCALE * jnp.tanh(attn @ A)
        h = _rmsnorm(residual, ln2_w)
        gate_pre = h @ W_in_base.T + mod * (h @ A) @ B
        gate = jax.nn.silu(gate_pre)
        up = h @ W_up_base.T
        mlp_out = gate * up @ W_down.T
        return residual + mlp_out
    x = x + _L0_attn_ref(_layernorm(x, axis=-1), L0_attn_Wq, L0_attn_Wk, L0_attn_Wv, L0_attn_Wb, L0_attn_bb, L0_attn_Wg, L0_attn_Wo, L0_attn_qconv_w, L0_attn_qconv_b, L0_attn_kconv_w, L0_attn_kconv_b, L0_attn_qn_w, L0_attn_qn_b, L0_attn_kn_w, L0_attn_kn_b)
    x = x + _L0_xattn_ref(64, 64, 256, L0_xattn_w, L0_xattn_u, _layernorm(x, axis=-1), ctx_2048)
    x = x + _L0_ffn_ref(_layernorm(x, axis=-1), L0_ffn_router_weight, L0_ffn_router_bias, L0_ffn_gate_up_proj, L0_ffn_gate_up_proj_bias, L0_ffn_down_proj, L0_ffn_down_proj_bias)
    x = x + _L1_attn_ref(_layernorm(x, axis=-1), L1_attn_wq, L1_attn_wk, L1_attn_wv, L1_attn_wo, L1_attn_sink)
    x = x + _L1_xattn_ref(_layernorm(x, axis=-1), ctx_2048, ctx_2048, L1_xattn_Wq, L1_xattn_bq, L1_xattn_Wk, L1_xattn_bk, L1_xattn_Wv, L1_xattn_bv, L1_xattn_Wo, L1_xattn_bo)
    x = x + _L1_ffn_ref(_layernorm(x, axis=-1), L1_ffn_ln1_w, L1_ffn_ln2_w, L1_ffn_Wq, L1_ffn_Wk, L1_ffn_Wv, L1_ffn_Wo, L1_ffn_A, L1_ffn_B, L1_ffn_W_in_base, L1_ffn_W_up_base, L1_ffn_W_down)
    return x

_drawn_inputs = setup_inputs


def setup_inputs(seed=0):
    import zlib

    import numpy as np

    out = dict(_drawn_inputs(seed))
    spreads = {'L0_attn_bb': (-2.0, 0.2),
     'L0_attn_qconv_b': (0.0, 0.1),
     'L0_attn_kconv_b': (0.0, 0.1),
     'L0_attn_qn_w': (1.0, 0.2),
     'L0_attn_qn_b': (0.0, 0.553),
     'L0_attn_kn_w': (1.0, 0.2),
     'L0_attn_kn_b': (0.0, 0.543),
     'L1_attn_sink': (0.0, 2.0),
     'L1_xattn_bq': (0.0, 0.1),
     'L1_xattn_bk': (0.0, 0.1),
     'L1_xattn_bv': (0.0, 0.1),
     'L1_xattn_bo': (0.0, 0.1),
     'L1_ffn_ln1_w': (1.0, 0.6),
     'L1_ffn_ln2_w': (1.0, 0.6)}
    factors = {'L0_ffn_router_bias': 6.749,
     'L0_ffn_gate_up_proj_bias': 8.0,
     'L0_ffn_down_proj_bias': 4.173,
     'L1_attn_wq': 8.0,
     'L1_attn_wk': 8.0,
     'L1_ffn_Wq': 64.0,
     'L1_ffn_Wk': 64.0,
     'L1_ffn_Wv': 64.0,
     'L1_ffn_Wo': 64.0,
     'L1_ffn_A': 64.0,
     'L1_ffn_B': 64.0,
     'L1_ffn_W_in_base': 3.978,
     'L1_ffn_W_up_base': 3.926,
     'L1_ffn_W_down': 3.933}
    for name, (base, spread) in spreads.items():
        noise = np.random.default_rng([zlib.crc32(name.encode()), seed]).standard_normal(out[name].shape)
        drawn = base * np.exp(spread * noise) if base else spread * noise
        out[name] = jnp.asarray(drawn.astype(out[name].dtype))
    for name, factor in factors.items():
        out[name] = (out[name] * factor).astype(out[name].dtype)
    return out
```

```python
from contextlib import ExitStack

import concourse.bass as bass
from concourse import mybir

F32 = mybir.dt.float32
BF16 = mybir.dt.bfloat16
ALU = mybir.AluOpType
ACT = mybir.ActivationFunctionType

P = 128
SEQ = 64
SEQS = 64
D = 256
DC = D // P
TOK = SEQS * SEQ
TILES = TOK // P
BT = 4
BLK = BT * P
BLOCKS = TOK // BLK
H0 = 16
KW = 4
LN_EPS = 1e-5


def run_steps(eng, step):
    pairs = H0 // 2

    def one_block(b, final):
        for par in range(2):
            step(b * pairs, par, b, 0, True, False, final)
        with eng.Fori(1, pairs - 1) as hp:
            for par in range(2):
                step(b * pairs + hp, par, b, hp, False, False, final)
        for par in range(2):
            step(b * pairs + pairs - 1, par, b, pairs - 1, False, True, final)

    one_block(0, False)
    with eng.Fori(1, BLOCKS - 1) as b:
        one_block(b, False)
    one_block(BLOCKS - 1, True)


def emit_masks(nc, pool, made, ident, tri, tri_strict, mask4):
    count = 0

    def done(ins):
        nonlocal count
        ins.then_inc(made, 1)
        count += 1
        pool.wait_ge(made, count)

    def select(view, op, base, pattern, mult, fill):
        done(nc.gpsimd.affine_select(out=view, in_=view, compare_op=op, fill=fill, base=base, pattern=pattern,
                                     channel_multiplier=mult))

    done(nc.gpsimd.memset(ident[:], 0.0))
    select(ident[:], ALU.not_equal, 0, [[-1, P]], 1, 1.0)
    for m in (tri, tri_strict, mask4):
        done(nc.gpsimd.memset(m[:], 1.0))
    select(tri[:], ALU.is_ge, 0, [[1, P]], -1, 0.0)
    select(mask4[:], ALU.is_ge, 0, [[0, BT], [1, P]], -1, 0.0)
    select(tri_strict[:], ALU.is_gt, 0, [[0, BT], [-1, P]], 1, 0.0)
    select(tri[:, SEQ:], ALU.is_ge, -SEQ, [[0, SEQ]], 1, 0.0)
    select(mask4[:, :, SEQ:], ALU.is_ge, -SEQ, [[0, BT], [0, SEQ]], 1, 0.0)
    select(tri_strict[:, :, 0:SEQ], ALU.is_gt, SEQ, [[0, BT], [0, SEQ]], -1, 0.0)


def linear_attention(nc, new_sem, x_sb, ident, tri, tri_strict, mask4, w_qk, w_vg, w_o, w_beta, b_beta, ln_cols):
    NW = 2 * DC * P
    TAPQ, TAPK, BQ, BK = NW, NW + KW, NW + 2 * KW, NW + 2 * KW + 1
    PAIRS = H0 // 2
    with ExitStack() as ctx:
        def sb(name, shape, dt=F32):
            return ctx.enter_context(nc.sbuf_tensor("a_" + name, shape, dt))

        def two(name, shape):
            return [sb(f"{name}{i}", shape) for i in range(2)]

        def psum(name, shape, dt=F32):
            return ctx.enter_context(nc.psum_tensor("a_" + name, shape, dt))

        def sem(name):
            return new_sem("a_" + name)

        wqk = two("wqk", [P, NW + 2 * KW + 2])
        wvg = two("wvg", [P, NW])
        wo = two("wo", [P, D])
        wbeta, bbeta, lncol = sb("wbeta", [P, DC, H0]), sb("bbeta", [P, H0]), sb("lncol", [P, 4])
        neghalf = sb("neghalf", [P, TILES])
        xnT = sb("xnT", [P, DC, TOK])
        xv = sb("xv", [P, DC, BLK])
        st, mv = sb("st", [P, TILES, 6]), sb("mv", [P, TILES, 2])
        ve, rs = sb("ve", [P, TILES]), sb("rs", [P, TILES])
        z, u1, u2, spz = (sb(n, [P, TILES, H0]) for n in ("z", "u1", "u2", "spz"))
        lnd, beta = sb("lnd", [P, TILES, H0]), sb("beta", [P, TILES, H0])
        cq, ck, tq, tk, sq, sk = (two(n, [P, BLK]) for n in ("cq", "ck", "tq", "tk", "sq", "sk"))
        qn, kn, qh, kh = two("qn", [P, BT, P]), two("kn", [P, BT, P]), two("qh", [P, BLK]), two("kh", [P, BLK])
        hst, hm = two("hst", [P, 2 * BT, 6]), two("hm", [P, 4, 2 * BT])
        hve, hrs, hnb = (two(n, [P, 2 * BT]) for n in ("hve", "hrs", "hnb"))
        vs, tg, gs = two("vs", [P, BT, P]), two("tg", [P, BLK]), two("gs", [P, BLK])
        dlt, mb, ex, em, at = (two(n, [P, BT, P]) for n in ("dlt", "mb", "ex", "em", "at"))
        og = two("og", [P, BLK])
        xn = cq[0][:], ck[0][:], tq[0][:], tk[0][:]

        QK = [psum(f"QK{i}", [P, 2, BLK]) for i in range(2)]
        X0, X1, Y = psum("X0", [P, BLK]), psum("X1", [P, BLK]), psum("Y", [P, BT, D])

        wqk_in, wvg_in, wo_in = ([sem(f"{n}{i}") for i in range(2)] for n in ("wqk_in", "wvg_in", "wo_in"))
        const_in, const_set = sem("const_in"), sem("const_set")
        xstat, xvar, xrstd, xnorm, xT, xvc, xTc, zmm, zc, zmath, zact, xv_set = (sem(n) for n in (
            "xstat", "xvar", "xrstd", "xnorm", "xT", "xvc", "xTc", "zmm", "zc", "zmath", "zact", "xv_set"))
        s_qk, s_fwd, s_arg, s_g, s_v, s_bck, s_s, s_y, s_o = (sem(n) for n in (
            "qk", "fwd", "arg", "g", "v", "bck", "s", "y", "o"))
        s_ex, s_tap0, s_norm, s_tg, s_vc, s_tanh, s_qkh = (sem(n) for n in (
            "ex", "tap0", "norm", "tg", "vc", "tanh", "qkh"))
        s_hstat, s_hmath, s_hvar, s_hnb, s_conv, s_silu, s_gs, s_at, s_og, s_yout = (sem(n) for n in (
            "hstat", "hmath", "hvar", "hnb", "conv", "silu", "gs", "at", "og", "yout"))
        s_em, s_hrstd, s_dl = sem("em"), sem("hrstd"), sem("dl")
        block = ctx.enter_context(nc.Block())

        @block.sync
        def _(sp):
            for dst, src in ((wbeta[:], w_beta), (bbeta[:], b_beta), (lncol[:], ln_cols)):
                sp.dma_start(dst, src).then_inc(const_in, 16)

            def load_qk(row, p):
                sp.dma_start(wqk[p][:], w_qk[row, :, :]).then_inc(wqk_in[p], 16)

            def load_vg(row, p):
                sp.dma_start(wvg[p][:], w_vg[row, :, :]).then_inc(wvg_in[p], 16)

            def load_o(row, p):
                sp.dma_start(wo[p][:], w_o[row, :, :]).then_inc(wo_in[p], 16)

            load_qk(0, 0)
            load_qk(1, 1)
            load_vg(0, 0)
            load_o(0, 0)
            sp.wait_ge(s_conv, 6)
            load_qk(2, 0)

            def ahead(g, hp, par):
                n = 2 * g + par
                sp.wait_ge(s_conv, 6 * n + 12)
                load_qk(bass.ds(2 * hp + par + 3, 1), 1 - par)
                sp.wait_ge(s_v, n)
                load_vg(bass.ds(2 * hp + par + 1, 1), 1 - par)
                sp.wait_ge(s_y, n)
                load_o(bass.ds(2 * hp + par + 1, 1), 1 - par)

            for par in range(2):
                ahead(0, 0, par)
            with sp.Fori(1, PAIRS) as hp:
                for par in range(2):
                    ahead(hp, hp, par)
            with sp.Fori(1, BLOCKS - 1) as b:
                with sp.Fori(0, PAIRS) as hp:
                    for par in range(2):
                        ahead(b * PAIRS + hp, hp, par)
            with sp.Fori(0, PAIRS - 1) as hp:
                for par in range(2):
                    ahead((BLOCKS - 1) * PAIRS + hp, hp, par)
            n = BLOCKS * H0 - 2
            sp.wait_ge(s_v, n)
            load_vg(H0 - 1, 1)
            sp.wait_ge(s_y, n)
            load_o(H0 - 1, 1)
            sp.wait_ge(wqk_in[0], 16 * (BLOCKS * PAIRS + 1))

        @block.gpsimd
        def _(pool):
            nc.gpsimd.memset(neghalf[:], -0.5).then_inc(const_set, 1)
            pool.wait_ge(const_set, 1)
            pool.wait_ge(xvar, 1)
            nc.gpsimd.tensor_tensor(out=rs[:], in0=ve[:], in1=neghalf[:], op=ALU.pow).then_inc(xrstd, 1)

            def rstd(m, p):
                pool.wait_ge(s_hvar, m + 1)
                nc.gpsimd.tensor_tensor(out=hrs[p][:], in0=hve[p][:], in1=neghalf[:, 0:2 * BT], op=ALU.pow).then_inc(s_hrstd, 1)

            def decay(m, p, blk, head):
                tiles = bass.ds(blk * BT, BT)
                pool.wait_ge(s_dl, 2 * m)
                nc.gpsimd.tensor_tensor(out=dlt[p][:], in0=tri_strict, in1=lnd[:, tiles, bass.ds(head, 1)].to_broadcast([P, BT, P]),
                                        op=ALU.mult).then_inc(s_dl, 1)
                nc.gpsimd.tensor_tensor(out=mb[p][:], in0=mask4, in1=beta[:, tiles, bass.ds(head, 1)].to_broadcast([P, BT, P]),
                                        op=ALU.mult).then_inc(s_dl, 1)

            def copy_block(blk):
                pool.wait_ge(s_v, blk * H0)
                nc.gpsimd.tensor_copy(xv[:], xnT[:, :, bass.ds(blk * BLK, BLK)]).then_inc(xv_set, 1)

            def step(g, par, b, hp, first, last, final):
                n = 2 * g + par
                pool.wait_ge(s_ex, n + 1)
                pool.wait_ge(s_dl, 2 * n + 2)
                pool.wait_ge(s_at, n)
                nc.gpsimd.tensor_tensor(out=em[par][:], in0=ex[par][:], in1=mb[par][:], op=ALU.mult).then_inc(s_em, 1)
                if final and last and par == 1:
                    return
                cross = last and par == 1
                pool.wait_ge(s_norm, 8 * n + 8)
                rstd(n + 1, 1 - par)
                pool.wait_ge(s_em, n + 1)
                decay(n + 1, 1 - par, b + 1 if cross else b, 0 if cross else 2 * hp + par + 1)
                if cross:
                    copy_block(b + 1)

            pool.wait_ge(zact, 3)
            pool.wait_ge(zmath, 4)
            pool.wait_ge(xTc, 2 * BLOCKS)
            pool.wait_ge(zmm, BLOCKS)
            decay(0, 0, 0, 0)
            rstd(0, 0)
            copy_block(0)
            run_steps(pool, step)

        @block.tensor
        def _(pe):
            pe.wait_ge(const_in, 48)

            def transpose_block(b, p):
                for i in range(BT):
                    pe.wait_ge(xnorm, 4 * b + i + 1)
                    for c in range(DC):
                        last = nc.tensor.transpose(QK[p][:, c, i * P:(i + 1) * P], xn[i][:, c * P:(c + 1) * P], ident)
                    last.then_inc(xT, 1)

            def beta_logits(bb):
                for p in range(2):
                    b = 2 * bb + p
                    pe.wait_ge(xTc, 4 * bb)
                    transpose_block(b, p)
                    pe.wait_ge(xvc, 2 * b + 2)
                    pe.wait_ge(zc, b)
                    for j in range(BT):
                        for c in range(DC):
                            last = nc.tensor.matmul(X0[:, j * H0:(j + 1) * H0], xv[:, c, j * P:(j + 1) * P], wbeta[:, c, :],
                                                    start=c == 0, stop=c == DC - 1)
                    last.then_inc(zmm, 1)

            beta_logits(0)
            with pe.Fori(1, BLOCKS // 2) as bb:
                beta_logits(bb)

            def proj_qk(m, p, arrived, blk):
                pe.wait_ge(wqk_in[p], arrived)
                for i in range(2):
                    for c in range(DC):
                        lo = (i * DC + c) * P
                        last = nc.tensor.matmul(QK[p][:, i, :], wqk[p][:, lo:lo + P], xnT[:, c, bass.ds(blk * BLK, BLK)],
                                                start=c == 0, stop=c == DC - 1)
                last.then_inc(s_qk, 1)

            def forward(m, p):
                pe.wait_ge(s_silu, 2 * m + 2)
                for i, s in enumerate((sq, sk)):
                    for j in range(BT):
                        last = nc.tensor.transpose(QK[p][:, i, j * P:(j + 1) * P], s[p][:, j * P:(j + 1) * P], ident)
                last.then_inc(s_fwd, 1)

            def back(m, p):
                pe.wait_ge(s_norm, 8 * m + 8)
                for i, s in enumerate((qn, kn)):
                    for j in range(BT):
                        last = nc.tensor.transpose(QK[p][:, i, j * P:(j + 1) * P], s[p][:, j, :], ident)
                last.then_inc(s_bck, 1)

            def out_proj(m, p, arrived, blk, starts):
                pe.wait_ge(wo_in[p], arrived)
                pe.wait_ge(s_og, m + 1)
                if starts:
                    pe.wait_ge(s_yout, 2 * blk)
                for j in range(BT):
                    last = nc.tensor.matmul(Y[:, j, :], og[p][:, j * P:(j + 1) * P], wo[p][:], start=starts and j % 2 == 0,
                                            stop=True, skip_group_check=True)
                last.then_inc(s_y, 1)

            def step(g, par, b, hp, first, last_pair, final):
                n = 2 * g + par
                q = 1 - par
                end = final and last_pair
                if not (end and par == 1):
                    forward(n + 1, q)
                pe.wait_ge(s_dl, 2 * n + 2)
                pe.wait_ge(s_at, n)
                for j in range(BT):
                    last = nc.tensor.matmul(X1[:, j * P:(j + 1) * P], dlt[par][:, j, :], tri, start=True, stop=True)
                last.then_inc(s_arg, 1)
                if not end:
                    pe.wait_ge(s_qkh, 2 * n + 2)
                    proj_qk(n + 2, par, 16 * (g + 2), b + 1 if last_pair else b)
                pe.wait_ge(wvg_in[par], 16 * (g + 1))
                pe.wait_ge(s_ex, n + 1)
                for c in range(DC):
                    lo = (DC + c) * P
                    last = nc.tensor.matmul(X1[:], wvg[par][:, lo:lo + P], xnT[:, c, bass.ds(b * BLK, BLK)], start=c == 0, stop=c == DC - 1)
                last.then_inc(s_g, 1)
                pe.wait_ge(s_og, n)
                if first and par == 0:
                    pe.wait_ge(xv_set, b + 1)
                for j in range(BT):
                    for c in range(DC):
                        last = nc.tensor.matmul(X0[:, j * P:(j + 1) * P], xv[:, c, j * P:(j + 1) * P], wvg[par][:, c * P:(c + 1) * P],
                                                start=c == 0, stop=c == DC - 1)
                last.then_inc(s_v, 1)
                if not (end and par == 1):
                    back(n + 1, q)
                pe.wait_ge(s_qkh, 2 * n + 2)
                pe.wait_ge(s_gs, n + 1)
                for j in range(BT):
                    last = nc.tensor.matmul(X1[:, j * P:(j + 1) * P], kh[par][:, j * P:(j + 1) * P],
                                            qh[par][:, j * P:(j + 1) * P], start=True, stop=True)
                last.then_inc(s_s, 1)
                if par == 1:
                    out_proj(n - 1, 0, 16 * (g + 1), b, first)
                elif not first:
                    out_proj(n - 1, 1, 16 * g, b, False)
                pe.wait_ge(s_at, n + 1)
                pe.wait_ge(s_vc, n + 1)
                for j in range(BT):
                    last = nc.tensor.matmul(X0[:, j * P:(j + 1) * P], vs[par][:, j, :], at[par][:, j, :], start=True, stop=True)
                last.then_inc(s_o, 1)
                if last_pair and par == 1:
                    out_proj(n, 1, 16 * (g + 1), b, False)

            proj_qk(0, 0, 16, 0)
            proj_qk(1, 1, 16, 0)
            forward(0, 0)
            back(0, 0)
            run_steps(pe, step)

        @block.scalar
        def _(act):
            def transposed(bb):
                for p in range(2):
                    b = 2 * bb + p
                    act.wait_ge(xT, 4 * b + 4)
                    act.wait_ge(zmm, b)
                    act.wait_ge(xTc, 2 * b)
                    nc.scalar.activation(xv[:], QK[p][:], ACT.Copy).then_inc(xvc, 2)
                    act.wait_ge(xvc, 2 * b + 2)
                    nc.scalar.activation(xnT[:, :, bass.ds(b * BLK, BLK)], xv[:], ACT.Copy).then_inc(xTc, 2)

            transposed(0)
            with act.Fori(1, BLOCKS // 2) as bb:
                transposed(bb)
            act.wait_ge(zmath, 1)
            nc.scalar.activation(u2[:], u1[:], ACT.Exp, scale=-1.0).then_inc(zact, 1)
            act.wait_ge(zact, 1)
            nc.scalar.activation(u1[:], u2[:], ACT.Ln, bias=1.0).then_inc(zact, 1)
            act.wait_ge(zmath, 4)
            nc.scalar.activation(beta[:], u2[:], ACT.Exp).then_inc(zact, 1)

            def front(m, p):
                act.wait_ge(s_qk, m + 1)
                for i, (c, tap, bias) in enumerate(((cq, TAPQ, BQ), (ck, TAPK, BK))):
                    nc.scalar.activation(c[p][:], QK[p][:, i, :], ACT.Identity, bias=wqk[p][:, bias:bias + 1],
                                         scale=wqk[p][:, tap + KW - 1:tap + KW]).then_inc(s_tap0, 1)

            def front_tanh(m, p):
                for i, (c, t) in enumerate(((cq, tq), (ck, tk))):
                    act.wait_ge(s_conv, 6 * m + 5 + i)
                    nc.scalar.activation(t[p][:], c[p][:], ACT.Tanh, scale=0.5).then_inc(s_tanh, 1)

            def normalise(m, p):
                act.wait_ge(s_hrstd, m + 1)
                act.wait_ge(s_hnb, m + 1)
                for i, s in enumerate((qn, kn)):
                    for j in range(BT):
                        k = i * BT + j
                        nc.scalar.activation(s[p][:, j, :], QK[p][:, i, j * P:(j + 1) * P], ACT.Identity,
                                             bias=hnb[p][:, k:k + 1], scale=hrs[p][:, k:k + 1]).then_inc(s_norm, 1)

            def leave(m, p):
                act.wait_ge(s_bck, m + 1)
                for i, h in enumerate((qh, kh)):
                    nc.scalar.activation(h[p][:], QK[p][:, i, :], ACT.Identity, bias=lncol[:, 2 * i + 1:2 * i + 2],
                                         scale=lncol[:, 2 * i:2 * i + 1]).then_inc(s_qkh, 1)

            def step(g, par, b, hp, first, last_pair, final):
                n = 2 * g + par
                q = 1 - par
                end = final and last_pair
                act.wait_ge(s_arg, n + 1)
                nc.scalar.activation(ex[par][:], X1[:], ACT.Exp).then_inc(s_ex, 1)
                if not end:
                    front(n + 2, par)
                if not (end and par == 1):
                    normalise(n + 1, q)
                act.wait_ge(s_g, n + 1)
                nc.scalar.activation(tg[par][:], X1[:], ACT.Tanh, scale=0.5).then_inc(s_tg, 1)
                act.wait_ge(s_v, n + 1)
                nc.scalar.activation(vs[par][:], X0[:], ACT.Copy).then_inc(s_vc, 1)
                if not end:
                    front_tanh(n + 2, par)
                if not (end and par == 1):
                    leave(n + 1, q)

            act.wait_ge(wqk_in[0], 16)
            act.wait_ge(wqk_in[1], 16)
            act.wait_ge(const_in, 48)
            front(0, 0)
            front_tanh(0, 0)
            front(1, 1)
            front_tanh(1, 1)
            normalise(0, 0)
            leave(0, 0)
            run_steps(act, step)

        @block.vector
        def _(dve):
            with dve.Fori(0, TILES) as t:
                nc.vector.bn_stats(st[:, bass.ds(t, 1), :], x_sb[:, bass.ds(t, 1), :]).then_inc(xstat, 1)
            dve.wait_ge(xstat, TILES)
            for t in range(TILES):
                nc.vector.bn_aggr(mv[:, t, :], st[:, t, :]).then_inc(xstat, 1)
            dve.wait_ge(xstat, 2 * TILES)
            nc.vector.tensor_scalar(ve[:], mv[:, :, 1], LN_EPS, None, ALU.add).then_inc(xvar, 1)
            dve.wait_ge(xrstd, 1)

            def normalise_block(b):
                dve.wait_ge(xT, 4 * b)
                for i in range(BT):
                    t = b * BT + i
                    nc.vector.tensor_scalar(xn[i][:, 0:D], x_sb[:, bass.ds(t, 1), :], mv[:, bass.ds(t, 1), 0:1], rs[:, bass.ds(t, 1)],
                                            ALU.subtract, ALU.mult).then_inc(xnorm, 1)
                dve.wait_ge(const_in, 48)
                dve.wait_ge(zmm, b + 1)
                nc.vector.tensor_tensor(out=z[:, bass.ds(b * BT, BT), :], in0=X0[:, 0:BT * H0].rearrange("p (j h) -> p j h", j=BT),
                                        in1=bbeta[:].unsqueeze(1).to_broadcast([P, BT, H0]), op=ALU.add).then_inc(zc, 1)

            normalise_block(0)
            with dve.Fori(1, BLOCKS) as b:
                normalise_block(b)
            dve.wait_ge(zc, BLOCKS)
            nc.vector.scalar_tensor_tensor(out=u1[:], in0=z[:], scalar=-1.0, in1=z[:], op0=ALU.mult, op1=ALU.max).then_inc(zmath, 1)
            dve.wait_ge(zact, 2)
            nc.vector.scalar_tensor_tensor(out=spz[:], in0=z[:], scalar=0.0, in1=u1[:], op0=ALU.max, op1=ALU.add).then_inc(zmath, 1)
            dve.wait_ge(zmath, 2)
            nc.vector.tensor_scalar(lnd[:], spz[:], -1.0, None, ALU.mult).then_inc(zmath, 1)
            nc.vector.tensor_tensor(out=u2[:], in0=z[:], in1=spz[:], op=ALU.subtract).then_inc(zmath, 1)

            def conv(m, p):
                for k in range(KW - 2, -1, -1):
                    back = KW - 1 - k
                    for i, (c, tap) in enumerate(((cq, TAPQ), (ck, TAPK))):
                        if k == KW - 2:
                            dve.wait_ge(s_tap0, 2 * m + 1 + i)
                        else:
                            dve.wait_ge(s_conv, 6 * m + 2 * (KW - 2 - k) + i - 1)
                        acc = c[p][:].rearrange("p (s t) -> p s t", t=SEQ)[:, :, back:]
                        src = QK[p][:, i, :].rearrange("p (s t) -> p s t", t=SEQ)[:, :, :SEQ - back]
                        nc.vector.scalar_tensor_tensor(out=acc, in0=src, scalar=wqk[p][:, tap + k:tap + k + 1], in1=acc,
                                                       op0=ALU.mult, op1=ALU.add).then_inc(s_conv, 1)

            def silu(m, p):
                for i, (c, t, s) in enumerate(((cq, tq, sq), (ck, tk, sk))):
                    dve.wait_ge(s_tanh, 2 * m + 1 + i)
                    nc.vector.scalar_tensor_tensor(out=s[p][:], in0=t[p][:], scalar=1.0, in1=c[p][:],
                                                   op0=ALU.add, op1=ALU.mult).then_inc(s_silu, 1)

            def stats(m, p):
                dve.wait_ge(s_fwd, m + 1)
                for i in range(2):
                    for j in range(BT):
                        nc.vector.bn_stats(hst[p][:, i * BT + j, :], QK[p][:, i, j * P:(j + 1) * P]).then_inc(s_hstat, 1)
                me, mo, Me, Mo = (hst[p][:, :, k] for k in (1, 4, 2, 5))
                sm, df, m2, d2 = (hm[p][:, k, :] for k in range(4))
                dve.wait_ge(s_hstat, 8 * m + 8)
                nc.vector.tensor_tensor(out=df, in0=me, in1=mo, op=ALU.subtract).then_inc(s_hmath, 1)
                nc.vector.scalar_tensor_tensor(out=m2, in0=Me, scalar=P * 4 * LN_EPS, in1=Mo, op0=ALU.add, op1=ALU.add).then_inc(s_hmath, 1)
                nc.vector.tensor_tensor(out=sm, in0=me, in1=mo, op=ALU.add).then_inc(s_hmath, 1)
                dve.wait_ge(s_hmath, 4 * m + 3)
                nc.vector.scalar_tensor_tensor(out=d2, in0=df, scalar=0.25, in1=df, op0=ALU.mult, op1=ALU.mult).then_inc(s_hmath, 1)
                dve.wait_ge(s_hmath, 4 * m + 4)
                nc.vector.scalar_tensor_tensor(out=hve[p][:], in0=m2, scalar=1.0 / P, in1=d2, op0=ALU.mult, op1=ALU.add).then_inc(s_hvar, 1)

            def shift(m, p):
                dve.wait_ge(s_hrstd, m + 1)
                nc.vector.scalar_tensor_tensor(out=hnb[p][:], in0=hm[p][:, 0, :], scalar=-0.5, in1=hrs[p][:],
                                               op0=ALU.mult, op1=ALU.mult).then_inc(s_hnb, 1)

            def step(g, par, b, hp, first, last_pair, final):
                n = 2 * g + par
                q = 1 - par
                end = final and last_pair
                if not (end and par == 1):
                    stats(n + 1, q)
                    shift(n + 1, q)
                if not end:
                    conv(n + 2, par)
                dve.wait_ge(s_tg, n + 1)
                nc.vector.scalar_tensor_tensor(out=gs[par][:], in0=tg[par][:], scalar=1.0, in1=X1[:], op0=ALU.add, op1=ALU.mult).then_inc(s_gs, 1)
                dve.wait_ge(s_s, n + 1)
                dve.wait_ge(s_em, n + 1)
                nc.vector.tensor_tensor(out=at[par][:], in0=X1[:].rearrange("p (j t) -> p j t", j=BT), in1=em[par][:], op=ALU.mult).then_inc(s_at, 1)
                if not end:
                    silu(n + 2, par)
                dve.wait_ge(s_o, n + 1)
                nc.vector.scalar_tensor_tensor(out=og[par][:], in0=X0[:], scalar=0.5, in1=gs[par][:], op0=ALU.mult, op1=ALU.mult).then_inc(s_og, 1)
                if last_pair and par == 1:
                    dve.wait_ge(s_y, n + 1)
                    for i in range(2):
                        xs = x_sb[:, bass.ds(b * BT + 2 * i, 2), :]
                        nc.vector.tensor_tensor(out=xs, in0=Y[:, 2 * i:2 * i + 2, :], in1=xs, op=ALU.add).then_inc(s_yout, 1)

            dve.wait_ge(xT, 4 * BLOCKS)
            conv(0, 0)
            silu(0, 0)
            conv(1, 1)
            silu(1, 1)
            stats(0, 0)
            shift(0, 0)
            run_steps(dve, step)
            dve.wait_ge(s_yout, 2 * BLOCKS)


def wkv_and_experts(nc, new_sem, x_sb, ident, w_gate, w_up, w_down, b_gate, b_up, b_down, w_router, b_router, ctx_in, wu_cols):
    E = 8
    LIMIT, ALPHA = 7.0, 1.702
    NEG = -1e38
    SEG = SEQ + 1
    NS = DC * BLK // SEQ
    HALF = NS // DC
    with ExitStack() as ctx:
        def sb(name, shape, dt=F32):
            return ctx.enter_context(nc.sbuf_tensor("m_" + name, shape, dt))

        def two(name, shape):
            return [sb(f"{name}{i}", shape) for i in range(2)]

        def psum(name, shape, dt=F32):
            return ctx.enter_context(nc.psum_tensor("m_" + name, shape, dt))

        def sem(name):
            return new_sem("m_" + name)

        wg, wu, wd = sb("wg", [P, E, DC, D]), sb("wu", [P, E, DC, D]), sb("wd", [P, E, DC, D])
        bg, bu = sb("bg", [P, E, DC]), sb("bu", [P, E, DC])
        bd = sb("bd", [E, D])
        rw, rb = sb("rw", [P, DC, E]), sb("rb", [P, E])
        wuc = sb("wuc", [P, 2 * DC])
        neghalf, iota = sb("neghalf", [P, BT]), sb("iota", [P, E])
        mark = sb("mark", [P, 1])
        ctx_t, xn = sb("ctx_t", [P, BT, D]), sb("xn", [P, BT, D])
        st, mv, ve, rs = sb("st", [P, BT, 6]), sb("mv", [P, BT, 2]), sb("ve", [P, BT]), sb("rs", [P, BT])
        kp, wp, op, a2, e2, ev, pp, qp = (sb(n, [P, NS, SEG]) for n in ("kp", "wp", "op", "a2", "e2", "ev", "pp", "qp"))
        vt, d1, d2, ae, ee = (sb(n, [P, NS, SEQ]) for n in ("vt", "d1", "d2", "ae", "ee"))
        hT = sb("hT", [P, DC, TOK])
        hb = sb("hb", [P, DC, BLK])
        lg, mx8 = sb("lg", [P, BT, E]), sb("mx8", [P, BT, E])
        ix8 = sb("ix8", [P, BT, E], mybir.dt.uint32)
        ixf, te, wt, oh = sb("ixf", [P, BT, 2]), sb("te", [P, 4, BT]), sb("wt", [P, 2, BT]), sb("oh", [P, 2, BT, E])
        sc = sb("sc", [P, TILES, E])
        sT = sb("sT", [E, BLK])
        gp, th, ur = two("gp", [P, DC, BLK]), two("th", [P, DC, BLK]), two("ur", [P, DC, BLK])

        G, U = psum("G", [P, DC, BLK]), psum("U", [P, DC, BLK])
        O, T = psum("O", [P, BT, D]), psum("T", [P, DC, BLK])
        Tt = T[:].rearrange("p c (j d) -> p (c j) d", d=D)

        w_in, ctx_loaded, const_set = sem("w_in"), sem("ctx_loaded"), sem("const_set")
        (stat, var, rstd, norm, cT, kT, vev, kev, scan_o, dif, clip, exps, qscan, pscan, ev_mul, den, num, rec, yv, yT, yadd,
         hTr, hev, hcp, rout, lgs, top, texp, wts_, score, sTr, sTe, bias, biasadd) = (sem(n) for n in (
             "stat", "var", "rstd", "norm", "cT", "kT", "vev", "kev", "scan_o", "dif", "clip", "exps", "qscan", "pscan",
             "ev_mul", "den", "num", "rec", "yv", "yT", "yadd", "hTr", "hev", "hcp", "rout", "lgs", "top", "texp", "wts",
             "score", "sTr", "sTe", "bias", "biasadd"))
        lgs_oh = sem("lgs_oh")
        s_gu, s_d, s_gp, s_ue, s_th, s_uc, s_gl, s_act, s_acc = (sem(n) for n in (
            "gu", "d", "gp", "ue", "th", "uc", "gl", "act", "acc"))
        block = ctx.enter_context(nc.Block())

        def tiles(b):
            return bass.ds(b * BT, BT)

        def run_blocks(eng, pieces, step):
            for e in range(E):
                if e in pieces:
                    pieces[e](0)

            def one(b, nb):
                for e in range(E):
                    step(b, e, nb, lambda: pieces[e](nb) if nb is not None and e in pieces else None)
            step(0, -1, 0, lambda: None)
            one(0, 1)
            with eng.Fori(1, BLOCKS - 1) as b:
                one(b, b + 1)
            one(BLOCKS - 1, None)

        @block.sync
        def _(sp):
            loads = ((wuc[:], wu_cols), (rw[:], w_router), (rb[:], b_router), (bg[:], b_gate), (bu[:], b_up), (bd[:], b_down),
                     (wg[:], w_gate), (wu[:], w_up), (wd[:], w_down))
            for i, (dst, src) in enumerate(loads):
                sp.dma_start(dst, src).then_inc(w_in, 16)
                if i == 2:
                    sp.dma_start(ctx_t[:], ctx_in[0:BLK, :].rearrange("(j p) d -> p j d", p=P)).then_inc(ctx_loaded, 16)
            with sp.Fori(1, BLOCKS) as b:
                sp.wait_ge(cT, b)
                sp.dma_start(ctx_t[:], ctx_in[bass.ds(b * BLK, BLK), :].rearrange("(j p) d -> p j d", p=P)).then_inc(ctx_loaded, 16)

        @block.gpsimd
        def _(pool):
            steps = [nc.gpsimd.memset(neghalf[:], -0.5),
                     nc.gpsimd.iota(iota[:], [[1, E]], base=0, channel_multiplier=0, allow_small_or_imprecise_dtypes=True)]
            for t in (kp, wp):
                steps.append(nc.gpsimd.memset(t[:, :, 0:1], NEG))
            for t in (a2, e2, ev):
                steps.append(nc.gpsimd.memset(t[:, :, 0:1], 0.0))
            for s in steps:
                s.then_inc(const_set, 1)
            pool.wait_ge(w_in, 16 * 9)
            pool.wait_ge(const_set, 7)
            nc.gpsimd.memset(wp[:, :, 1:SEG], 0.0).then_inc(const_set, 1)
            pool.wait_ge(const_set, 8)
            for c in range(DC):
                v = wp[:, c * HALF:(c + 1) * HALF, 1:SEG]
                nc.gpsimd.tensor_scalar(v, v, wuc[:, c:c + 1], None, ALU.add).then_inc(const_set, 1)

            def rs1(nb):
                pool.wait_ge(var, 2 * nb + 1)
                nc.gpsimd.tensor_tensor(out=rs[:], in0=ve[:], in1=neghalf[:], op=ALU.pow).then_inc(rstd, 1)

            def sums(nb):
                pool.wait_ge(exps, 4 * nb + 4)
                pool.wait_ge(vev, nb + 1)
                pool.wait_ge(pscan, nb)
                nc.gpsimd.tensor_tensor(out=ev[:, :, 1:SEG], in0=e2[:, :, 1:SEG], in1=vt[:], op=ALU.mult).then_inc(ev_mul, 1)
                pool.wait_ge(ev_mul, 2 * nb + 1)
                nc.gpsimd.tensor_tensor(out=vt[:], in0=ee[:], in1=vt[:], op=ALU.mult).then_inc(ev_mul, 1)
                pool.wait_ge(qscan, nb + 1)
                nc.gpsimd.tensor_tensor(out=d1[:], in0=ae[:], in1=qp[:, :, 0:SEQ], op=ALU.mult).then_inc(den, 1)
                pool.wait_ge(den, 2 * nb + 1)
                nc.gpsimd.tensor_tensor(out=d1[:], in0=d1[:], in1=ee[:], op=ALU.add).then_inc(den, 1)
                pool.wait_ge(pscan, nb + 1)
                nc.gpsimd.tensor_tensor(out=ae[:], in0=ae[:], in1=pp[:, :, 0:SEQ], op=ALU.mult).then_inc(num, 1)
                pool.wait_ge(num, 2 * nb + 1)
                nc.gpsimd.tensor_tensor(out=ae[:], in0=ae[:], in1=vt[:], op=ALU.add).then_inc(num, 1)

            def quotient(nb):
                pool.wait_ge(rec, nb + 1)
                pool.wait_ge(num, 2 * nb + 2)
                nc.gpsimd.tensor_tensor(out=d2[:], in0=ae[:], in1=d1[:], op=ALU.mult).then_inc(yv, 1)

            def rs2(nb):
                pool.wait_ge(var, 2 * nb + 2)
                nc.gpsimd.tensor_tensor(out=rs[:], in0=ve[:], in1=neghalf[:], op=ALU.pow).then_inc(rstd, 1)

            def copy_h(nb):
                pool.wait_ge(hev, nb + 1)
                nc.gpsimd.tensor_copy(hT[:, :, bass.ds(nb * BLK, BLK)], hb[:]).then_inc(hcp, 1)

            def step(b, e, nb, piece):
                piece()

            run_blocks(pool, {0: rs1, 3: sums, 4: quotient, 5: rs2, 6: copy_h}, step)

        @block.tensor
        def _(pe):
            def to_channels(src, done):
                for j in range(BT):
                    for c in range(DC):
                        last = nc.tensor.transpose(T[:, c, j * P:(j + 1) * P], src[:, j, c * P:(c + 1) * P], ident)
                last.then_inc(done, 1)

            def ctx_T(nb):
                pe.wait_ge(ctx_loaded, 16 * nb + 16)
                pe.wait_ge(biasadd, 2 * nb)
                to_channels(ctx_t, cT)

            def k_T(nb):
                pe.wait_ge(norm, 8 * nb + 4)
                pe.wait_ge(vev, nb + 1)
                to_channels(xn, kT)

            def y_T(nb):
                pe.wait_ge(yv, nb + 1)
                pe.wait_ge(kev, 2 * nb + 2)
                yf = d2[:].rearrange("p (c s) t -> p c (s t)", c=DC)
                for j in range(BT):
                    for c in range(DC):
                        last = nc.tensor.transpose(Tt[:, j, c * P:(c + 1) * P], yf[:, c, j * P:(j + 1) * P], ident)
                last.then_inc(yT, 1)

            def h_T(nb):
                pe.wait_ge(norm, 8 * nb + 8)
                to_channels(xn, hTr)

            def router(nb):
                pe.wait_ge(hev, nb + 1)
                for j in range(BT):
                    for c in range(DC):
                        last = nc.tensor.matmul(T[:, 0, j * E:(j + 1) * E], hb[:, c, j * P:(j + 1) * P], rw[:, c, :],
                                                start=c == 0, stop=c == DC - 1)
                last.then_inc(rout, 1)
                pe.wait_ge(score, nb + 1)
                for j in range(BT):
                    last = nc.tensor.transpose(T[0:E, 1, j * P:(j + 1) * P], oh[:, 0, j, :], ident)
                last.then_inc(sTr, 1)
                pe.wait_ge(sTe, nb + 1)
                for j in range(BT):
                    last = nc.tensor.matmul(Tt[:, j, :], sT[:, j * P:(j + 1) * P], bd[:], start=True, stop=True)
                last.then_inc(bias, 1)

            def gate_up(m, e, b):
                for acc, w, read in ((G, wg, s_gp), (U, wu, s_ue)):
                    pe.wait_ge(read, 2 * m)
                    for i in range(DC):
                        for c in range(DC):
                            last = nc.tensor.matmul(acc[:, i, :], w[:, e, c, i * P:(i + 1) * P], hT[:, c, bass.ds(b * BLK, BLK)],
                                                    start=c == 0, stop=c == DC - 1)
                        last.then_inc(s_gu, 1)

            def down(n, e):
                pe.wait_ge(s_act, 2 * n + 2)
                pe.wait_ge(s_acc, 4 * n)
                for j in range(BT):
                    for i in range(DC):
                        last = nc.tensor.matmul(O[:, j, :], th[e % 2][:, i, j * P:(j + 1) * P], wd[:, e, i, :],
                                                start=i == 0, stop=i == DC - 1)
                    if j % 2:
                        last.then_inc(s_d, 1)

            def step(b, e, nb, piece):
                n = b * E + e
                if e < E - 1:
                    if e < 0:
                        pe.wait_ge(hcp, 1)
                    gate_up(n + 1, e + 1, b)
                elif nb is not None:
                    pe.wait_ge(hcp, nb + 1)
                    gate_up(n + 1, 0, nb)
                piece()
                if e >= 0:
                    down(n, e)

            pe.wait_ge(w_in, 16 * 9)
            pe.wait_ge(const_set, 10)

            run_blocks(pe, {0: ctx_T, 1: k_T, 5: y_T, 6: h_T, 7: router}, step)

        @block.scalar
        def _(act):
            def v_out(nb):
                act.wait_ge(cT, nb + 1)
                act.wait_ge(num, 2 * nb)
                nc.scalar.activation(vt[:], T[:].rearrange("p c (s t) -> p (c s) t", t=SEQ), ACT.Copy).then_inc(vev, 1)

            def k_out(nb):
                act.wait_ge(kT, nb + 1)
                for c in range(DC):
                    nc.scalar.activation(kp[:, c * HALF:(c + 1) * HALF, 1:SEG], T[:, c, :].rearrange("p (s t) -> p s t", t=SEQ),
                                         ACT.Copy).then_inc(kev, 1)

            def exponentials(nb):
                act.wait_ge(clip, 4 * nb + 4)
                nc.scalar.activation(a2[:, :, 1:SEG], a2[:, :, 1:SEG], ACT.Exp).then_inc(exps, 1)
                nc.scalar.activation(e2[:, :, 1:SEG], e2[:, :, 1:SEG], ACT.Exp, scale=-1.0).then_inc(exps, 1)
                nc.scalar.activation(ae[:], ae[:], ACT.Exp, scale=-1.0).then_inc(exps, 1)
                nc.scalar.activation(ee[:], ee[:], ACT.Exp).then_inc(exps, 1)

            def h_out(nb):
                act.wait_ge(hTr, nb + 1)
                act.wait_ge(rout, nb)
                act.wait_ge(hcp, nb)
                nc.scalar.activation(hb[:], T[:], ACT.Copy).then_inc(hev, 1)

            def weights(nb):
                act.wait_ge(top, 8 * nb + 8)
                act.wait_ge(texp, 2 * nb + 1)
                nc.scalar.activation(te[:, 1, :], te[:, 0, :], ACT.Exp).then_inc(texp, 1)
                act.wait_ge(sTr, nb + 1)
                nc.scalar.activation(sT[:], T[0:E, 1, :], ACT.Copy).then_inc(sTe, 1)

            def step(b, e, nb, piece):
                n = b * E + e
                if e < E - 1 or nb is not None:
                    m, p, x = n + 1, (e + 1) % 2, (e + 1) % E
                    for i in range(DC):
                        act.wait_ge(s_gp, 2 * m + 1 + i)
                        if e >= 0:
                            act.wait_ge(s_d, 2 * n)
                        nc.scalar.activation(th[p][:, i, :], gp[p][:, i, :], ACT.Tanh, scale=ALPHA / 2).then_inc(s_th, 1)
                    for i in range(DC):
                        act.wait_ge(s_gu, 4 * m + 3 + i)
                        if e >= 0:
                            act.wait_ge(s_act, 2 * n)
                        nc.scalar.activation(ur[p][:, i, :], U[:, i, :], ACT.Identity, bias=bu[:, x, i:i + 1]).then_inc(s_ue, 1)
                piece()

            act.wait_ge(w_in, 16 * 9)
            run_blocks(act, {0: v_out, 1: k_out, 2: exponentials, 6: h_out, 7: weights}, step)

        @block.vector
        def _(dve):
            def statistics(nb, k):
                nc.vector.memset(mark[:], 0.0)
                for j in range(BT):
                    nc.vector.bn_stats(st[:, j, :], x_sb[:, bass.ds(nb * BT + j, 1), :]).then_inc(stat, 1)
                dve.wait_ge(stat, 16 * nb + 8 * k + 4)
                nc.vector.memset(mark[:], 0.0)
                for j in range(BT):
                    nc.vector.bn_aggr(mv[:, j, :], st[:, j, :]).then_inc(stat, 1)
                dve.wait_ge(stat, 16 * nb + 8 * k + 8)
                nc.vector.tensor_scalar(ve[:], mv[:, :, 1], LN_EPS, None, ALU.add).then_inc(var, 1)

            def normalise(nb, k):
                dve.wait_ge(rstd, 2 * nb + k + 1)
                for j in range(BT):
                    nc.vector.tensor_scalar(xn[:, j, :], x_sb[:, bass.ds(nb * BT + j, 1), :], mv[:, j, 0:1], rs[:, j:j + 1],
                                            ALU.subtract, ALU.mult).then_inc(norm, 1)

            def ln1(nb):
                statistics(nb, 0)

            def ln1_out(nb):
                dve.wait_ge(hTr, nb)
                normalise(nb, 0)

            def running_max(nb):
                dve.wait_ge(kev, 2 * nb + 2)
                flat = lambda t: t[:].rearrange("p s t -> p (s t)")
                nc.vector.tensor_tensor_scan(out=flat(op), data0=flat(wp), data1=flat(kp), initial=NEG, op0=ALU.add,
                                             op1=ALU.max).then_inc(scan_o, 1)
                dve.wait_ge(scan_o, nb + 1)
                dve.wait_ge(yT, nb)
                for c in range(DC):
                    s = slice(c * HALF, (c + 1) * HALF)
                    nc.vector.scalar_tensor_tensor(out=d1[:, s, :], in0=kp[:, s, 1:SEG], scalar=wuc[:, DC + c:DC + c + 1],
                                                   in1=op[:, s, 0:SEQ], op0=ALU.add, op1=ALU.subtract).then_inc(dif, 1)
                    nc.vector.scalar_tensor_tensor(out=d2[:, s, :], in0=op[:, s, 0:SEQ], scalar=wuc[:, c:c + 1],
                                                   in1=kp[:, s, 1:SEG], op0=ALU.add, op1=ALU.subtract).then_inc(dif, 1)

            def clips(nb):
                dve.wait_ge(dif, 4 * nb + 4)
                dve.wait_ge(pscan, nb)
                nc.vector.tensor_scalar(a2[:, :, 1:SEG], d2[:], 0.0, None, ALU.min).then_inc(clip, 1)
                nc.vector.tensor_scalar(e2[:, :, 1:SEG], d2[:], 0.0, None, ALU.max).then_inc(clip, 1)
                nc.vector.tensor_scalar(ae[:], d1[:], 0.0, None, ALU.max).then_inc(clip, 1)
                nc.vector.tensor_scalar(ee[:], d1[:], 0.0, None, ALU.min).then_inc(clip, 1)

            def scans(nb):
                flat = lambda t: t[:].rearrange("p s t -> p (s t)")
                dve.wait_ge(exps, 4 * nb + 4)
                nc.vector.tensor_tensor_scan(out=flat(qp), data0=flat(a2), data1=flat(e2), initial=0.0, op0=ALU.mult,
                                             op1=ALU.add).then_inc(qscan, 1)
                dve.wait_ge(ev_mul, 2 * nb + 1)
                nc.vector.tensor_tensor_scan(out=flat(pp), data0=flat(a2), data1=flat(ev), initial=0.0, op0=ALU.mult,
                                             op1=ALU.add).then_inc(pscan, 1)

            def reciprocals(nb):
                dve.wait_ge(den, 2 * nb + 2)
                nc.vector.reciprocal(d1[:], d1[:]).then_inc(rec, 1)

            def residual(nb):
                dve.wait_ge(yT, nb + 1)
                for i in range(2):
                    xs = x_sb[:, bass.ds(nb * BT + 2 * i, 2), :]
                    nc.vector.tensor_tensor(out=xs, in0=Tt[:, 2 * i:2 * i + 2, :], in1=xs, op=ALU.add).then_inc(yadd, 1)
                dve.wait_ge(yadd, 2 * nb + 2)
                dve.wait_ge(kT, nb + 1)
                statistics(nb, 1)

            def ln2_out(nb):
                normalise(nb, 1)

            def choose(nb):
                dve.wait_ge(rout, nb + 1)
                nc.vector.tensor_tensor(out=lg[:], in0=T[:, 0, 0:BT * E].rearrange("p (j e) -> p j e", e=E),
                                        in1=rb[:].unsqueeze(1).to_broadcast([P, BT, E]), op=ALU.add).then_inc(lgs, 1)
                dve.wait_ge(lgs, nb + 1)
                nc.vector.memset(mark[:], 0.0)
                for j in range(BT):
                    nc.vector.max(mx8[:, j, :], lg[:, j, :]).then_inc(top, 1)
                dve.wait_ge(top, 8 * nb + 4)
                nc.vector.memset(mark[:], 0.0)
                for j in range(BT):
                    nc.vector.max_index(ix8[:, j, :], mx8[:, j, :], lg[:, j, :]).then_inc(top, 1)
                dve.wait_ge(top, 8 * nb + 8)
                nc.vector.tensor_tensor(out=te[:, 0, :], in0=mx8[:, :, 1], in1=mx8[:, :, 0], op=ALU.subtract).then_inc(texp, 1)
                nc.vector.tensor_copy(ixf[:], ix8[:, :, 0:2]).then_inc(wts_, 1)
                dve.wait_ge(texp, 2 * nb + 2)
                nc.vector.tensor_scalar(te[:, 2, :], te[:, 1, :], 1.0, 2.0, ALU.add, ALU.mult).then_inc(wts_, 1)
                dve.wait_ge(wts_, 5 * nb + 2)
                nc.vector.reciprocal(wt[:, 0, :], te[:, 2, :]).then_inc(wts_, 1)
                dve.wait_ge(wts_, 5 * nb + 3)
                nc.vector.tensor_tensor(out=wt[:, 1, :], in0=wt[:, 0, :], in1=te[:, 1, :], op=ALU.mult).then_inc(wts_, 1)
                dve.wait_ge(wts_, 5 * nb + 4)
                dve.wait_ge(sTr, nb)
                for k in range(2):
                    for j in range(BT):
                        last = nc.vector.tensor_scalar(oh[:, k, j, :], iota[:], ixf[:, j, k:k + 1], wt[:, k, j:j + 1], ALU.is_equal, ALU.mult)
                        last.then_inc(lgs_oh, 1)
                dve.wait_ge(lgs_oh, 8 * nb + 8)
                nc.vector.tensor_tensor(out=sc[:, tiles(nb), :], in0=oh[:, 0, :, :], in1=oh[:, 1, :, :], op=ALU.add).then_inc(wts_, 1)
                nc.vector.tensor_tensor(out=oh[:, 0, :, :], in0=oh[:, 0, :, :], in1=oh[:, 1, :, :], op=ALU.add).then_inc(score, 1)
                dve.wait_ge(bias, nb + 1)
                dve.wait_ge(norm, 8 * nb + 8)
                for i in range(2):
                    xs = x_sb[:, bass.ds(nb * BT + 2 * i, 2), :]
                    nc.vector.scalar_tensor_tensor(out=xs, in0=Tt[:, 2 * i:2 * i + 2, :], scalar=2.0, in1=xs, op0=ALU.mult,
                                                   op1=ALU.add).then_inc(biasadd, 1)

            def step(b, e, nb, piece):
                n = b * E + e
                if e < E - 1 or nb is not None:
                    m, p, x = n + 1, (e + 1) % 2, (e + 1) % E
                    for i in range(DC):
                        dve.wait_ge(s_gu, 4 * m + 1 + i)
                        if e >= 0:
                            dve.wait_ge(s_gl, 2 * n)
                        nc.vector.tensor_scalar(gp[p][:, i, :], G[:, i, :], bg[:, x, i:i + 1], LIMIT, ALU.add, ALU.min).then_inc(s_gp, 1)
                    for i in range(DC):
                        dve.wait_ge(s_th, 2 * m + 1 + i)
                        nc.vector.scalar_tensor_tensor(out=th[p][:, i, :], in0=th[p][:, i, :], scalar=1.0, in1=gp[p][:, i, :],
                                                       op0=ALU.add, op1=ALU.mult).then_inc(s_gl, 1)
                    for i in range(DC):
                        dve.wait_ge(s_ue, 2 * m + 1 + i)
                        nc.vector.tensor_scalar(ur[p][:, i, :], ur[p][:, i, :], -LIMIT, LIMIT, ALU.max, ALU.min).then_inc(s_uc, 1)
                    for i in range(DC):
                        dve.wait_ge(s_uc, 2 * m + 1 + i)
                        nc.vector.scalar_tensor_tensor(out=th[p][:, i, :], in0=ur[p][:, i, :], scalar=1.0, in1=th[p][:, i, :],
                                                       op0=ALU.add, op1=ALU.mult).then_inc(s_act, 1)
                piece()
                if e >= 0:
                    if e == 0:
                        dve.wait_ge(biasadd, 2 * b + 2)
                    dve.wait_ge(s_acc, 4 * n)
                    for j in range(BT):
                        dve.wait_ge(s_d, 2 * n + 1 + j // 2)
                        t = bass.ds(b * BT + j, 1)
                        nc.vector.scalar_tensor_tensor(out=x_sb[:, t, :], in0=O[:, j, :], scalar=sc[:, t, e:e + 1],
                                                       in1=x_sb[:, t, :], op0=ALU.mult, op1=ALU.add).then_inc(s_acc, 1)

            dve.wait_ge(w_in, 16 * 9)
            dve.wait_ge(const_set, 10)
            run_blocks(dve, {0: lambda nb: (ln1(nb), ln1_out(nb)), 1: running_max, 2: clips, 3: scans, 4: reciprocals,
                             5: residual, 6: ln2_out, 7: choose}, step)
            dve.wait_ge(s_acc, 4 * BLOCKS * E)


def layer_one(nc, new_sem, x_sb, ident, a):
    H, HD = 16, 16
    G8 = P // HD
    SC = float(HD) ** -0.5
    F_ = 1024
    FT = F_ // P
    R = 16
    RMS_EPS = 1e-6
    MOD_SCALE = 0.1
    AV = HD + 1
    AX = mybir.AxisListType.X
    FIRST = dict(D=0, E=1, Et=2, F=3, Ft=4, M=5)
    with ExitStack() as ctx:
        def sb(name, shape, dt=F32):
            return ctx.enter_context(nc.sbuf_tensor("l_" + name, shape, dt))

        def psum(name, shape, dt=F32):
            return ctx.enter_context(nc.psum_tensor("l_" + name, shape, dt))

        counters = {}

        def S(name):
            if name not in counters:
                counters[name] = new_sem("l_" + name)
            return counters[name]

        dwqk, dwv, dwo = sb("dwqk", [P, DC, 8 * P]), sb("dwv", [P, DC, 64]), sb("dwo", [P, DC, D])
        rope, sink = sb("rope", [P, 2, P]), sb("sink", [P, H])
        ewq, ewkv, ewo = sb("ewq", [P, DC, D]), sb("ewkv", [P, DC, 2 * D]), sb("ewo", [P, DC, D])
        ebq, ebkv, ebo = sb("ebq", [P, D]), sb("ebkv", [P, 2 * D]), sb("ebo", [P, D])
        fwqk, fwv, fwo = sb("fwqk", [P, DC, 4 * P]), sb("fwv", [P, DC, D]), sb("fwo", [P, DC, D])
        fa, fb, lnw = sb("fa", [P, DC, R]), sb("fb", [R, F_]), sb("lnw", [P, 2 * DC])
        win, wup, wdn = sb("win", [P, DC, F_]), sb("wup", [P, DC, F_]), sb("wdn", [P, FT, D])
        headmask = sb("headmask", [P, G8])
        cmask = sb("cmask", [P, G8, SEQ], BF16)
        identb = sb("identb", [P, P], BF16)
        neghalf = sb("neghalf", [P, 2])
        xn = {k: sb("xn" + k, [P, D]) for k in "DEF"}
        xT = {k: sb("xT" + k, [P, DC, 2, 2, SEQ]) for k in "DF"}
        xTE = sb("xTE", [P, DC, P])
        st, mv = {k: sb("st" + k, [P, 6]) for k in "DEF"}, {k: sb("mv" + k, [P, 2]) for k in "DEF"}
        ve, rs = {k: sb("ve" + k, [P, 2]) for k in "DEF"}, {k: sb("rs" + k, [P, 2]) for k in "DEF"}
        qk = {k: sb("qk" + k, [P, 4, P]) for k in "DF"}
        vbd = {k: sb("vbd" + k, [P, 2, H // 2, 2, AV]) for k in "DF"}
        hm = {k: sb("hm" + k, [P, 3, H]) for k in "DF"}
        rec = {k: sb("rec" + k, [P, H]) for k in "DF"}
        o, oT = {k: sb("o" + k, [P, D]) for k in "DF"}, {k: sb("oT" + k, [P, DC, P]) for k in "DF"}
        rt = sb("rt", [P, 2, 4, P])
        mark = sb("mark", [P, 1])
        kx = sb("kx", [P, 2, 2, G8, SEQ])
        ex, eT = sb("ex", [P, H, SEQ]), sb("eT", [P, H // 2, P])
        ctx_t, cT = sb("ctx_t", [P, D]), sb("cT", [P, DC, P])
        kv, q = sb("kv", [P, 2, D]), sb("q", [P, D])
        vE = sb("vE", [P, D])
        prod = sb("prod", [P, H, H, HD])
        sco, se = sb("sco", [P, H, H]), sb("se", [P, 3, H])
        att, attT = sb("att", [P, D]), sb("attT", [P, DC, P])
        y = sb("y", [P, D])
        atT, modT, gmT = sb("atT", [P, DC, P]), sb("modT", [R, P]), sb("gmT", [R, P])
        x2T = sb("x2T", [P, DC, TOK])
        th, hid = sb("th", [P, 4 * P]), sb("hid", [P, FT, P])

        SS, PJ = psum("SS", [P, 2, BLK]), psum("PJ", [P, 2, BLK])
        GA, UA, MI, EB = (psum(n, [P, BLK]) for n in ("GA", "UA", "MI", "EB"))
        block = ctx.enter_context(nc.Block())

        def tile(t):
            return bass.ds(t, 1)

        def started(n):
            return not isinstance(n, int) or n > 0

        def wait_if(eng, sem, n):
            if started(n):
                eng.wait_ge(sem, n)

        def cap(n):
            return min(n, TILES) if isinstance(n, int) else n

        def iterate(eng, pieces):
            def one(i, check):
                for stage, piece in pieces:
                    t = i - FIRST[stage]
                    if not check or 0 <= t < TILES:
                        piece(t)
            start = max(FIRST.values()) + 1
            for i in range(start):
                one(i, True)
            with eng.Fori(start, TILES) as i:
                one(i, False)
            for i in range(TILES, TILES + max(FIRST.values())):
                one(i, True)

        USES = {
            "EB": [("d_xT", "D", [("D_xT", 1, 1)]), ("e_cT", "E", [("E_cT", 1, 1)]), ("e_kv", "E", [("E_kv", 1, 1)]),
                   ("d_v", "D", [("D_vb", 2, 2)]), ("e_xT", "E", [("E_xT", 1, 1)]), ("e_q", "E", [("E_q", 1, 1)]),
                   ("d_av", "D", [("D_o", 1, 1)]), ("d_oT", "D", [("D_oT", 1, 1)]), ("d_wo", "D", [("D_x", 1, 1)]),
                   ("et_aT", "Et", [("E_aT", 1, 1)]), ("et_wo", "Et", [("E_x", 2, 1)])],
            "SS": [("ft_eT", "Ft", [("F_eT", 1, 1)]), ("d_s", "D", [("D_arg", 1, 1)]), ("d_eT", "D", [("D_eT", 1, 1)]),
                   ("f_s", "F", [("F_arg", 1, 1)])],
            "PJ": [("d_qk", "D", [("D_rt", 2, 2)]), ("f_qkv", "F", [("F_qk", 1, 1), ("F_vb", 2, 2)])],
            "MI": [("ft_av", "Ft", [("F_o", 1, 1)]), ("ft_oT", "Ft", [("F_oT", 1, 1)]), ("ft_at", "Ft", [("F_at", 1, 1)]),
                   ("ft_a", "Ft", [("F_gm", 1, 1)]), ("f_zT", "F", [("F_x1", 2, 2), ("F_x2", 2, 2)])],
            "GA": [("m_0", "M", [("M_silu", 2, 1)]), ("m_1", "M", [("M_silu", 2, 2)]), ("m_down", "M", [("M_x", 1, 1)])],
            "UA": [("m_0", "M", [("M_hid", 2, 1)]), ("m_1", "M", [("M_hid", 2, 2)])],
        }
        WEIGHTS = 21
        CONSTS = 9

        @block.sync
        def _(sp):
            for tensor, name in ((dwqk, "dwqk"), (dwv, "dwv"), (dwo, "dwo"), (rope, "rope"), (sink, "sink"), (ewq, "ewq"),
                                 (ewkv, "ewkv"), (ewo, "ewo"), (ebq, "ebq"), (ebkv, "ebkv"), (ebo, "ebo"), (fwqk, "fwqk"),
                                 (fwv, "fwv"), (fwo, "fwo"), (fa, "fa"), (fb, "fb"), (lnw, "lnw"), (headmask, "headmask"),
                                 (win, "win"), (wup, "wup"), (wdn, "wdn")):
                sp.dma_start(tensor[:], a[name]).then_inc(S("w_in"), 16)

            def load_ctx(t):
                wait_if(sp, S("E_cTp"), t)
                sp.dma_start(ctx_t[:], a["ctx_in"][bass.ds(t * P, P), :]).then_inc(S("ctx_in"), 16)

            def store(t):
                sp.wait_ge(S("M_x"), t + 1)
                sp.dma_start(a["out"][bass.ds(t * P, P), :], x_sb[:, tile(t), :]).then_inc(S("stored"), 16)

            iterate(sp, [("E", load_ctx), ("M", store)])
            sp.wait_ge(S("stored"), 16 * TILES)

        @block.gpsimd
        def _(pool):
            nc.gpsimd.memset(neghalf[:], -0.5).then_inc(S("const"), 1)
            nc.gpsimd.tensor_copy(identb[:], ident).then_inc(S("const"), 1)
            nc.gpsimd.memset(cmask[:], 0.0).then_inc(S("const"), 1)
            for k in "DF":
                nc.gpsimd.memset(vbd[k][:], 0.0).then_inc(S("const"), 1)
            pool.wait_ge(S("const"), 5)
            for s in range(2):
                v = cmask[s * SEQ:(s + 1) * SEQ, :, :]
                nc.gpsimd.affine_select(out=v, in_=v, compare_op=ALU.is_ge, fill=-1e30, base=0, pattern=[[0, G8], [-1, SEQ]],
                                        channel_multiplier=1).then_inc(S("const"), 1)
            for k in "DF":
                for h in range(2):
                    ones = vbd[k][h * SEQ:(h + 1) * SEQ, :, :, h, HD:AV]
                    nc.gpsimd.memset(ones, 1.0).then_inc(S("const"), 1)
            pool.wait_ge(S("w_in"), 16 * WEIGHTS)

            def power(k, n):
                def piece(t):
                    pool.wait_ge(S(k + "_ve"), n * t + n)
                    nc.gpsimd.tensor_tensor(out=rs[k][:, 0:n], in0=ve[k][:, 0:n], in1=neghalf[:, 0:n], op=ALU.pow).then_inc(S(k + "_rs"), 1)
                return piece

            def rotate(t):
                pool.wait_ge(S("D_rt"), 2 * t + 2)
                wait_if(pool, S("D_s"), t)
                nc.gpsimd.tensor_tensor(out=qk["D"][:], in0=rt[:, 0], in1=rt[:, 1], op=ALU.add).then_inc(S("D_qk"), 1)

            def expand_keys(k, other, ahead):
                def piece(t):
                    pool.wait_ge(S(k + "_qk"), t + 1)
                    wait_if(pool, S(k + "_s"), t)
                    wait_if(pool, S(other + "_s"), cap(t + ahead))
                    for c in range(2):
                        for s in range(2):
                            keys = qk[k][:, 2 + c, s * SEQ:(s + 1) * SEQ].unsqueeze(1).to_broadcast([P, G8, SEQ])
                            nc.gpsimd.tensor_tensor(out=kx[:, c, s], in0=keys, in1=headmask[:].unsqueeze(2).to_broadcast([P, G8, SEQ]),
                                                    op=ALU.mult).then_inc(S(k + "_kx"), 1)
                return piece

            def products_qk(t):
                pool.wait_ge(S("E_q"), t + 1)
                pool.wait_ge(S("E_kv"), t + 1)
                wait_if(pool, S("E_att"), 4 * t)
                qv = q[:].rearrange("p (h d) -> p h d", d=HD)
                kk = kv[:, 0, :].rearrange("p (g d) -> p g d", d=HD)
                for h in range(H):
                    nc.gpsimd.tensor_tensor(out=prod[:, h], in0=qv[:, h:h + 1, :].to_broadcast([P, H, HD]), in1=kk,
                                            op=ALU.mult).then_inc(S("E_pqk"), 1)

            def products_av(t):
                pool.wait_ge(S("E_w"), t + 1)
                pool.wait_ge(S("E_keep"), t + 1)
                vv = vE[:].rearrange("p (g d) -> p d g", d=HD)
                for h in range(H):
                    nc.gpsimd.tensor_tensor(out=prod[:, h], in0=sco[:, h:h + 1, :].to_broadcast([P, HD, H]), in1=vv,
                                            op=ALU.mult).then_inc(S("E_pav"), 1)

            iterate(pool, [("D", power("D", 1)), ("E", power("E", 1)), ("F", power("F", 2)), ("Et", products_av),
                           ("D", rotate), ("D", expand_keys("D", "F", -3)), ("E", products_qk), ("F", expand_keys("F", "D", 4))])

        @block.tensor
        def _(pe):
            def free(bank, use, t):
                uses = USES[bank]
                k = [u[0] for u in uses].index(use)
                i = t + FIRST[uses[k][1]]
                for back in range(1, 2 * len(uses) + 1):
                    laps, at = divmod(k - back, len(uses))
                    _, stage, left = uses[at]
                    before = i + laps - FIRST[stage]
                    if not isinstance(before, int) or 0 <= before < TILES:
                        for sem, per, n in left:
                            pe.wait_ge(S(sem), per * before + n)
                        return

            def product(out, lhsT, rhs):
                for c in range(DC):
                    last = nc.tensor.matmul(out, lhsT(c), rhs(c), start=c == 0, stop=c == DC - 1)
                return last

            def turn(bank, src):
                for c in range(DC):
                    last = nc.tensor.transpose(bank[:, c * P:(c + 1) * P], src[:, c * P:(c + 1) * P], ident)
                return last

            def twice(k, c, s):
                return xT[k][:, c, s].rearrange("p r n -> p (r n)")

            def projections(k, w, count):
                for m in range(count):
                    last = product(PJ[:, m // 4, (m % 4) * P:(m % 4 + 1) * P], lambda c: w[:, c, m * P:(m + 1) * P],
                                   lambda c: xT[k][:, c, :, 0, :])
                return last

            def scores(k):
                for c in range(2):
                    for s in range(2):
                        last = nc.tensor.matmul(SS[s * SEQ:(s + 1) * SEQ, c, :], qk[k][:, c, s * SEQ:(s + 1) * SEQ], kx[:, c, s],
                                                start=True, stop=k == "D", skip_group_check=True)
                    if k == "F":
                        last = nc.tensor.matmul(SS[:, c, :], identb[:], cmask[:], start=False, stop=True, skip_group_check=True)
                return last

            def weights_T():
                for j in range(H // 2):
                    last = nc.tensor.transpose(SS[:, j // 4, (j % 4) * P:(j % 4 + 1) * P], ex[:, 2 * j:2 * j + 2, :], ident)
                return last

            def weighted_values(k, bank):
                for j in range(H // 2):
                    for s in range(2):
                        last = nc.tensor.matmul(bank[s * SEQ:(s + 1) * SEQ, j * 2 * AV:(j + 1) * 2 * AV], eT[:, j, s * SEQ:(s + 1) * SEQ],
                                                vbd[k][:, s, j], start=True, stop=True)
                return last

            def d_xT(t):
                pe.wait_ge(S("D_xn"), t + 1)
                free("EB", "d_xT", t)
                turn(EB, xn["D"]).then_inc(S("D_xTp"), 1)

            def d_qk(t):
                pe.wait_ge(S("D_xT"), t + 1)
                free("PJ", "d_qk", t)
                projections("D", dwqk, 8).then_inc(S("D_pj"), 1)

            def d_v(t):
                free("EB", "d_v", t)
                for s in range(2):
                    last = product(EB[:, s * 64:(s + 1) * 64], lambda c: twice("D", c, s), lambda c: dwv[:, c, :])
                last.then_inc(S("D_pv"), 1)

            def d_s(t):
                pe.wait_ge(S("D_kx"), 4 * t + 4)
                free("SS", "d_s", t)
                scores("D").then_inc(S("D_s"), 1)

            def d_eT(t):
                pe.wait_ge(S("D_exp"), t + 1)
                free("SS", "d_eT", t)
                weights_T().then_inc(S("D_eTp"), 1)

            def d_av(t):
                pe.wait_ge(S("D_eT"), t + 1)
                pe.wait_ge(S("D_vb"), 2 * t + 2)
                free("EB", "d_av", t)
                weighted_values("D", EB).then_inc(S("D_av"), 1)

            def d_oT(t):
                pe.wait_ge(S("D_o"), t + 1)
                free("EB", "d_oT", t)
                turn(EB, o["D"]).then_inc(S("D_oTp"), 1)

            def d_wo(t):
                pe.wait_ge(S("D_oT"), t + 1)
                free("EB", "d_wo", t)
                product(EB[:, 0:D], lambda c: oT["D"][:, c, :], lambda c: dwo[:, c, :]).then_inc(S("D_wo"), 1)

            def e_cT(t):
                pe.wait_ge(S("ctx_in"), 16 * t + 16)
                free("EB", "e_cT", t)
                turn(EB, ctx_t).then_inc(S("E_cTp"), 1)

            def e_kv(t):
                pe.wait_ge(S("E_cT"), t + 1)
                free("EB", "e_kv", t)
                product(EB[:], lambda c: cT[:, c, :], lambda c: ewkv[:, c, :]).then_inc(S("E_kvp"), 1)

            def e_xT(t):
                pe.wait_ge(S("E_xn"), t + 1)
                free("EB", "e_xT", t)
                turn(EB, xn["E"]).then_inc(S("E_xTp"), 1)

            def e_q(t):
                pe.wait_ge(S("E_xT"), t + 1)
                free("EB", "e_q", t)
                product(EB[:, 0:D], lambda c: xTE[:, c, :], lambda c: ewq[:, c, :]).then_inc(S("E_qp"), 1)

            def et_aT(t):
                pe.wait_ge(S("E_att"), 4 * t + 4)
                free("EB", "et_aT", t)
                turn(EB, att).then_inc(S("E_aTp"), 1)

            def et_wo(t):
                pe.wait_ge(S("E_aT"), t + 1)
                free("EB", "et_wo", t)
                product(EB[:, 0:D], lambda c: attT[:, c, :], lambda c: ewo[:, c, :]).then_inc(S("E_wo"), 1)

            def f_zT(t):
                pe.wait_ge(S("F_xn"), 3 * t + 3)
                free("MI", "f_zT", t)
                turn(MI, xn["F"]).then_inc(S("F_zTp"), 1)

            def f_qkv(t):
                pe.wait_ge(S("F_x1"), 2 * t + 2)
                free("PJ", "f_qkv", t)
                projections("F", fwqk, 4)
                for s in range(2):
                    last = product(PJ[:, 1, s * D:(s + 1) * D], lambda c: twice("F", c, s), lambda c: fwv[:, c, :])
                last.then_inc(S("F_pj"), 1)

            def f_s(t):
                pe.wait_ge(S("F_kx"), 4 * t + 4)
                free("SS", "f_s", t)
                scores("F").then_inc(S("F_s"), 1)

            def ft_eT(t):
                pe.wait_ge(S("F_exp"), t + 1)
                free("SS", "ft_eT", t)
                weights_T().then_inc(S("F_eTp"), 1)

            def ft_av(t):
                pe.wait_ge(S("F_eT"), t + 1)
                pe.wait_ge(S("F_vb"), 2 * t + 2)
                free("MI", "ft_av", t)
                weighted_values("F", MI).then_inc(S("F_av"), 1)

            def ft_oT(t):
                pe.wait_ge(S("F_o"), t + 1)
                free("MI", "ft_oT", t)
                turn(MI, o["F"]).then_inc(S("F_oTp"), 1)

            def ft_at(t):
                pe.wait_ge(S("F_oT"), t + 1)
                free("MI", "ft_at", t)
                for m in range(DC):
                    last = product(MI[:, m * P:(m + 1) * P], lambda c: fwo[:, c, m * P:(m + 1) * P], lambda c: oT["F"][:, c, :])
                last.then_inc(S("F_atp"), 1)

            def ft_a(t):
                pe.wait_ge(S("F_at"), t + 1)
                pe.wait_ge(S("F_x2"), 2 * t + 2)
                free("MI", "ft_a", t)
                product(MI[0:R, 0:P], lambda c: fa[:, c, :], lambda c: atT[:, c, :])
                product(MI[0:R, P:2 * P], lambda c: fa[:, c, :], lambda c: x2T[:, c, bass.ds(t * P, P)]).then_inc(S("F_ap"), 1)

            def m_half(half):
                def piece(t):
                    pe.wait_ge(S("F_gm"), t + 1)
                    free("GA", f"m_{half}", t)
                    h = lambda c: x2T[:, c, bass.ds(t * P, P)]
                    for k in range(4):
                        units = slice((4 * half + k) * P, (4 * half + k + 1) * P)
                        bank = GA[:, k * P:(k + 1) * P]
                        for c in range(DC):
                            nc.tensor.matmul(bank, win[:, c, units], h(c), start=c == 0, stop=False)
                        last = nc.tensor.matmul(bank, fb[:, units], gmT[:], start=False, stop=True)
                    last.then_inc(S("M_g"), 1)
                    free("UA", f"m_{half}", t)
                    for k in range(4):
                        units = slice((4 * half + k) * P, (4 * half + k + 1) * P)
                        last = product(UA[:, k * P:(k + 1) * P], lambda c: wup[:, c, units], h)
                    last.then_inc(S("M_u"), 1)
                return piece

            def m_down(t):
                pe.wait_ge(S("M_hid"), 2 * t + 2)
                free("GA", "m_down", t)
                for k in range(FT):
                    last = nc.tensor.matmul(GA[:, 0:D], hid[:, k, :], wdn[:, k, :], start=k == 0, stop=k == FT - 1)
                last.then_inc(S("M_dn"), 1)

            pe.wait_ge(S("w_in"), 16 * WEIGHTS)
            pe.wait_ge(S("const"), 11)
            iterate(pe, [("D", d_xT), ("Ft", ft_eT), ("M", m_half(0)), ("Ft", ft_av), ("E", e_cT), ("D", d_qk), ("Ft", ft_oT),
                         ("E", e_kv), ("M", m_half(1)), ("Ft", ft_at), ("D", d_v), ("D", d_s), ("Ft", ft_a), ("E", e_xT),
                         ("F", f_zT), ("M", m_down), ("E", e_q), ("F", f_qkv), ("D", d_eT), ("D", d_av), ("D", d_oT),
                         ("F", f_s), ("D", d_wo), ("Et", et_aT), ("Et", et_wo)])

        @block.scalar
        def _(act):
            def leave(out, bank, filled, read, done):
                def piece(t):
                    wait_if(act, S(read), t)
                    act.wait_ge(S(filled), t + 1)
                    nc.scalar.activation(out[:], bank[:, 0:D].rearrange("p (c n) -> p c n", c=DC), ACT.Copy).then_inc(S(done), 1)
                return piece

            def d_xT(t):
                wait_if(act, S("D_pv"), t)
                act.wait_ge(S("D_xTp"), t + 1)
                nc.scalar.activation(xT["D"][:].rearrange("p c s r n -> p (c s) r n"),
                                     EB[:, 0:D].rearrange("p (s n) -> p s n", n=SEQ).unsqueeze(2).to_broadcast([P, 4, 2, SEQ]),
                                     ACT.Copy).then_inc(S("D_xT"), 1)

            def exponentials(k):
                def piece(t):
                    act.wait_ge(S(k + "_arg"), t + 1)
                    nc.scalar.activation(ex[:], ex[:], ACT.Exp).then_inc(S(k + "_exp"), 1)
                return piece

            def weights_T(k, other, ahead):
                def piece(t):
                    wait_if(act, S(k + "_av"), t)
                    wait_if(act, S(other + "_av"), cap(t + ahead))
                    act.wait_ge(S(k + "_eTp"), t + 1)
                    nc.scalar.activation(eT[:], SS[:].rearrange("p b (j n) -> p (b j) n", n=P), ACT.Copy).then_inc(S(k + "_eT"), 1)
                return piece

            def f_x1(t):
                wait_if(act, S("F_pj"), t)
                act.wait_ge(S("F_zTp"), t + 1)
                for c in range(DC):
                    nc.scalar.activation(xT["F"][:, c], MI[:, c * P:(c + 1) * P].rearrange("p (s n) -> p s n", n=SEQ).unsqueeze(2)
                                         .to_broadcast([P, 2, 2, SEQ]), ACT.Identity, scale=lnw[:, c:c + 1]).then_inc(S("F_x1"), 1)

            def f_x2(t):
                act.wait_ge(S("F_zTp"), t + 1)
                for c in range(DC):
                    nc.scalar.activation(x2T[:, c, bass.ds(t * P, P)], MI[:, c * P:(c + 1) * P], ACT.Identity,
                                         scale=lnw[:, DC + c:DC + c + 1]).then_inc(S("F_x2"), 1)

            def f_qk(t):
                wait_if(act, S("F_s"), t)
                act.wait_ge(S("F_pj"), t + 1)
                nc.scalar.activation(qk["F"][:], PJ[:, 0, :].rearrange("p (m n) -> p m n", n=P), ACT.Copy).then_inc(S("F_qk"), 1)

            def ft_mod(t):
                wait_if(act, S("F_gm"), t)
                act.wait_ge(S("F_ap"), t + 1)
                nc.scalar.activation(modT[:], MI[0:R, 0:P], ACT.Tanh).then_inc(S("F_mod"), 1)

            def m_tanh(half):
                def piece(t):
                    wait_if(act, S("M_silu"), 2 * t + half)
                    act.wait_ge(S("M_g"), 2 * t + half + 1)
                    nc.scalar.activation(th[:], GA[:], ACT.Tanh, scale=0.5).then_inc(S("M_th"), 1)
                return piece

            def e_exp(t):
                act.wait_ge(S("E_sub"), t + 1)
                nc.scalar.activation(sco[:], sco[:], ACT.Exp).then_inc(S("E_exp"), 1)

            def e_keep(t):
                wait_if(act, S("E_pav"), 16 * t)
                act.wait_ge(S("E_kv"), t + 1)
                nc.scalar.activation(vE[:], kv[:, 1, :], ACT.Copy).then_inc(S("E_keep"), 1)

            act.wait_ge(S("w_in"), 16 * WEIGHTS)
            iterate(act, [("D", d_xT), ("Ft", weights_T("F", "D", 4)), ("M", m_tanh(0)),
                          ("E", leave(cT, EB, "E_cTp", "E_kvp", "E_cT")), ("Ft", leave(oT["F"], MI, "F_oTp", "F_atp", "F_oT")),
                          ("M", m_tanh(1)), ("Ft", leave(atT, MI, "F_atp", "F_ap", "F_at")), ("D", exponentials("D")),
                          ("Ft", ft_mod), ("E", leave(xTE, EB, "E_xTp", "E_qp", "E_xT")), ("F", f_x1), ("F", f_x2), ("F", f_qk),
                          ("D", weights_T("D", "F", -3)), ("D", leave(oT["D"], EB, "D_oTp", "D_wo", "D_oT")), ("E", e_exp),
                          ("E", e_keep), ("Et", leave(attT, EB, "E_aTp", "E_wo", "E_aT")), ("F", exponentials("F"))])

        @block.vector
        def _(dve):
            def row(t):
                return x_sb[:, tile(t), :].rearrange("p t d -> p (t d)")

            def statistics(k, before, per):
                def piece(t):
                    wait_if(dve, S(k + "_xn"), (3 if k == "F" else 1) * t)
                    if before:
                        dve.wait_ge(S(before), per * t + per)
                    nc.vector.bn_stats(st[k][:], row(t)).then_inc(S(k + "_st"), 1)
                    dve.wait_ge(S(k + "_st"), t + 1)
                    nc.vector.memset(mark[:], 0.0)
                    nc.vector.bn_aggr(mv[k][:], st[k][:]).then_inc(S(k + "_mv"), 1)
                    dve.wait_ge(S(k + "_mv"), t + 1)
                    nc.vector.tensor_scalar(ve[k][:, 0:1], mv[k][:, 1:2], LN_EPS, None, ALU.add).then_inc(S(k + "_ve"), 1)
                    if k == "F":
                        nc.vector.tensor_scalar(ve[k][:, 1:2], mv[k][:, 1:2], 1.0 + RMS_EPS, RMS_EPS * LN_EPS, ALU.mult,
                                                ALU.add).then_inc(S(k + "_ve"), 1)
                return piece

            def normalise(k):
                def piece(t):
                    wait_if(dve, S(k + "_xTp"), t)
                    dve.wait_ge(S(k + "_rs"), t + 1)
                    nc.vector.tensor_scalar(xn[k][:], row(t), mv[k][:, 0:1], rs[k][:, 0:1], ALU.subtract, ALU.mult).then_inc(S(k + "_xn"), 1)
                return piece

            def f_norm(t):
                wait_if(dve, S("F_zTp"), t)
                dve.wait_ge(S("F_rs"), t + 1)
                nc.vector.tensor_scalar(y[:], row(t), mv["F"][:, 0:1], rs["F"][:, 0:1], ALU.subtract, ALU.mult).then_inc(S("F_xn"), 1)
                nc.vector.tensor_scalar(xn["F"][:], row(t), mv["F"][:, 0:1], rs["F"][:, 1:2], ALU.subtract, ALU.mult).then_inc(S("F_xn"), 1)
                dve.wait_ge(S("F_xn"), 3 * t + 2)
                nc.vector.tensor_tensor(out=row(t), in0=row(t), in1=y[:], op=ALU.add).then_inc(S("F_xn"), 1)

            def d_rope(t):
                wait_if(dve, S("D_qk"), t)
                dve.wait_ge(S("D_pj"), t + 1)
                for i in range(2):
                    nc.vector.tensor_tensor(out=rt[:, i], in0=PJ[:, i, :].rearrange("p (m n) -> p m n", n=P),
                                            in1=rope[:, i, :].unsqueeze(1).to_broadcast([P, 4, P]), op=ALU.mult).then_inc(S("D_rt"), 1)

            def d_vb(t):
                wait_if(dve, S("D_av"), t)
                dve.wait_ge(S("D_pv"), t + 1)
                for h in range(2):
                    rows = slice(h * SEQ, (h + 1) * SEQ)
                    to = vbd["D"][rows].rearrange("p s (v r) h a -> p (s v) r h a", r=2)[:, :, :, h, 0:HD]
                    src = EB[rows, 0:P].rearrange("p (g d) -> p g d", d=HD).unsqueeze(2).to_broadcast([SEQ, 2 * 4, 2, HD])
                    nc.vector.tensor_copy(to, src).then_inc(S("D_vb"), 1)

            def f_vb(t):
                wait_if(dve, S("F_av"), t)
                dve.wait_ge(S("F_pj"), t + 1)
                for h in range(2):
                    rows = slice(h * SEQ, (h + 1) * SEQ)
                    to = vbd["F"][rows].rearrange("p s j h a -> p (s j) h a")[:, :, h, 0:HD]
                    src = PJ[rows, 1, :].rearrange("p (j h d) -> p j h d", h=2, d=HD)[:, :, h, :]
                    nc.vector.tensor_copy(to, src).then_inc(S("F_vb"), 1)

            def arguments(k, other, ahead):
                def piece(t):
                    ss = SS[:].rearrange("p b (h n) -> p (b h) n", n=SEQ)
                    wait_if(dve, S(k + "_arg"), t)
                    dve.wait_ge(S(k + "_s"), t + 1)
                    nc.vector.reduce_max(hm[k][:, 0, :], ss, axis=AX).then_inc(S(k + "_max"), 1)
                    dve.wait_ge(S(k + "_max"), t + 1)
                    if k == "D":
                        nc.vector.scalar_tensor_tensor(out=hm[k][:, 1, :], in0=hm[k][:, 0, :], scalar=SC, in1=sink[:], op0=ALU.mult,
                                                       op1=ALU.add).then_inc(S("D_top"), 1)
                        dve.wait_ge(S("D_top"), t + 1)
                        nc.vector.tensor_tensor(out=hm[k][:, 2, :], in0=sink[:], in1=hm[k][:, 1, :], op=ALU.subtract).then_inc(S("D_shift"), 1)
                    else:
                        nc.vector.tensor_scalar(hm[k][:, 2, :], hm[k][:, 0, :], -SC, None, ALU.mult).then_inc(S("F_shift"), 1)
                    wait_if(dve, S(k + "_eTp"), t)
                    wait_if(dve, S(other + "_eTp"), cap(t + ahead))
                    dve.wait_ge(S(k + "_shift"), t + 1)
                    nc.vector.scalar_tensor_tensor(out=ex[:], in0=ss, scalar=SC, in1=hm[k][:, 2, :].unsqueeze(2).to_broadcast([P, H, SEQ]),
                                                   op0=ALU.mult, op1=ALU.add).then_inc(S(k + "_arg"), 1)
                return piece

            def divide(k, bank):
                def piece(t):
                    av = bank[:, 0:H * AV].rearrange("p (h a) -> p h a", a=AV)
                    wait_if(dve, S(k + "_o"), t)
                    dve.wait_ge(S(k + "_av"), t + 1)
                    nc.vector.reciprocal(rec[k][:], av[:, :, HD]).then_inc(S(k + "_rec"), 1)
                    wait_if(dve, S(k + "_oTp"), t)
                    dve.wait_ge(S(k + "_rec"), t + 1)
                    nc.vector.tensor_tensor(out=o[k][:].rearrange("p (h d) -> p h d", d=HD), in0=av[:, :, 0:HD],
                                            in1=rec[k][:].unsqueeze(2).to_broadcast([P, H, HD]), op=ALU.mult).then_inc(S(k + "_o"), 1)
                return piece

            def d_x(t):
                dve.wait_ge(S("D_wo"), t + 1)
                nc.vector.tensor_tensor(out=row(t), in0=EB[:, 0:D], in1=row(t), op=ALU.add).then_inc(S("D_x"), 1)

            def e_kv(t):
                wait_if(dve, S("E_pqk"), H * t)
                wait_if(dve, S("E_keep"), t)
                dve.wait_ge(S("E_kvp"), t + 1)
                nc.vector.tensor_tensor(out=kv[:].rearrange("p k d -> p (k d)"), in0=EB[:], in1=ebkv[:], op=ALU.add).then_inc(S("E_kv"), 1)

            def e_q(t):
                wait_if(dve, S("E_pqk"), H * t)
                dve.wait_ge(S("E_qp"), t + 1)
                nc.vector.tensor_tensor(out=q[:], in0=EB[:, 0:D], in1=ebq[:], op=ALU.add).then_inc(S("E_q"), 1)

            def e_scores(t):
                wait_if(dve, S("E_pav"), H * t)
                for k in range(4):
                    dve.wait_ge(S("E_pqk"), H * t + 4 * k + 4)
                    nc.vector.reduce_sum(sco[:, 4 * k:4 * k + 4, :], prod[:, 4 * k:4 * k + 4], axis=AX).then_inc(S("E_sc"), 1)
                dve.wait_ge(S("E_sc"), 4 * t + 4)
                nc.vector.reduce_max(se[:, 0, :], sco[:], axis=AX).then_inc(S("E_max"), 1)
                dve.wait_ge(S("E_max"), t + 1)
                nc.vector.tensor_tensor(out=sco[:], in0=sco[:], in1=se[:, 0, :].unsqueeze(2).to_broadcast([P, H, H]),
                                        op=ALU.subtract).then_inc(S("E_sub"), 1)

            def e_weights(t):
                dve.wait_ge(S("E_exp"), t + 1)
                nc.vector.reduce_sum(se[:, 1, :], sco[:], axis=AX).then_inc(S("E_sum"), 1)
                dve.wait_ge(S("E_sum"), t + 1)
                nc.vector.reciprocal(se[:, 2, :], se[:, 1, :]).then_inc(S("E_rec"), 1)
                dve.wait_ge(S("E_rec"), t + 1)
                nc.vector.tensor_tensor(out=sco[:], in0=sco[:], in1=se[:, 2, :].unsqueeze(2).to_broadcast([P, H, H]),
                                        op=ALU.mult).then_inc(S("E_w"), 1)

            def et_values(t):
                wait_if(dve, S("E_aTp"), t)
                av = att[:].rearrange("p (h d) -> p h d", d=HD)
                for k in range(4):
                    dve.wait_ge(S("E_pav"), H * t + 4 * k + 4)
                    nc.vector.reduce_sum(av[:, 4 * k:4 * k + 4, :], prod[:, 4 * k:4 * k + 4], axis=AX).then_inc(S("E_att"), 1)

            def et_x(t):
                dve.wait_ge(S("E_wo"), t + 1)
                nc.vector.tensor_tensor(out=row(t), in0=EB[:, 0:D], in1=row(t), op=ALU.add).then_inc(S("E_x"), 1)
                dve.wait_ge(S("E_x"), 2 * t + 1)
                nc.vector.tensor_tensor(out=row(t), in0=row(t), in1=ebo[:], op=ALU.add).then_inc(S("E_x"), 1)

            def ft_gm(t):
                wait_if(dve, S("M_u"), 2 * t)
                dve.wait_ge(S("F_mod"), t + 1)
                nc.vector.scalar_tensor_tensor(out=gmT[:], in0=MI[0:R, P:2 * P], scalar=MOD_SCALE, in1=modT[:], op0=ALU.mult,
                                               op1=ALU.mult).then_inc(S("F_gm"), 1)

            def m_hidden(half):
                def piece(t):
                    part = hid[:, 4 * half:4 * half + 4, :].rearrange("p k n -> p (k n)")
                    wait_if(dve, S("M_dn"), t)
                    dve.wait_ge(S("M_th"), 2 * t + half + 1)
                    nc.vector.scalar_tensor_tensor(out=part, in0=th[:], scalar=1.0, in1=GA[:], op0=ALU.add, op1=ALU.mult).then_inc(S("M_silu"), 1)
                    dve.wait_ge(S("M_u"), 2 * t + half + 1)
                    dve.wait_ge(S("M_silu"), 2 * t + half + 1)
                    nc.vector.tensor_tensor(out=part, in0=part, in1=UA[:], op=ALU.mult).then_inc(S("M_hid"), 1)
                return piece

            def m_x(t):
                dve.wait_ge(S("F_xn"), 3 * t + 3)
                dve.wait_ge(S("M_dn"), t + 1)
                nc.vector.scalar_tensor_tensor(out=row(t), in0=GA[:, 0:D], scalar=0.5, in1=row(t), op0=ALU.mult,
                                               op1=ALU.add).then_inc(S("M_x"), 1)

            dve.wait_ge(S("w_in"), 16 * WEIGHTS)
            dve.wait_ge(S("const"), 11)
            iterate(dve, [("D", statistics("D", None, 0)), ("E", statistics("E", "D_x", 1)), ("F", statistics("F", "E_x", 2)),
                          ("D", normalise("D")), ("E", normalise("E")), ("F", f_norm), ("M", m_hidden(0)), ("Ft", divide("F", MI)),
                          ("D", d_rope), ("E", e_kv), ("M", m_hidden(1)), ("D", d_vb), ("Et", et_values),
                          ("D", arguments("D", "F", -3)), ("Ft", ft_gm), ("M", m_x), ("E", e_q), ("F", f_vb),
                          ("D", divide("D", EB)), ("E", e_scores), ("D", d_x), ("E", e_weights), ("Et", et_x),
                          ("F", arguments("F", "D", 4))])


def decoder(nc, a, x_in, out):
    with ExitStack() as ctx:
        x_sb = ctx.enter_context(nc.sbuf_tensor("x_sb", [P, TILES, D], F32))
        ident = ctx.enter_context(nc.sbuf_tensor("ident", [P, P], F32))
        x_loaded, masks_made = (ctx.enter_context(nc.semaphore(n)) for n in ("x_loaded", "masks_made"))

        held = []

        def new_sem(name):
            held.append(nc.alloc_semaphore(name=name))
            return held[-1]

        def clear_semaphores():
            nc.clear_and_free_semaphores(list(held))
            held.clear()
            nc.all_engine_barrier()

        with ExitStack() as first:
            tri = first.enter_context(nc.sbuf_tensor("tri", [P, P], F32))
            tri_strict, mask4 = (first.enter_context(nc.sbuf_tensor(n, [P, BT, P], F32)) for n in ("tri_strict", "mask4"))
            with nc.Block() as block:
                @block.sync
                def _(sp):
                    sp.dma_start(x_sb[:], x_in.rearrange("(t p) d -> p t d", p=P)).then_inc(x_loaded, 16)
                    sp.wait_ge(x_loaded, 16)

                @block.gpsimd
                def _(pool):
                    emit_masks(nc, pool, masks_made, ident, tri, tri_strict, mask4)

            linear_attention(nc, new_sem, x_sb, ident[:], tri[:], tri_strict[:], mask4[:], a["w_qk"], a["w_vg"], a["w_o"], a["w_beta"],
                             a["b_beta"], a["ln_cols"])
        clear_semaphores()
        wkv_and_experts(nc, new_sem, x_sb, ident[:], a["w_gate"], a["w_up"], a["w_down"], a["b_gate"], a["b_up"], a["b_down"],
                        a["w_router"], a["b_router"], a["ctx_in"], a["wu_cols"])
        clear_semaphores()
        layer_one(nc, new_sem, x_sb, ident[:], dict(a, out=out))


def head_tiles(w):
    rows, cols = w.shape
    return w.reshape(rows // P, P, cols // P, P).transpose(2, 1, 0, 3).reshape(cols // P, P, rows)


def attention_0_layout(np, i):
    heads = np.arange(H0 + 3) % H0
    by_channel = lambda a: a.reshape(H0, P, -1)
    qk = np.concatenate([head_tiles(i["L0_attn_Wq"]), head_tiles(i["L0_attn_Wk"]), by_channel(i["L0_attn_qconv_w"]),
                         by_channel(i["L0_attn_kconv_w"]), by_channel(i["L0_attn_qconv_b"]), by_channel(i["L0_attn_kconv_b"])], axis=2)
    vg = np.concatenate([head_tiles(i["L0_attn_Wv"]), head_tiles(i["L0_attn_Wg"])], axis=2)
    return {
        "w_qk": qk[heads], "w_vg": vg[heads], "w_o": i["L0_attn_Wo"].reshape(H0, P, D)[heads],
        "w_beta": i["L0_attn_Wb"].reshape(DC, P, H0).transpose(1, 0, 2),
        "b_beta": np.broadcast_to(i["L0_attn_bb"], (P, H0)),
        "ln_cols": np.stack([i["L0_attn_qn_w"], i["L0_attn_qn_b"], i["L0_attn_kn_w"], i["L0_attn_kn_b"]], axis=1),
    }


def experts_layout(np, i):
    gu, gub = i["L0_ffn_gate_up_proj"], i["L0_ffn_gate_up_proj_bias"]
    rows = lambda w: w.reshape(w.shape[0], DC, P, D).transpose(2, 0, 1, 3)
    cols = lambda v: v.reshape(-1, DC, P).transpose(2, 0, 1)
    return {
        "w_gate": rows(gu[:, :, 0::2]), "w_up": rows(gu[:, :, 1::2]), "w_down": rows(i["L0_ffn_down_proj"]),
        "b_gate": cols(gub[:, 0::2]), "b_up": cols(gub[:, 1::2]), "b_down": i["L0_ffn_down_proj_bias"],
        "w_router": i["L0_ffn_router_weight"].T.reshape(DC, P, -1).transpose(1, 0, 2),
        "b_router": np.broadcast_to(i["L0_ffn_router_bias"], (P, 8)),
        "ctx_in": i["ctx_2048"].reshape(TOK, D),
        "wu_cols": np.concatenate([i["L0_xattn_w"].reshape(DC, P).T, i["L0_xattn_u"].reshape(DC, P).T], axis=1),
    }


def layer_one_layout(np, i):
    heads, hd, kv_heads = 16, 16, 4
    half = hd // 2
    rows = lambda w: w.reshape(w.shape[0] // P, P, w.shape[1]).transpose(1, 0, 2)
    everywhere = lambda v: np.broadcast_to(v.reshape(1, -1), (P, v.size))
    columns = lambda v: v.reshape(DC, P).T
    h, f, j = (v.reshape(-1) for v in np.meshgrid(np.arange(heads), np.arange(2), np.arange(half), indexing="ij"))
    column = lambda head, f: head * hd + 2 * j + f
    wq, wk = i["L1_attn_wq"], i["L1_attn_wk"]
    shared = h // (heads // kv_heads)
    dwqk = np.concatenate([wq[:, column(h, f)], wk[:, column(shared, f)], wq[:, column(h, 1 - f)], wk[:, column(shared, 1 - f)]], axis=1)
    inv = 1.0 / np.float32(10000.0) ** (np.arange(half, dtype=np.float32) / half)
    angle = np.arange(SEQ, dtype=np.float32)[:, None] * inv.astype(np.float32)[None, :]
    place = np.arange(P) % SEQ
    channel = np.arange(P)
    cos, sin = (g(angle).astype(np.float32)[place][:, channel % half].T for g in (np.cos, np.sin))
    sign = np.where(channel % hd < half, -1.0, 1.0).astype(np.float32)[:, None]
    return {
        "dwqk": rows(dwqk), "dwv": rows(i["L1_attn_wv"]), "dwo": rows(i["L1_attn_wo"]),
        "rope": np.stack([cos, sign * sin], axis=1), "sink": everywhere(i["L1_attn_sink"]),
        "ewq": rows(i["L1_xattn_Wq"].T), "ewo": rows(i["L1_xattn_Wo"].T),
        "ewkv": rows(np.concatenate([i["L1_xattn_Wk"].T, i["L1_xattn_Wv"].T], axis=1)),
        "ebq": everywhere(i["L1_xattn_bq"]), "ebo": everywhere(i["L1_xattn_bo"]),
        "ebkv": everywhere(np.concatenate([i["L1_xattn_bk"], i["L1_xattn_bv"]])),
        "fwqk": rows(np.concatenate([i["L1_ffn_Wq"].T, i["L1_ffn_Wk"].T], axis=1)), "fwv": rows(i["L1_ffn_Wv"].T),
        "fwo": rows(i["L1_ffn_Wo"].T), "fa": rows(i["L1_ffn_A"]), "fb": i["L1_ffn_B"],
        "lnw": np.concatenate([columns(i["L1_ffn_ln1_w"]), columns(i["L1_ffn_ln2_w"])], axis=1),
        "headmask": (channel[:, None] // hd == np.arange(P // hd)[None, :]).astype(np.float32),
        "win": rows(i["L1_ffn_W_in_base"].T), "wup": rows(i["L1_ffn_W_up_base"].T), "wdn": rows(i["L1_ffn_W_down"].T),
    }


def kernel(**inputs):
    import numpy as _np
    import concourse.bacc as _bacc
    from concourse import mybir as _mybir
    from concourse.bass_utils import run_bass_kernel_spmd as _run

    laid = {"x_in": inputs["x"].reshape(TOK, D)}
    for layout in (attention_0_layout, experts_layout, layer_one_layout):
        laid.update(layout(_np, inputs))
    nc = _bacc.Bacc("TRN2", target_bir_lowering=False, num_devices=1)
    arrays, aps = {}, {}
    for name, a in laid.items():
        a = _np.ascontiguousarray(a)
        arrays[f"in_{name}_dram"] = a
        aps[name] = nc.dram_tensor(f"in_{name}_dram", a.shape, _mybir.dt.from_np(a.dtype), kind="ExternalInput").ap()
    out = nc.dram_tensor("out_0_dram", (TOK, D), _mybir.dt.float32, kind="ExternalOutput").ap()
    x_in = aps.pop("x_in")
    decoder(nc, aps, x_in, out)
    r = _run(nc, [arrays], core_ids=[0])
    return r.results[0]["out_0_dram"].reshape(SEQS, SEQ, D)
```

```python
from contextlib import ExitStack

import concourse.bass as bass
from concourse import mybir

F32 = mybir.dt.float32
BF16 = mybir.dt.bfloat16
F32R = mybir.dt.float32r
ALU = mybir.AluOpType
ACT = mybir.ActivationFunctionType

P = 128
SEQ = 64
SEQS = 64
D = 256
DC = D // P
TOK = SEQS * SEQ
TILES = TOK // P
BT = 4
BLK = BT * P
BLOCKS = TOK // BLK
H0 = 16
KW = 4
LN_EPS = 1e-5


def run_steps(eng, step):
    pairs = H0 // 2

    def one_block(b, final):
        for par in range(2):
            step(b * pairs, par, b, 0, True, False, final)
        with eng.Fori(1, pairs - 1) as hp:
            for par in range(2):
                step(b * pairs + hp, par, b, hp, False, False, final)
        for par in range(2):
            step(b * pairs + pairs - 1, par, b, pairs - 1, False, True, final)

    one_block(0, False)
    with eng.Fori(1, BLOCKS - 1) as b:
        one_block(b, False)
    one_block(BLOCKS - 1, True)


def emit_masks(nc, pool, made, ident, tri, tri_strict, mask4):
    count = 0

    def done(ins):
        nonlocal count
        ins.then_inc(made, 1)
        count += 1
        pool.wait_ge(made, count)

    def select(view, op, base, pattern, mult, fill):
        done(nc.gpsimd.affine_select(out=view, in_=view, compare_op=op, fill=fill, base=base, pattern=pattern,
                                     channel_multiplier=mult))

    done(nc.gpsimd.memset(ident[:], 0.0))
    select(ident[:], ALU.not_equal, 0, [[-1, P]], 1, 1.0)
    for m in (tri, tri_strict, mask4):
        done(nc.gpsimd.memset(m[:], 1.0))
    select(tri[:], ALU.is_ge, 0, [[1, P]], -1, 0.0)
    select(mask4[:], ALU.is_ge, 0, [[0, BT], [1, P]], -1, 0.0)
    select(tri_strict[:], ALU.is_gt, 0, [[0, BT], [-1, P]], 1, 0.0)
    select(tri[:, SEQ:], ALU.is_ge, -SEQ, [[0, SEQ]], 1, 0.0)
    select(mask4[:, :, SEQ:], ALU.is_ge, -SEQ, [[0, BT], [0, SEQ]], 1, 0.0)
    select(tri_strict[:, :, 0:SEQ], ALU.is_gt, SEQ, [[0, BT], [0, SEQ]], -1, 0.0)


def linear_attention(nc, new_sem, x_sb, ident, tri, tri_strict, mask4, w_qk, w_vg, w_o, w_beta, b_beta, ln_cols):
    NW = 2 * DC * P
    TAPQ, TAPK, BQ, BK = NW, NW + KW, NW + 2 * KW, NW + 2 * KW + 1
    PAIRS = H0 // 2
    with ExitStack() as ctx:
        def sb(name, shape, dt=F32):
            return ctx.enter_context(nc.sbuf_tensor("a_" + name, shape, dt))

        def two(name, shape):
            return [sb(f"{name}{i}", shape) for i in range(2)]

        def psum(name, shape, dt=F32):
            return ctx.enter_context(nc.psum_tensor("a_" + name, shape, dt))

        def sem(name):
            return new_sem("a_" + name)

        wqk = two("wqk", [P, NW + 2 * KW + 2])
        wvg = two("wvg", [P, NW])
        wqk_hi, wqk_lo = ([sb(f"{n}{i}", [P, NW], F32R) for i in range(2)] for n in ("wqk_hi", "wqk_lo"))
        wg_hi, wg_lo = ([sb(f"{n}{i}", [P, DC * P], F32R) for i in range(2)] for n in ("wg_hi", "wg_lo"))
        wo = two("wo", [P, D])
        wbeta, bbeta, lncol = sb("wbeta", [P, DC, H0]), sb("bbeta", [P, H0]), sb("lncol", [P, 4])
        neghalf = sb("neghalf", [P, TILES])
        x_hi, x_lo = sb("x_hi", [P, DC, TOK], F32R), sb("x_lo", [P, DC, TOK], F32R)
        xv = sb("xv", [P, DC, BLK])
        st, mv = sb("st", [P, TILES, 6]), sb("mv", [P, TILES, 2])
        ve, rs = sb("ve", [P, TILES]), sb("rs", [P, TILES])
        z, u1, u2, spz = (sb(n, [P, TILES, H0]) for n in ("z", "u1", "u2", "spz"))
        lnd, beta = sb("lnd", [P, TILES, H0]), sb("beta", [P, TILES, H0])
        cq, ck, tq, tk = (two(n, [P, BLK]) for n in ("cq", "ck", "tq", "tk"))
        sq, sk = tq, tk
        qn, kn, qh, kh = two("qn", [P, BT, P]), two("kn", [P, BT, P]), two("qh", [P, BLK]), two("kh", [P, BLK])
        hst, hm = two("hst", [P, 2 * BT, 6]), two("hm", [P, 4, 2 * BT])
        hve, hrs, hnb = (two(n, [P, 2 * BT]) for n in ("hve", "hrs", "hnb"))
        vs, tg = two("vs", [P, BT, P]), two("tg", [P, BLK])
        gs = tg
        dlt, mb = sb("dlt", [P, BT, P]), sb("mb", [P, BT, P])
        ex = two("ex", [P, BT, P])
        em = at = ex
        og = two("og", [P, BLK])
        xn = cq[0][:], ck[0][:], tq[0][:], tk[0][:]

        QK = [psum(f"QK{i}", [P, 2, BLK]) for i in range(2)]
        X0, X1, Y = psum("X0", [P, BLK]), psum("X1", [P, BLK]), psum("Y", [P, BT, D])

        wqk_in, wvg_in, wo_in = ([sem(f"{n}{i}") for i in range(2)] for n in ("wqk_in", "wvg_in", "wo_in"))
        const_in, const_set = sem("const_in"), sem("const_set")
        xstat, xvar, xrstd, xnorm, xT, xvc, xTc, zmm, zc, zmath, zact, xv_set = (sem(n) for n in (
            "xstat", "xvar", "xrstd", "xnorm", "xT", "xvc", "xTc", "zmm", "zc", "zmath", "zact", "xv_set"))
        s_qk, s_fwd, s_arg, s_g, s_v, s_bck, s_s, s_y, s_o = (sem(n) for n in (
            "qk", "fwd", "arg", "g", "v", "bck", "s", "y", "o"))
        s_ex, s_tap0, s_norm, s_tg, s_vc, s_tanh, s_qkh = (sem(n) for n in (
            "ex", "tap0", "norm", "tg", "vc", "tanh", "qkh"))
        s_hstat, s_hmath, s_hvar, s_hnb, s_conv, s_silu, s_gs, s_at, s_og, s_yout = (sem(n) for n in (
            "hstat", "hmath", "hvar", "hnb", "conv", "silu", "gs", "at", "og", "yout"))
        s_em, s_hrstd, s_dl = sem("em"), sem("hrstd"), sem("dl")
        xlo, qk_hi, qk_lo, vg_hi, vg_lo = (sem(n) for n in ("xlo", "qk_hi", "qk_lo", "vg_hi", "vg_lo"))
        block = ctx.enter_context(nc.Block())

        @block.sync
        def _(sp):
            for dst, src in ((wbeta[:], w_beta), (bbeta[:], b_beta), (lncol[:], ln_cols)):
                sp.dma_start(dst, src).then_inc(const_in, 16)

            def load_qk(row, p):
                sp.dma_start(wqk[p][:], w_qk[row, :, :]).then_inc(wqk_in[p], 16)

            def load_vg(row, p):
                sp.dma_start(wvg[p][:], w_vg[row, :, :]).then_inc(wvg_in[p], 16)

            def load_o(row, p):
                sp.dma_start(wo[p][:], w_o[row, :, :]).then_inc(wo_in[p], 16)

            load_qk(0, 0)
            load_qk(1, 1)
            load_vg(0, 0)
            load_o(0, 0)
            sp.wait_ge(s_conv, 6)
            load_qk(2, 0)

            def ahead(g, hp, par):
                n = 2 * g + par
                sp.wait_ge(s_conv, 6 * n + 12)
                load_qk(bass.ds(2 * hp + par + 3, 1), 1 - par)
                sp.wait_ge(s_v, n)
                load_vg(bass.ds(2 * hp + par + 1, 1), 1 - par)
                sp.wait_ge(s_y, n)
                load_o(bass.ds(2 * hp + par + 1, 1), 1 - par)

            for par in range(2):
                ahead(0, 0, par)
            with sp.Fori(1, PAIRS) as hp:
                for par in range(2):
                    ahead(hp, hp, par)
            with sp.Fori(1, BLOCKS - 1) as b:
                with sp.Fori(0, PAIRS) as hp:
                    for par in range(2):
                        ahead(b * PAIRS + hp, hp, par)
            with sp.Fori(0, PAIRS - 1) as hp:
                for par in range(2):
                    ahead((BLOCKS - 1) * PAIRS + hp, hp, par)
            n = BLOCKS * H0 - 2
            sp.wait_ge(s_v, n)
            load_vg(H0 - 1, 1)
            sp.wait_ge(s_y, n)
            load_o(H0 - 1, 1)
            sp.wait_ge(wqk_in[0], 16 * (BLOCKS * PAIRS + 1))

        @block.gpsimd
        def _(pool):
            nc.gpsimd.memset(neghalf[:], -0.5).then_inc(const_set, 1)
            pool.wait_ge(const_set, 1)
            pool.wait_ge(xvar, 1)
            nc.gpsimd.tensor_tensor(out=rs[:], in0=ve[:], in1=neghalf[:], op=ALU.pow).then_inc(xrstd, 1)

            def rstd(m, p):
                pool.wait_ge(s_hvar, m + 1)
                nc.gpsimd.tensor_tensor(out=hrs[p][:], in0=hve[p][:], in1=neghalf[:, 0:2 * BT], op=ALU.pow).then_inc(s_hrstd, 1)

            def decay(m, p, blk, head):
                tiles = bass.ds(blk * BT, BT)
                pool.wait_ge(s_dl, 2 * m)
                nc.gpsimd.tensor_tensor(out=dlt[:], in0=tri_strict, in1=lnd[:, tiles, bass.ds(head, 1)].to_broadcast([P, BT, P]),
                                        op=ALU.mult).then_inc(s_dl, 1)
                nc.gpsimd.tensor_tensor(out=mb[:], in0=mask4, in1=beta[:, tiles, bass.ds(head, 1)].to_broadcast([P, BT, P]),
                                        op=ALU.mult).then_inc(s_dl, 1)

            def low_parts(hi, lo, w, high, low, m):
                pool.wait_ge(high, m + 1)
                nc.gpsimd.tensor_tensor(out=lo[:], in0=w, in1=hi[:].bitcast(F32), op=ALU.subtract).then_inc(low, 1)

            def low_qk(m, p):
                low_parts(wqk_hi[p], wqk_lo[p], wqk[p][:, 0:NW], qk_hi, qk_lo, m)

            def low_vg(m, p):
                low_parts(wg_hi[p], wg_lo[p], wvg[p][:, DC * P:NW], vg_hi, vg_lo, m)

            def step(g, par, b, hp, first, last, final):
                n = 2 * g + par
                if not (final and last and par == 1):
                    pool.wait_ge(s_norm, 8 * n + 8)
                    rstd(n + 1, 1 - par)
                pool.wait_ge(s_ex, n + 1)
                pool.wait_ge(s_dl, 2 * n + 2)
                pool.wait_ge(s_at, n)
                nc.gpsimd.tensor_tensor(out=em[par][:], in0=ex[par][:], in1=mb[:], op=ALU.mult).then_inc(s_em, 1)
                if final and last and par == 1:
                    return
                cross = last and par == 1
                pool.wait_ge(s_em, n + 1)
                decay(n + 1, 1 - par, b + 1 if cross else b, 0 if cross else 2 * hp + par + 1)
                if not (final and last):
                    low_qk(n + 3, 1 - par)
                low_vg(n + 1, 1 - par)

            def low_x(b):
                pool.wait_ge(xTc, 2 * b + 2)
                nc.gpsimd.tensor_tensor(out=x_lo[:, :, bass.ds(b * BLK, BLK)], in0=xv[:], in1=x_hi[:, :, bass.ds(b * BLK, BLK)].bitcast(F32),
                                        op=ALU.subtract).then_inc(xlo, 1)

            with pool.Fori(0, BLOCKS) as b:
                low_x(b)
            low_vg(0, 0)
            for m in range(3):
                low_qk(m, m % 2)
            pool.wait_ge(zact, 3)
            pool.wait_ge(zmath, 4)
            pool.wait_ge(xTc, 2 * BLOCKS)
            pool.wait_ge(zmm, BLOCKS)
            decay(0, 0, 0, 0)
            rstd(0, 0)
            run_steps(pool, step)

        @block.tensor
        def _(pe):
            pe.wait_ge(const_in, 48)

            def transpose_block(b, p):
                for i in range(BT):
                    pe.wait_ge(xnorm, 4 * b + i + 1)
                    for c in range(DC):
                        last = nc.tensor.transpose(QK[p][:, c, i * P:(i + 1) * P], xn[i][:, c * P:(c + 1) * P], ident)
                    last.then_inc(xT, 1)

            def beta_logits(bb):
                for p in range(2):
                    b = 2 * bb + p
                    pe.wait_ge(xTc, 4 * bb)
                    transpose_block(b, p)
                    pe.wait_ge(xvc, 2 * b + 2)
                    pe.wait_ge(zc, b)
                    for j in range(BT):
                        for c in range(DC):
                            last = nc.tensor.matmul(X0[:, j * H0:(j + 1) * H0], xv[:, c, j * P:(j + 1) * P], wbeta[:, c, :],
                                                    start=c == 0, stop=c == DC - 1)
                    last.then_inc(zmm, 1)

            beta_logits(0)
            with pe.Fori(1, BLOCKS // 2) as bb:
                beta_logits(bb)

            def split_product(out, lhs, rhs):
                passes = [(c, i, j) for c in range(DC) for i, j in ((0, 0), (0, 1), (1, 0))]
                for c, i, j in passes:
                    last = nc.tensor.matmul(out, lhs[i](c), rhs[j](c), start=(c, i, j) == passes[0], stop=(c, i, j) == passes[-1])
                return last

            def columns(ws, first):
                return [lambda c, w=w: w[:, (first + c) * P:(first + c + 1) * P] for w in ws]

            def block_of_x(blk):
                return [lambda c, x=x: x[:, c, bass.ds(blk * BLK, BLK)] for x in (x_hi, x_lo)]

            def proj_qk(m, p, blk):
                pe.wait_ge(qk_lo, m + 1)
                for i in range(2):
                    split_product(QK[p][:, i, :], columns((wqk_hi[p], wqk_lo[p]), i * DC), block_of_x(blk)).then_inc(s_qk, 1)

            def forward(m, p):
                pe.wait_ge(s_silu, 2 * m + 2)
                for i, s in enumerate((sq, sk)):
                    for j in range(BT):
                        last = nc.tensor.transpose(QK[p][:, i, j * P:(j + 1) * P], s[p][:, j * P:(j + 1) * P], ident)
                last.then_inc(s_fwd, 1)

            def back(m, p):
                pe.wait_ge(s_norm, 8 * m + 8)
                for i, s in enumerate((qn, kn)):
                    for j in range(BT):
                        last = nc.tensor.transpose(QK[p][:, i, j * P:(j + 1) * P], s[p][:, j, :], ident)
                last.then_inc(s_bck, 1)

            def out_proj(m, p, arrived, blk, starts):
                pe.wait_ge(wo_in[p], arrived)
                pe.wait_ge(s_og, m + 1)
                if starts:
                    pe.wait_ge(s_yout, 2 * blk)
                for j in range(BT):
                    last = nc.tensor.matmul(Y[:, j, :], og[p][:, j * P:(j + 1) * P], wo[p][:], start=starts and j % 2 == 0,
                                            stop=True, skip_group_check=True)
                last.then_inc(s_y, 1)

            def step(g, par, b, hp, first, last_pair, final):
                n = 2 * g + par
                q = 1 - par
                end = final and last_pair
                if not (end and par == 1):
                    forward(n + 1, q)
                pe.wait_ge(s_dl, 2 * n + 2)
                pe.wait_ge(s_at, n)
                for j in range(BT):
                    last = nc.tensor.matmul(X1[:, j * P:(j + 1) * P], dlt[:, j, :], tri, start=True, stop=True)
                last.then_inc(s_arg, 1)
                if not end:
                    pe.wait_ge(s_qkh, 2 * n + 2)
                    proj_qk(n + 2, par, b + 1 if last_pair else b)
                pe.wait_ge(vg_lo, n + 1)
                pe.wait_ge(s_ex, n + 1)
                split_product(X1[:], columns((wg_hi[par], wg_lo[par]), 0), block_of_x(b)).then_inc(s_g, 1)
                pe.wait_ge(s_og, n)
                if first and par == 0:
                    pe.wait_ge(xv_set, b + 1)
                for j in range(BT):
                    for c in range(DC):
                        last = nc.tensor.matmul(X0[:, j * P:(j + 1) * P], xv[:, c, j * P:(j + 1) * P], wvg[par][:, c * P:(c + 1) * P],
                                                start=c == 0, stop=c == DC - 1)
                last.then_inc(s_v, 1)
                pe.wait_ge(s_qkh, 2 * n + 2)
                pe.wait_ge(s_gs, n + 1)
                for j in range(BT):
                    last = nc.tensor.matmul(X1[:, j * P:(j + 1) * P], kh[par][:, j * P:(j + 1) * P],
                                            qh[par][:, j * P:(j + 1) * P], start=True, stop=True)
                last.then_inc(s_s, 1)
                if par == 1:
                    out_proj(n - 1, 0, 16 * (g + 1), b, first)
                elif not first:
                    out_proj(n - 1, 1, 16 * g, b, False)
                if not (end and par == 1):
                    back(n + 1, q)
                pe.wait_ge(s_at, n + 1)
                pe.wait_ge(s_vc, n + 1)
                for j in range(BT):
                    last = nc.tensor.matmul(X0[:, j * P:(j + 1) * P], vs[par][:, j, :], at[par][:, j, :], start=True, stop=True)
                last.then_inc(s_o, 1)
                if last_pair and par == 1:
                    out_proj(n, 1, 16 * (g + 1), b, False)

            pe.wait_ge(xlo, BLOCKS)
            proj_qk(0, 0, 0)
            proj_qk(1, 1, 0)
            forward(0, 0)
            back(0, 0)
            run_steps(pe, step)

        @block.scalar
        def _(act):
            def transposed(bb):
                for p in range(2):
                    b = 2 * bb + p
                    act.wait_ge(xT, 4 * b + 4)
                    act.wait_ge(zmm, b)
                    act.wait_ge(xlo, b)
                    nc.scalar.activation(xv[:], QK[p][:], ACT.Copy).then_inc(xvc, 2)
                    act.wait_ge(xvc, 2 * b + 2)
                    nc.scalar.activation(x_hi[:, :, bass.ds(b * BLK, BLK)], xv[:], ACT.Copy).then_inc(xTc, 2)

            transposed(0)
            with act.Fori(1, BLOCKS // 2) as bb:
                transposed(bb)
            act.wait_ge(zmath, 1)
            nc.scalar.activation(u2[:], u1[:], ACT.Exp, scale=-1.0).then_inc(zact, 1)
            act.wait_ge(zact, 1)
            nc.scalar.activation(u1[:], u2[:], ACT.Ln, bias=1.0).then_inc(zact, 1)
            act.wait_ge(zmath, 4)
            nc.scalar.activation(beta[:], u2[:], ACT.Exp).then_inc(zact, 1)

            def front(m, p):
                for i, (c, tap, bias) in enumerate(((cq, TAPQ, BQ), (ck, TAPK, BK))):
                    act.wait_ge(s_qk, 2 * m + 1 + i)
                    nc.scalar.activation(c[p][:], QK[p][:, i, :], ACT.Identity, bias=wqk[p][:, bias:bias + 1],
                                         scale=wqk[p][:, tap + KW - 1:tap + KW]).then_inc(s_tap0, 1)

            def front_tanh(m, p):
                for i, (c, t) in enumerate(((cq, tq), (ck, tk))):
                    act.wait_ge(s_conv, 6 * m + 5 + i)
                    nc.scalar.activation(t[p][:], c[p][:], ACT.Tanh, scale=0.5).then_inc(s_tanh, 1)

            def normalise(m, p):
                act.wait_ge(s_hrstd, m + 1)
                act.wait_ge(s_hnb, m + 1)
                for i, s in enumerate((qn, kn)):
                    for j in range(BT):
                        k = i * BT + j
                        nc.scalar.activation(s[p][:, j, :], QK[p][:, i, j * P:(j + 1) * P], ACT.Identity,
                                             bias=hnb[p][:, k:k + 1], scale=hrs[p][:, k:k + 1]).then_inc(s_norm, 1)

            def leave(m, p):
                act.wait_ge(s_bck, m + 1)
                for i, h in enumerate((qh, kh)):
                    nc.scalar.activation(h[p][:], QK[p][:, i, :], ACT.Identity, bias=lncol[:, 2 * i + 1:2 * i + 2],
                                         scale=lncol[:, 2 * i:2 * i + 1]).then_inc(s_qkh, 1)

            def high_qk(m, p, arrived):
                act.wait_ge(wqk_in[p], arrived)
                act.wait_ge(s_qk, 2 * m - 2)
                nc.scalar.activation(wqk_hi[p][:], wqk[p][:, 0:NW], ACT.Copy).then_inc(qk_hi, 1)

            def high_vg(m, p, arrived):
                act.wait_ge(wvg_in[p], arrived)
                act.wait_ge(s_v, m - 1)
                nc.scalar.activation(wg_hi[p][:], wvg[p][:, DC * P:NW], ACT.Copy).then_inc(vg_hi, 1)

            def step(g, par, b, hp, first, last_pair, final):
                n = 2 * g + par
                q = 1 - par
                end = final and last_pair
                act.wait_ge(s_arg, n + 1)
                nc.scalar.activation(ex[par][:], X1[:], ACT.Exp).then_inc(s_ex, 1)
                if not end:
                    front(n + 2, par)
                act.wait_ge(s_g, n + 1)
                nc.scalar.activation(tg[par][:], X1[:], ACT.Tanh, scale=0.5).then_inc(s_tg, 1)
                if not (end and par == 1):
                    normalise(n + 1, q)
                act.wait_ge(s_v, n + 1)
                nc.scalar.activation(vs[par][:], X0[:], ACT.Copy).then_inc(s_vc, 1)
                if not end:
                    front_tanh(n + 2, par)
                    high_qk(n + 3, q, 16 * (g + 2 + par))
                if not (end and par == 1):
                    high_vg(n + 1, q, 16 * (g + 1 + par))
                    leave(n + 1, q)

            act.wait_ge(const_in, 48)
            act.wait_ge(xTc, 2 * BLOCKS)
            act.wait_ge(wqk_in[0], 16)
            nc.scalar.activation(wqk_hi[0][:], wqk[0][:, 0:NW], ACT.Copy).then_inc(qk_hi, 1)
            act.wait_ge(wqk_in[1], 16)
            nc.scalar.activation(wqk_hi[1][:], wqk[1][:, 0:NW], ACT.Copy).then_inc(qk_hi, 1)
            act.wait_ge(wvg_in[0], 16)
            nc.scalar.activation(wg_hi[0][:], wvg[0][:, DC * P:NW], ACT.Copy).then_inc(vg_hi, 1)
            front(0, 0)
            front_tanh(0, 0)
            high_qk(2, 0, 32)
            front(1, 1)
            front_tanh(1, 1)
            normalise(0, 0)
            leave(0, 0)
            run_steps(act, step)

        @block.vector
        def _(dve):
            with dve.Fori(0, TILES) as t:
                nc.vector.bn_stats(st[:, bass.ds(t, 1), :], x_sb[:, bass.ds(t, 1), :]).then_inc(xstat, 1)
            dve.wait_ge(xstat, TILES)
            for t in range(TILES):
                nc.vector.bn_aggr(mv[:, t, :], st[:, t, :]).then_inc(xstat, 1)
            dve.wait_ge(xstat, 2 * TILES)
            nc.vector.tensor_scalar(ve[:], mv[:, :, 1], LN_EPS, None, ALU.add).then_inc(xvar, 1)
            dve.wait_ge(xrstd, 1)

            def normalise_block(b):
                dve.wait_ge(xT, 4 * b)
                for i in range(BT):
                    t = b * BT + i
                    nc.vector.tensor_scalar(xn[i][:, 0:D], x_sb[:, bass.ds(t, 1), :], mv[:, bass.ds(t, 1), 0:1], rs[:, bass.ds(t, 1)],
                                            ALU.subtract, ALU.mult).then_inc(xnorm, 1)
                dve.wait_ge(const_in, 48)
                dve.wait_ge(zmm, b + 1)
                nc.vector.tensor_tensor(out=z[:, bass.ds(b * BT, BT), :], in0=X0[:, 0:BT * H0].rearrange("p (j h) -> p j h", j=BT),
                                        in1=bbeta[:].unsqueeze(1).to_broadcast([P, BT, H0]), op=ALU.add).then_inc(zc, 1)

            normalise_block(0)
            with dve.Fori(1, BLOCKS) as b:
                normalise_block(b)
            dve.wait_ge(zc, BLOCKS)
            nc.vector.scalar_tensor_tensor(out=u1[:], in0=z[:], scalar=-1.0, in1=z[:], op0=ALU.mult, op1=ALU.max).then_inc(zmath, 1)
            dve.wait_ge(zact, 2)
            nc.vector.scalar_tensor_tensor(out=spz[:], in0=z[:], scalar=0.0, in1=u1[:], op0=ALU.max, op1=ALU.add).then_inc(zmath, 1)
            dve.wait_ge(zmath, 2)
            nc.vector.tensor_scalar(lnd[:], spz[:], -1.0, None, ALU.mult).then_inc(zmath, 1)
            nc.vector.tensor_tensor(out=u2[:], in0=z[:], in1=spz[:], op=ALU.subtract).then_inc(zmath, 1)

            def conv(m, p, taps=range(KW - 2, -1, -1), of=range(2)):
                for k in taps:
                    back = KW - 1 - k
                    for i in of:
                        c, tap = ((cq, TAPQ), (ck, TAPK))[i]
                        if k == KW - 2:
                            dve.wait_ge(s_tap0, 2 * m + 1 + i)
                        else:
                            dve.wait_ge(s_conv, 6 * m + 2 * (KW - 2 - k) + i - 1)
                        acc = c[p][:].rearrange("p (s t) -> p s t", t=SEQ)[:, :, back:]
                        src = QK[p][:, i, :].rearrange("p (s t) -> p s t", t=SEQ)[:, :, :SEQ - back]
                        nc.vector.scalar_tensor_tensor(out=acc, in0=src, scalar=wqk[p][:, tap + k:tap + k + 1], in1=acc,
                                                       op0=ALU.mult, op1=ALU.add).then_inc(s_conv, 1)

            def silu(m, p):
                for i, (c, t, s) in enumerate(((cq, tq, sq), (ck, tk, sk))):
                    dve.wait_ge(s_tanh, 2 * m + 1 + i)
                    nc.vector.scalar_tensor_tensor(out=s[p][:], in0=t[p][:], scalar=1.0, in1=c[p][:],
                                                   op0=ALU.add, op1=ALU.mult).then_inc(s_silu, 1)

            def stats(m, p):
                dve.wait_ge(s_fwd, m + 1)
                for i in range(2):
                    for j in range(BT):
                        nc.vector.bn_stats(hst[p][:, i * BT + j, :], QK[p][:, i, j * P:(j + 1) * P]).then_inc(s_hstat, 1)
                me, mo, Me, Mo = (hst[p][:, :, k] for k in (1, 4, 2, 5))
                sm, df, m2, d2 = (hm[p][:, k, :] for k in range(4))
                dve.wait_ge(s_hstat, 8 * m + 8)
                nc.vector.tensor_tensor(out=df, in0=me, in1=mo, op=ALU.subtract).then_inc(s_hmath, 1)
                nc.vector.scalar_tensor_tensor(out=m2, in0=Me, scalar=P * 4 * LN_EPS, in1=Mo, op0=ALU.add, op1=ALU.add).then_inc(s_hmath, 1)
                nc.vector.tensor_tensor(out=sm, in0=me, in1=mo, op=ALU.add).then_inc(s_hmath, 1)
                dve.wait_ge(s_hmath, 4 * m + 3)
                nc.vector.scalar_tensor_tensor(out=d2, in0=df, scalar=0.25, in1=df, op0=ALU.mult, op1=ALU.mult).then_inc(s_hmath, 1)
                dve.wait_ge(s_hmath, 4 * m + 4)
                nc.vector.scalar_tensor_tensor(out=hve[p][:], in0=m2, scalar=1.0 / P, in1=d2, op0=ALU.mult, op1=ALU.add).then_inc(s_hvar, 1)

            def shift(m, p):
                dve.wait_ge(s_hrstd, m + 1)
                nc.vector.scalar_tensor_tensor(out=hnb[p][:], in0=hm[p][:, 0, :], scalar=-0.5, in1=hrs[p][:],
                                               op0=ALU.mult, op1=ALU.mult).then_inc(s_hnb, 1)

            def step(g, par, b, hp, first, last_pair, final):
                n = 2 * g + par
                q = 1 - par
                end = final and last_pair
                if first and par == 0:
                    dve.wait_ge(s_v, b * H0)
                    high, low = (x[:, :, bass.ds(b * BLK, BLK)].bitcast(F32) for x in (x_hi, x_lo))
                    nc.vector.tensor_tensor(out=xv[:], in0=high, in1=low, op=ALU.add).then_inc(xv_set, 1)
                if not (end and par == 1):
                    stats(n + 1, q)
                if not end:
                    conv(n + 2, par, [KW - 2], [0])
                if not (end and par == 1):
                    shift(n + 1, q)
                if not end:
                    conv(n + 2, par, [KW - 2], [1])
                dve.wait_ge(s_tg, n + 1)
                nc.vector.scalar_tensor_tensor(out=gs[par][:], in0=tg[par][:], scalar=1.0, in1=X1[:], op0=ALU.add, op1=ALU.mult).then_inc(s_gs, 1)
                if not end:
                    conv(n + 2, par, range(KW - 3, -1, -1))
                dve.wait_ge(s_s, n + 1)
                dve.wait_ge(s_em, n + 1)
                nc.vector.tensor_tensor(out=at[par][:], in0=X1[:].rearrange("p (j t) -> p j t", j=BT), in1=em[par][:], op=ALU.mult).then_inc(s_at, 1)
                if not end:
                    silu(n + 2, par)
                dve.wait_ge(s_o, n + 1)
                nc.vector.scalar_tensor_tensor(out=og[par][:], in0=X0[:], scalar=0.5, in1=gs[par][:], op0=ALU.mult, op1=ALU.mult).then_inc(s_og, 1)
                if last_pair and par == 1:
                    dve.wait_ge(s_y, n + 1)
                    for i in range(2):
                        xs = x_sb[:, bass.ds(b * BT + 2 * i, 2), :]
                        nc.vector.tensor_tensor(out=xs, in0=Y[:, 2 * i:2 * i + 2, :], in1=xs, op=ALU.add).then_inc(s_yout, 1)

            dve.wait_ge(xT, 4 * BLOCKS)
            dve.wait_ge(xlo, BLOCKS)
            dve.wait_ge(zmm, BLOCKS)
            conv(0, 0)
            silu(0, 0)
            conv(1, 1)
            silu(1, 1)
            stats(0, 0)
            shift(0, 0)
            run_steps(dve, step)
            dve.wait_ge(s_yout, 2 * BLOCKS)


def wkv_and_experts(nc, new_sem, x_sb, ident, w_gate, w_up, w_down, b_gate, b_up, b_down, w_router, b_router, ctx_in, wu_cols):
    E = 8
    LIMIT, ALPHA = 7.0, 1.702
    NEG = -1e38
    SEG = SEQ + 1
    NS = DC * BLK // SEQ
    HALF = NS // DC
    with ExitStack() as ctx:
        def sb(name, shape, dt=F32):
            return ctx.enter_context(nc.sbuf_tensor("m_" + name, shape, dt))

        def two(name, shape):
            return [sb(f"{name}{i}", shape) for i in range(2)]

        def psum(name, shape, dt=F32):
            return ctx.enter_context(nc.psum_tensor("m_" + name, shape, dt))

        def sem(name):
            return new_sem("m_" + name)

        wg, wu, wd = sb("wg", [P, E, DC, D]), sb("wu", [P, E, DC, D]), sb("wd", [P, E, DC, D])
        bg, bu = sb("bg", [P, E, DC]), sb("bu", [P, E, DC])
        bd = sb("bd", [E, D])
        rw, rb = sb("rw", [P, DC, E]), sb("rb", [P, E])
        wuc = sb("wuc", [P, 2 * DC])
        neghalf, iota = sb("neghalf", [P, BT]), sb("iota", [P, E])
        mark = sb("mark", [P, 1])
        ctx_t, xn = sb("ctx_t", [P, BT, D]), sb("xn", [P, BT, D])
        st, mv, ve, rs = sb("st", [P, BT, 6]), sb("mv", [P, BT, 2]), sb("ve", [P, BT]), sb("rs", [P, BT])
        kp, wp, op, a2, e2, ev, pp, qp = (sb(n, [P, NS, SEG]) for n in ("kp", "wp", "op", "a2", "e2", "ev", "pp", "qp"))
        vt, d1, d2, ae, ee = (sb(n, [P, NS, SEQ]) for n in ("vt", "d1", "d2", "ae", "ee"))
        hT = sb("hT", [P, DC, TOK])
        hb = sb("hb", [P, DC, BLK])
        lg, mx8 = sb("lg", [P, BT, E]), sb("mx8", [P, BT, E])
        ix8 = sb("ix8", [P, BT, E], mybir.dt.uint32)
        ixf, te, wt, oh = sb("ixf", [P, BT, 2]), sb("te", [P, 4, BT]), sb("wt", [P, 2, BT]), sb("oh", [P, 2, BT, E])
        sc = sb("sc", [P, TILES, E])
        sT = sb("sT", [E, BLK])
        gp, th, ur = two("gp", [P, DC, BLK]), two("th", [P, DC, BLK]), two("ur", [P, DC, BLK])

        G, U = psum("G", [P, DC, BLK]), psum("U", [P, DC, BLK])
        O, T = psum("O", [P, BT, D]), psum("T", [P, DC, BLK])
        Tt = T[:].rearrange("p c (j d) -> p (c j) d", d=D)

        w_in, experts_in, ctx_loaded, const_set = sem("w_in"), sem("experts_in"), sem("ctx_loaded"), sem("const_set")
        (stat, var, rstd, norm, cT, kT, vev, kev, scan_o, dif, clip, exps, qscan, pscan, ev_mul, den, num, rec, yv, yT, yadd,
         hTr, hev, hcp, rout, lgs, top, texp, wts_, score, sTr, sTe, bias, biasadd) = (sem(n) for n in (
             "stat", "var", "rstd", "norm", "cT", "kT", "vev", "kev", "scan_o", "dif", "clip", "exps", "qscan", "pscan",
             "ev_mul", "den", "num", "rec", "yv", "yT", "yadd", "hTr", "hev", "hcp", "rout", "lgs", "top", "texp", "wts",
             "score", "sTr", "sTe", "bias", "biasadd"))
        lgs_oh = sem("lgs_oh")
        s_gu, s_d, s_gp, s_ue, s_th, s_uc, s_gl, s_act, s_acc = (sem(n) for n in (
            "gu", "d", "gp", "ue", "th", "uc", "gl", "act", "acc"))
        block = ctx.enter_context(nc.Block())

        def tiles(b):
            return bass.ds(b * BT, BT)

        def run_blocks(eng, pieces, step):
            for e in range(E):
                if e in pieces:
                    pieces[e](0)

            def one(b, nb):
                for e in range(E):
                    step(b, e, nb, lambda: pieces[e](nb) if nb is not None and e in pieces else None)
            step(0, -1, 0, lambda: None)
            one(0, 1)
            with eng.Fori(1, BLOCKS - 1) as b:
                one(b, b + 1)
            one(BLOCKS - 1, None)

        @block.sync
        def _(sp):
            loads = ((wuc[:], wu_cols), (rw[:], w_router), (rb[:], b_router), (bg[:], b_gate), (bu[:], b_up), (bd[:], b_down),
                     (wg[:], w_gate), (wu[:], w_up), (wd[:], w_down))
            for i, (dst, src) in enumerate(loads):
                sp.dma_start(dst, src).then_inc(w_in if i < 6 else experts_in, 16)
                if i == 2:
                    sp.dma_start(ctx_t[:], ctx_in[0:BLK, :].rearrange("(j p) d -> p j d", p=P)).then_inc(ctx_loaded, 16)
            with sp.Fori(1, BLOCKS) as b:
                sp.wait_ge(cT, b)
                sp.dma_start(ctx_t[:], ctx_in[bass.ds(b * BLK, BLK), :].rearrange("(j p) d -> p j d", p=P)).then_inc(ctx_loaded, 16)

        @block.gpsimd
        def _(pool):
            steps = [nc.gpsimd.memset(neghalf[:], -0.5),
                     nc.gpsimd.iota(iota[:], [[1, E]], base=0, channel_multiplier=0, allow_small_or_imprecise_dtypes=True)]
            for t in (kp, wp):
                steps.append(nc.gpsimd.memset(t[:, :, 0:1], NEG))
            for t in (a2, e2, ev):
                steps.append(nc.gpsimd.memset(t[:, :, 0:1], 0.0))
            for s in steps:
                s.then_inc(const_set, 1)
            pool.wait_ge(w_in, 16 * 6)
            pool.wait_ge(const_set, 7)
            nc.gpsimd.memset(wp[:, :, 1:SEG], 0.0).then_inc(const_set, 1)
            pool.wait_ge(const_set, 8)
            for c in range(DC):
                v = wp[:, c * HALF:(c + 1) * HALF, 1:SEG]
                nc.gpsimd.tensor_scalar(v, v, wuc[:, c:c + 1], None, ALU.add).then_inc(const_set, 1)

            def rs1(nb):
                pool.wait_ge(var, 2 * nb + 1)
                nc.gpsimd.tensor_tensor(out=rs[:], in0=ve[:], in1=neghalf[:], op=ALU.pow).then_inc(rstd, 1)

            def sums(nb):
                pool.wait_ge(exps, 4 * nb + 4)
                pool.wait_ge(vev, nb + 1)
                pool.wait_ge(pscan, nb)
                nc.gpsimd.tensor_tensor(out=ev[:, :, 1:SEG], in0=e2[:, :, 1:SEG], in1=vt[:], op=ALU.mult).then_inc(ev_mul, 1)
                pool.wait_ge(ev_mul, 2 * nb + 1)
                nc.gpsimd.tensor_tensor(out=vt[:], in0=ee[:], in1=vt[:], op=ALU.mult).then_inc(ev_mul, 1)
                pool.wait_ge(qscan, nb + 1)
                nc.gpsimd.tensor_tensor(out=d1[:], in0=ae[:], in1=qp[:, :, 0:SEQ], op=ALU.mult).then_inc(den, 1)
                pool.wait_ge(den, 2 * nb + 1)
                nc.gpsimd.tensor_tensor(out=d1[:], in0=d1[:], in1=ee[:], op=ALU.add).then_inc(den, 1)
                pool.wait_ge(pscan, nb + 1)
                nc.gpsimd.tensor_tensor(out=ae[:], in0=ae[:], in1=pp[:, :, 0:SEQ], op=ALU.mult).then_inc(num, 1)
                pool.wait_ge(num, 2 * nb + 1)
                nc.gpsimd.tensor_tensor(out=ae[:], in0=ae[:], in1=vt[:], op=ALU.add).then_inc(num, 1)

            def quotient(nb):
                pool.wait_ge(rec, nb + 1)
                pool.wait_ge(num, 2 * nb + 2)
                nc.gpsimd.tensor_tensor(out=d2[:], in0=ae[:], in1=d1[:], op=ALU.mult).then_inc(yv, 1)

            def rs2(nb):
                pool.wait_ge(var, 2 * nb + 2)
                nc.gpsimd.tensor_tensor(out=rs[:], in0=ve[:], in1=neghalf[:], op=ALU.pow).then_inc(rstd, 1)

            def copy_h(nb):
                pool.wait_ge(hev, nb + 1)
                nc.gpsimd.tensor_copy(hT[:, :, bass.ds(nb * BLK, BLK)], hb[:]).then_inc(hcp, 1)

            def step(b, e, nb, piece):
                piece()

            run_blocks(pool, {0: rs1, 3: sums, 4: quotient, 5: rs2, 6: copy_h}, step)

        @block.tensor
        def _(pe):
            def to_channels(src, done):
                for j in range(BT):
                    for c in range(DC):
                        last = nc.tensor.transpose(T[:, c, j * P:(j + 1) * P], src[:, j, c * P:(c + 1) * P], ident)
                last.then_inc(done, 1)

            def ctx_T(nb):
                pe.wait_ge(ctx_loaded, 16 * nb + 16)
                pe.wait_ge(biasadd, 2 * nb)
                to_channels(ctx_t, cT)

            def k_T(nb):
                pe.wait_ge(norm, 8 * nb + 4)
                pe.wait_ge(vev, nb + 1)
                to_channels(xn, kT)

            def y_T(nb):
                pe.wait_ge(yv, nb + 1)
                pe.wait_ge(kev, 2 * nb + 2)
                yf = d2[:].rearrange("p (c s) t -> p c (s t)", c=DC)
                for j in range(BT):
                    for c in range(DC):
                        last = nc.tensor.transpose(Tt[:, j, c * P:(c + 1) * P], yf[:, c, j * P:(j + 1) * P], ident)
                last.then_inc(yT, 1)

            def h_T(nb):
                pe.wait_ge(norm, 8 * nb + 8)
                to_channels(xn, hTr)

            def router(nb):
                pe.wait_ge(hev, nb + 1)
                for j in range(BT):
                    for c in range(DC):
                        last = nc.tensor.matmul(T[:, 0, j * E:(j + 1) * E], hb[:, c, j * P:(j + 1) * P], rw[:, c, :],
                                                start=c == 0, stop=c == DC - 1)
                last.then_inc(rout, 1)
                pe.wait_ge(score, nb + 1)
                for j in range(BT):
                    last = nc.tensor.transpose(T[0:E, 1, j * P:(j + 1) * P], oh[:, 0, j, :], ident)
                last.then_inc(sTr, 1)
                pe.wait_ge(sTe, nb + 1)
                for j in range(BT):
                    last = nc.tensor.matmul(Tt[:, j, :], sT[:, j * P:(j + 1) * P], bd[:], start=True, stop=True)
                last.then_inc(bias, 1)

            def gate_up(m, e, b):
                for acc, w, read in ((G, wg, s_gp), (U, wu, s_ue)):
                    pe.wait_ge(read, 2 * m)
                    for i in range(DC):
                        for c in range(DC):
                            last = nc.tensor.matmul(acc[:, i, :], w[:, e, c, i * P:(i + 1) * P], hT[:, c, bass.ds(b * BLK, BLK)],
                                                    start=c == 0, stop=c == DC - 1)
                        last.then_inc(s_gu, 1)

            def down(n, e):
                pe.wait_ge(s_act, 2 * n + 2)
                pe.wait_ge(s_acc, 4 * n)
                for j in range(BT):
                    for i in range(DC):
                        last = nc.tensor.matmul(O[:, j, :], th[e % 2][:, i, j * P:(j + 1) * P], wd[:, e, i, :],
                                                start=i == 0, stop=i == DC - 1)
                    if j % 2:
                        last.then_inc(s_d, 1)

            def step(b, e, nb, piece):
                n = b * E + e
                if e < E - 1:
                    if e < 0:
                        pe.wait_ge(experts_in, 16 * 3)
                        pe.wait_ge(hcp, 1)
                    gate_up(n + 1, e + 1, b)
                elif nb is not None:
                    pe.wait_ge(hcp, nb + 1)
                    gate_up(n + 1, 0, nb)
                piece()
                if e >= 0:
                    down(n, e)

            pe.wait_ge(w_in, 16 * 6)
            pe.wait_ge(const_set, 10)

            run_blocks(pe, {0: ctx_T, 1: k_T, 5: y_T, 6: h_T, 7: router}, step)

        @block.scalar
        def _(act):
            def v_out(nb):
                act.wait_ge(cT, nb + 1)
                act.wait_ge(num, 2 * nb)
                nc.scalar.activation(vt[:], T[:].rearrange("p c (s t) -> p (c s) t", t=SEQ), ACT.Copy).then_inc(vev, 1)

            def k_out(nb):
                act.wait_ge(kT, nb + 1)
                for c in range(DC):
                    nc.scalar.activation(kp[:, c * HALF:(c + 1) * HALF, 1:SEG], T[:, c, :].rearrange("p (s t) -> p s t", t=SEQ),
                                         ACT.Copy).then_inc(kev, 1)

            def exponentials(nb):
                act.wait_ge(clip, 4 * nb + 4)
                nc.scalar.activation(a2[:, :, 1:SEG], a2[:, :, 1:SEG], ACT.Exp).then_inc(exps, 1)
                nc.scalar.activation(e2[:, :, 1:SEG], e2[:, :, 1:SEG], ACT.Exp, scale=-1.0).then_inc(exps, 1)
                nc.scalar.activation(ae[:], ae[:], ACT.Exp, scale=-1.0).then_inc(exps, 1)
                nc.scalar.activation(ee[:], ee[:], ACT.Exp).then_inc(exps, 1)

            def h_out(nb):
                act.wait_ge(hTr, nb + 1)
                act.wait_ge(rout, nb)
                act.wait_ge(hcp, nb)
                nc.scalar.activation(hb[:], T[:], ACT.Copy).then_inc(hev, 1)

            def weights(nb):
                act.wait_ge(top, 8 * nb + 8)
                act.wait_ge(texp, 2 * nb + 1)
                nc.scalar.activation(te[:, 1, :], te[:, 0, :], ACT.Exp).then_inc(texp, 1)
                act.wait_ge(sTr, nb + 1)
                nc.scalar.activation(sT[:], T[0:E, 1, :], ACT.Copy).then_inc(sTe, 1)

            def step(b, e, nb, piece):
                n = b * E + e
                if e < E - 1 or nb is not None:
                    m, p, x = n + 1, (e + 1) % 2, (e + 1) % E
                    for i in range(DC):
                        act.wait_ge(s_gp, 2 * m + 1 + i)
                        if e >= 0:
                            act.wait_ge(s_d, 2 * n)
                        nc.scalar.activation(th[p][:, i, :], gp[p][:, i, :], ACT.Tanh, scale=ALPHA / 2).then_inc(s_th, 1)
                    for i in range(DC):
                        act.wait_ge(s_gu, 4 * m + 3 + i)
                        if e >= 0:
                            act.wait_ge(s_act, 2 * n)
                        nc.scalar.activation(ur[p][:, i, :], U[:, i, :], ACT.Identity, bias=bu[:, x, i:i + 1]).then_inc(s_ue, 1)
                piece()

            act.wait_ge(w_in, 16 * 6)
            run_blocks(act, {0: v_out, 1: k_out, 2: exponentials, 6: h_out, 7: weights}, step)

        @block.vector
        def _(dve):
            def statistics(nb, k):
                nc.vector.memset(mark[:], 0.0)
                for j in range(BT):
                    nc.vector.bn_stats(st[:, j, :], x_sb[:, bass.ds(nb * BT + j, 1), :]).then_inc(stat, 1)
                dve.wait_ge(stat, 16 * nb + 8 * k + 4)
                nc.vector.memset(mark[:], 0.0)
                for j in range(BT):
                    nc.vector.bn_aggr(mv[:, j, :], st[:, j, :]).then_inc(stat, 1)
                dve.wait_ge(stat, 16 * nb + 8 * k + 8)
                nc.vector.tensor_scalar(ve[:], mv[:, :, 1], LN_EPS, None, ALU.add).then_inc(var, 1)

            def normalise(nb, k):
                dve.wait_ge(rstd, 2 * nb + k + 1)
                for j in range(BT):
                    nc.vector.tensor_scalar(xn[:, j, :], x_sb[:, bass.ds(nb * BT + j, 1), :], mv[:, j, 0:1], rs[:, j:j + 1],
                                            ALU.subtract, ALU.mult).then_inc(norm, 1)

            def ln1(nb):
                statistics(nb, 0)

            def ln1_out(nb):
                dve.wait_ge(hTr, nb)
                normalise(nb, 0)

            def running_max(nb):
                dve.wait_ge(kev, 2 * nb + 2)
                flat = lambda t: t[:].rearrange("p s t -> p (s t)")
                nc.vector.tensor_tensor_scan(out=flat(op), data0=flat(wp), data1=flat(kp), initial=NEG, op0=ALU.add,
                                             op1=ALU.max).then_inc(scan_o, 1)
                dve.wait_ge(scan_o, nb + 1)
                dve.wait_ge(yT, nb)
                for c in range(DC):
                    s = slice(c * HALF, (c + 1) * HALF)
                    nc.vector.scalar_tensor_tensor(out=d1[:, s, :], in0=kp[:, s, 1:SEG], scalar=wuc[:, DC + c:DC + c + 1],
                                                   in1=op[:, s, 0:SEQ], op0=ALU.add, op1=ALU.subtract).then_inc(dif, 1)
                    nc.vector.scalar_tensor_tensor(out=d2[:, s, :], in0=op[:, s, 0:SEQ], scalar=wuc[:, c:c + 1],
                                                   in1=kp[:, s, 1:SEG], op0=ALU.add, op1=ALU.subtract).then_inc(dif, 1)

            def clips(nb):
                dve.wait_ge(dif, 4 * nb + 4)
                dve.wait_ge(pscan, nb)
                nc.vector.tensor_scalar(a2[:, :, 1:SEG], d2[:], 0.0, None, ALU.min).then_inc(clip, 1)
                nc.vector.tensor_scalar(e2[:, :, 1:SEG], d2[:], 0.0, None, ALU.max).then_inc(clip, 1)
                nc.vector.tensor_scalar(ae[:], d1[:], 0.0, None, ALU.max).then_inc(clip, 1)
                nc.vector.tensor_scalar(ee[:], d1[:], 0.0, None, ALU.min).then_inc(clip, 1)

            def scans(nb):
                flat = lambda t: t[:].rearrange("p s t -> p (s t)")
                dve.wait_ge(exps, 4 * nb + 4)
                nc.vector.tensor_tensor_scan(out=flat(qp), data0=flat(a2), data1=flat(e2), initial=0.0, op0=ALU.mult,
                                             op1=ALU.add).then_inc(qscan, 1)
                dve.wait_ge(ev_mul, 2 * nb + 1)
                nc.vector.tensor_tensor_scan(out=flat(pp), data0=flat(a2), data1=flat(ev), initial=0.0, op0=ALU.mult,
                                             op1=ALU.add).then_inc(pscan, 1)

            def reciprocals(nb):
                dve.wait_ge(den, 2 * nb + 2)
                nc.vector.reciprocal(d1[:], d1[:]).then_inc(rec, 1)

            def residual(nb):
                dve.wait_ge(yT, nb + 1)
                for i in range(2):
                    xs = x_sb[:, bass.ds(nb * BT + 2 * i, 2), :]
                    nc.vector.tensor_tensor(out=xs, in0=Tt[:, 2 * i:2 * i + 2, :], in1=xs, op=ALU.add).then_inc(yadd, 1)
                dve.wait_ge(yadd, 2 * nb + 2)
                dve.wait_ge(kT, nb + 1)
                statistics(nb, 1)

            def ln2_out(nb):
                normalise(nb, 1)

            def choose(nb):
                dve.wait_ge(rout, nb + 1)
                nc.vector.tensor_tensor(out=lg[:], in0=T[:, 0, 0:BT * E].rearrange("p (j e) -> p j e", e=E),
                                        in1=rb[:].unsqueeze(1).to_broadcast([P, BT, E]), op=ALU.add).then_inc(lgs, 1)
                dve.wait_ge(lgs, nb + 1)
                nc.vector.memset(mark[:], 0.0)
                for j in range(BT):
                    nc.vector.max(mx8[:, j, :], lg[:, j, :]).then_inc(top, 1)
                dve.wait_ge(top, 8 * nb + 4)
                nc.vector.memset(mark[:], 0.0)
                for j in range(BT):
                    nc.vector.max_index(ix8[:, j, :], mx8[:, j, :], lg[:, j, :]).then_inc(top, 1)
                dve.wait_ge(top, 8 * nb + 8)
                nc.vector.tensor_tensor(out=te[:, 0, :], in0=mx8[:, :, 1], in1=mx8[:, :, 0], op=ALU.subtract).then_inc(texp, 1)
                nc.vector.tensor_copy(ixf[:], ix8[:, :, 0:2]).then_inc(wts_, 1)
                dve.wait_ge(texp, 2 * nb + 2)
                nc.vector.tensor_scalar(te[:, 2, :], te[:, 1, :], 1.0, 2.0, ALU.add, ALU.mult).then_inc(wts_, 1)
                dve.wait_ge(wts_, 5 * nb + 2)
                nc.vector.reciprocal(wt[:, 0, :], te[:, 2, :]).then_inc(wts_, 1)
                dve.wait_ge(wts_, 5 * nb + 3)
                nc.vector.tensor_tensor(out=wt[:, 1, :], in0=wt[:, 0, :], in1=te[:, 1, :], op=ALU.mult).then_inc(wts_, 1)
                dve.wait_ge(wts_, 5 * nb + 4)
                dve.wait_ge(sTr, nb)
                for k in range(2):
                    for j in range(BT):
                        last = nc.vector.tensor_scalar(oh[:, k, j, :], iota[:], ixf[:, j, k:k + 1], wt[:, k, j:j + 1], ALU.is_equal, ALU.mult)
                        last.then_inc(lgs_oh, 1)
                dve.wait_ge(lgs_oh, 8 * nb + 8)
                nc.vector.tensor_tensor(out=sc[:, tiles(nb), :], in0=oh[:, 0, :, :], in1=oh[:, 1, :, :], op=ALU.add).then_inc(wts_, 1)
                nc.vector.tensor_tensor(out=oh[:, 0, :, :], in0=oh[:, 0, :, :], in1=oh[:, 1, :, :], op=ALU.add).then_inc(score, 1)
                dve.wait_ge(bias, nb + 1)
                dve.wait_ge(norm, 8 * nb + 8)
                for i in range(2):
                    xs = x_sb[:, bass.ds(nb * BT + 2 * i, 2), :]
                    nc.vector.scalar_tensor_tensor(out=xs, in0=Tt[:, 2 * i:2 * i + 2, :], scalar=2.0, in1=xs, op0=ALU.mult,
                                                   op1=ALU.add).then_inc(biasadd, 1)

            def step(b, e, nb, piece):
                n = b * E + e
                if e < E - 1 or nb is not None:
                    m, p, x = n + 1, (e + 1) % 2, (e + 1) % E
                    for i in range(DC):
                        dve.wait_ge(s_gu, 4 * m + 1 + i)
                        if e >= 0:
                            dve.wait_ge(s_gl, 2 * n)
                        nc.vector.tensor_scalar(gp[p][:, i, :], G[:, i, :], bg[:, x, i:i + 1], LIMIT, ALU.add, ALU.min).then_inc(s_gp, 1)
                    for i in range(DC):
                        dve.wait_ge(s_th, 2 * m + 1 + i)
                        nc.vector.scalar_tensor_tensor(out=th[p][:, i, :], in0=th[p][:, i, :], scalar=1.0, in1=gp[p][:, i, :],
                                                       op0=ALU.add, op1=ALU.mult).then_inc(s_gl, 1)
                    for i in range(DC):
                        dve.wait_ge(s_ue, 2 * m + 1 + i)
                        nc.vector.tensor_scalar(ur[p][:, i, :], ur[p][:, i, :], -LIMIT, LIMIT, ALU.max, ALU.min).then_inc(s_uc, 1)
                    for i in range(DC):
                        dve.wait_ge(s_uc, 2 * m + 1 + i)
                        nc.vector.scalar_tensor_tensor(out=th[p][:, i, :], in0=ur[p][:, i, :], scalar=1.0, in1=th[p][:, i, :],
                                                       op0=ALU.add, op1=ALU.mult).then_inc(s_act, 1)
                piece()
                if e >= 0:
                    if e == 0:
                        dve.wait_ge(biasadd, 2 * b + 2)
                    dve.wait_ge(s_acc, 4 * n)
                    for j in range(BT):
                        dve.wait_ge(s_d, 2 * n + 1 + j // 2)
                        t = bass.ds(b * BT + j, 1)
                        nc.vector.scalar_tensor_tensor(out=x_sb[:, t, :], in0=O[:, j, :], scalar=sc[:, t, e:e + 1],
                                                       in1=x_sb[:, t, :], op0=ALU.mult, op1=ALU.add).then_inc(s_acc, 1)

            dve.wait_ge(w_in, 16 * 6)
            dve.wait_ge(const_set, 10)
            run_blocks(dve, {0: lambda nb: (ln1(nb), ln1_out(nb)), 1: running_max, 2: clips, 3: scans, 4: reciprocals,
                             5: residual, 6: ln2_out, 7: choose}, step)
            dve.wait_ge(s_acc, 4 * BLOCKS * E)


def layer_one(nc, new_sem, x_sb, ident, a):
    H, HD = 16, 16
    G8 = P // HD
    SC = float(HD) ** -0.5
    F_ = 1024
    FT = F_ // P
    R = 16
    RMS_EPS = 1e-6
    MOD_SCALE = 0.1
    AV = HD + 1
    AX = mybir.AxisListType.X
    FIRST = dict(Dn=-1, D=0, Dt=1, En=1, E=2, Et=3, F=4, Ft=5, M=6)
    with ExitStack() as ctx:
        def sb(name, shape, dt=F32):
            return ctx.enter_context(nc.sbuf_tensor("l_" + name, shape, dt))

        def psum(name, shape, dt=F32):
            return ctx.enter_context(nc.psum_tensor("l_" + name, shape, dt))

        counters = {}

        def S(name):
            if name not in counters:
                counters[name] = new_sem("l_" + name)
            return counters[name]

        dwqk, dwv, dwo = sb("dwqk", [P, DC, 8 * P]), sb("dwv", [P, DC, 64]), sb("dwo", [P, DC, D])
        rope, sink = sb("rope", [P, 2, P]), sb("sink", [P, H])
        ewq, ewkv, ewo = sb("ewq", [P, DC, D]), sb("ewkv", [P, DC, 2 * D]), sb("ewo", [P, DC, D])
        ebq, ebkv, ebo = sb("ebq", [P, D]), sb("ebkv", [P, 2 * D]), sb("ebo", [P, D])
        fwqk, fwv, fwo = sb("fwqk", [P, DC, 4 * P]), sb("fwv", [P, DC, D]), sb("fwo", [P, DC, D])
        fa, fb, lnw = sb("fa", [P, DC, R]), sb("fb", [R, F_]), sb("lnw", [P, 2 * DC])
        win, wup, wdn = sb("win", [P, DC, F_]), sb("wup", [P, DC, F_]), sb("wdn", [P, FT, D])
        headmask = sb("headmask", [P, G8])
        cmask = sb("cmask", [P, G8, SEQ], BF16)
        identb = sb("identb", [P, P], BF16)
        neghalf = sb("neghalf", [P, 2])
        xn = {k: sb("xn" + k, [P, D]) for k in "DEF"}
        xT = {k: sb("xT" + k, [P, DC, 2, 2, SEQ]) for k in "DF"}
        xTE = sb("xTE", [P, DC, P])
        st, mv = {k: sb("st" + k, [P, 6]) for k in "DEF"}, {k: sb("mv" + k, [P, 2]) for k in "DEF"}
        ve, rs = {k: sb("ve" + k, [P, 2]) for k in "DEF"}, {k: sb("rs" + k, [P, 2]) for k in "DEF"}
        qk = {"D": sb("qkD", [P, 4, P]), "F": sb("qkF", [P, DC, P])}
        vbd = {k: sb("vbd" + k, [P, 2, H // 2, 2, AV]) for k in "DF"}
        hm = {k: sb("hm" + k, [P, 3, H]) for k in "DF"}
        rec = {k: sb("rec" + k, [P, H]) for k in "DF"}
        o, oT = {k: sb("o" + k, [P, D]) for k in "DF"}, {k: sb("oT" + k, [P, DC, P]) for k in "DF"}
        rt = sb("rt", [P, 4, P])
        mark = sb("mark", [P, 1])
        kx = {k: sb("kx" + k, [P, 2, 2, G8, SEQ]) for k in "DF"}
        ex = {k: sb("ex" + k, [P, H, SEQ]) for k in "DF"}
        eT = sb("eT", [P, H // 2, P])
        ctx_t, cT = sb("ctx_t", [P, D]), sb("cT", [P, DC, P])
        kv, q = sb("kv", [P, 2, D]), sb("q", [P, D])
        vE = sb("vE", [P, D])
        prod = sb("prod", [P, H, H, HD])
        sco, se = sb("sco", [P, H, H]), sb("se", [P, 3, H])
        att, attT = sb("att", [P, D]), sb("attT", [P, DC, P])
        y = att
        atT, modT, gmT = sb("atT", [P, DC, P]), sb("modT", [R, P]), sb("gmT", [R, P])
        x2T = sb("x2T", [P, DC, TOK])
        hid = sb("hid", [P, FT, P])

        SS, PJ = psum("SS", [P, 2, BLK]), psum("PJ", [P, 2, BLK])
        GA, UA, MI, EB = (psum(n, [P, BLK]) for n in ("GA", "UA", "MI", "EB"))
        block = ctx.enter_context(nc.Block())

        def tile(t):
            return bass.ds(t, 1)

        def started(n):
            return not isinstance(n, int) or n > 0

        def wait_if(eng, sem, n):
            if started(n):
                eng.wait_ge(sem, n)

        def cap(n):
            return min(n, TILES) if isinstance(n, int) else n

        def iterate(eng, pieces):
            def one(i, check):
                for stage, piece in pieces:
                    t = i - FIRST[stage]
                    if not check or 0 <= t < TILES:
                        piece(t)
            start = max(FIRST.values()) + 1
            stop = TILES + min(FIRST.values())
            for i in range(min(FIRST.values()), start):
                one(i, True)
            with eng.Fori(start, stop) as i:
                one(i, False)
            for i in range(stop, TILES + max(FIRST.values())):
                one(i, True)

        KX = DC * G8
        USES = {
            "EB": [("d_xT", "D", [("D_xT", 1, 1)]), ("e_xT", "E", [("E_xT", 1, 1)]), ("d_av", "Dt", [("D_o", 1, 1)]),
                   ("e_cT", "E", [("E_cT", 1, 1)]), ("e_q", "E", [("E_q", 1, 1)]), ("e_kv", "E", [("E_kv", 1, 1)]),
                   ("d_oT", "Dt", [("D_oT", 1, 1)]), ("d_wo", "Dt", [("D_x", 1, 1)]), ("d_v", "D", [("D_vb", 2, 2)]),
                   ("et_aT", "Et", [("E_aT", 1, 1)]), ("et_wo", "Et", [("E_x", 2, 1)])],
            "SS": [("d_eT", "Dt", [("D_eT", 1, 1)]), ("ft_eT", "Ft", [("F_eT", 1, 1)]), ("d_s", "D", [("D_arg", 1, 1)]),
                   ("f_s", "F", [("F_arg", 1, 1)])],
            "PJ": [("d_qk", "D", [("D_rt", 2, 2)]), ("f_qkv", "F", [("F_qk", 1, 1), ("F_kx", KX, KX), ("F_vb", 2, 2)])],
            "MI": [("f_zT", "F", [("F_x2", 2, 2)]), ("ft_av", "Ft", [("F_o", 1, 1)]), ("ft_oT", "Ft", [("F_oT", 1, 1)]),
                   ("ft_at", "Ft", [("F_at", 1, 1)]), ("ft_a", "Ft", [("F_gm", 1, 1)])],
            "GA": [("m_0", "M", [("M_silu", 2, 1)]), ("m_1", "M", [("M_silu", 2, 2)]), ("m_down", "M", [("M_x", 1, 1)])],
            "UA": [("m_0", "M", [("M_hid", 2, 1)]), ("m_1", "M", [("M_hid", 2, 2)])],
        }
        WEIGHTS, D_WEIGHTS = 15, 6
        CONSTS = 9

        @block.sync
        def _(sp):
            for tensor, name in ((dwqk, "dwqk"), (rope, "rope"), (sink, "sink"), (headmask, "headmask"), (dwv, "dwv"), (dwo, "dwo")):
                sp.dma_start(tensor[:], a[name]).then_inc(S("d_in"), 16)
            for tensor, name in ((ewq, "ewq"),
                                 (ewkv, "ewkv"), (ewo, "ewo"), (ebq, "ebq"), (ebkv, "ebkv"), (ebo, "ebo"), (fwqk, "fwqk"),
                                 (fwv, "fwv"), (fwo, "fwo"), (fa, "fa"), (fb, "fb"), (lnw, "lnw"),
                                 (win, "win"), (wup, "wup"), (wdn, "wdn")):
                sp.dma_start(tensor[:], a[name]).then_inc(S("w_in"), 16)

            def load_ctx(t):
                wait_if(sp, S("E_cTp"), t)
                sp.dma_start(ctx_t[:], a["ctx_in"][bass.ds(t * P, P), :]).then_inc(S("ctx_in"), 16)

            def store(t):
                sp.wait_ge(S("M_x"), t + 1)
                sp.dma_start(a["out"][bass.ds(t * P, P), :], x_sb[:, tile(t), :]).then_inc(S("stored"), 16)

            iterate(sp, [("E", load_ctx), ("M", store)])
            sp.wait_ge(S("stored"), 16 * TILES)

        @block.gpsimd
        def _(pool):
            nc.gpsimd.memset(neghalf[:], -0.5).then_inc(S("const"), 1)
            nc.gpsimd.tensor_copy(identb[:], ident).then_inc(S("const"), 1)
            nc.gpsimd.memset(cmask[:], 0.0).then_inc(S("const"), 1)
            for k in "DF":
                nc.gpsimd.memset(vbd[k][:], 0.0).then_inc(S("const"), 1)
            pool.wait_ge(S("const"), 5)
            for s in range(2):
                v = cmask[s * SEQ:(s + 1) * SEQ, :, :]
                nc.gpsimd.affine_select(out=v, in_=v, compare_op=ALU.is_ge, fill=-1e30, base=0, pattern=[[0, G8], [-1, SEQ]],
                                        channel_multiplier=1).then_inc(S("const"), 1)
            for k in "DF":
                for h in range(2):
                    ones = vbd[k][h * SEQ:(h + 1) * SEQ, :, :, h, HD:AV]
                    nc.gpsimd.memset(ones, 1.0).then_inc(S("const"), 1)
            def power(k, n):
                def piece(t):
                    pool.wait_ge(S(k + "_ve"), n * t + n)
                    nc.gpsimd.tensor_tensor(out=rs[k][:, 0:n], in0=ve[k][:, 0:n], in1=neghalf[:, 0:n], op=ALU.pow).then_inc(S(k + "_rs"), 1)
                return piece

            def products_qk(t):
                pool.wait_ge(S("E_q"), t + 1)
                pool.wait_ge(S("E_kv"), t + 1)
                wait_if(pool, S("E_att"), 4 * t)
                qv = q[:].rearrange("p (h d) -> p h d", d=HD)
                kk = kv[:, 0, :].rearrange("p (g d) -> p g d", d=HD)
                for h in range(H):
                    nc.gpsimd.tensor_tensor(out=prod[:, h], in0=qv[:, h:h + 1, :].to_broadcast([P, H, HD]), in1=kk,
                                            op=ALU.mult).then_inc(S("E_pqk"), 1)

            def products_av(t):
                pool.wait_ge(S("E_w"), t + 1)
                pool.wait_ge(S("E_keep"), t + 1)
                vv = vE[:].rearrange("p (g d) -> p d g", d=HD)
                for h in range(H):
                    nc.gpsimd.tensor_tensor(out=prod[:, h], in0=sco[:, h:h + 1, :].to_broadcast([P, HD, H]), in1=vv,
                                            op=ALU.mult).then_inc(S("E_pav"), 1)

            iterate(pool, [("Dn", power("D", 1)), ("F", power("F", 2)), ("Et", products_av), ("En", power("E", 1)),
                           ("E", products_qk)])

        @block.tensor
        def _(pe):
            def free(bank, use, t):
                uses = USES[bank]
                k = [u[0] for u in uses].index(use)
                i = t + FIRST[uses[k][1]]
                for back in range(1, 2 * len(uses) + 1):
                    laps, at = divmod(k - back, len(uses))
                    _, stage, left = uses[at]
                    before = i + laps - FIRST[stage]
                    if not isinstance(before, int) or 0 <= before < TILES:
                        for sem, per, n in left:
                            pe.wait_ge(S(sem), per * before + n)
                        return

            def product(out, lhsT, rhs):
                for c in range(DC):
                    last = nc.tensor.matmul(out, lhsT(c), rhs(c), start=c == 0, stop=c == DC - 1)
                return last

            def turn(bank, src):
                for c in range(DC):
                    last = nc.tensor.transpose(bank[:, c * P:(c + 1) * P], src[:, c * P:(c + 1) * P], ident)
                return last

            def twice(k, c, s):
                return xT[k][:, c, s].rearrange("p r n -> p (r n)")

            def projections(k, w, count):
                for m in range(count):
                    last = product(PJ[:, m // 4, (m % 4) * P:(m % 4 + 1) * P], lambda c: w[:, c, m * P:(m + 1) * P],
                                   lambda c: xT[k][:, c, :, 0, :])
                return last

            def scores(k):
                for c in range(2):
                    for s in range(2):
                        last = nc.tensor.matmul(SS[s * SEQ:(s + 1) * SEQ, c, :], qk[k][:, c, s * SEQ:(s + 1) * SEQ], kx[k][:, c, s],
                                                start=True, stop=k == "D", skip_group_check=True)
                    if k == "F":
                        last = nc.tensor.matmul(SS[:, c, :], identb[:], cmask[:], start=False, stop=True, skip_group_check=True)
                return last

            def weights_T(k):
                for j in range(H // 2):
                    last = nc.tensor.transpose(SS[:, j // 4, (j % 4) * P:(j % 4 + 1) * P], ex[k][:, 2 * j:2 * j + 2, :], ident)
                return last

            def weighted_values(k, bank):
                for j in range(H // 2):
                    for s in range(2):
                        last = nc.tensor.matmul(bank[s * SEQ:(s + 1) * SEQ, j * 2 * AV:(j + 1) * 2 * AV], eT[:, j, s * SEQ:(s + 1) * SEQ],
                                                vbd[k][:, s, j], start=True, stop=True)
                return last

            def d_xT(t):
                pe.wait_ge(S("D_xn"), t + 1)
                free("EB", "d_xT", t)
                turn(EB, xn["D"]).then_inc(S("D_xTp"), 1)

            def d_qk(t):
                pe.wait_ge(S("D_xT"), t + 1)
                free("PJ", "d_qk", t)
                projections("D", dwqk, 8).then_inc(S("D_pj"), 1)

            def d_v(t):
                free("EB", "d_v", t)
                for s in range(2):
                    last = product(EB[:, s * 64:(s + 1) * 64], lambda c: twice("D", c, s), lambda c: dwv[:, c, :])
                last.then_inc(S("D_pv"), 1)

            def d_s(t):
                pe.wait_ge(S("D_kx"), KX * (t + 1))
                free("SS", "d_s", t)
                scores("D").then_inc(S("D_s"), 1)

            def d_eT(t):
                pe.wait_ge(S("D_exp"), t + 1)
                free("SS", "d_eT", t)
                weights_T("D").then_inc(S("D_eTp"), 1)

            def d_av(t):
                pe.wait_ge(S("D_eT"), t + 1)
                pe.wait_ge(S("D_vb"), 2 * t + 2)
                free("EB", "d_av", t)
                weighted_values("D", EB).then_inc(S("D_av"), 1)

            def d_oT(t):
                pe.wait_ge(S("D_o"), t + 1)
                free("EB", "d_oT", t)
                turn(EB, o["D"]).then_inc(S("D_oTp"), 1)

            def d_wo(t):
                pe.wait_ge(S("D_oT"), t + 1)
                free("EB", "d_wo", t)
                product(EB[:, 0:D], lambda c: oT["D"][:, c, :], lambda c: dwo[:, c, :]).then_inc(S("D_wo"), 1)

            def e_cT(t):
                pe.wait_ge(S("ctx_in"), 16 * t + 16)
                free("EB", "e_cT", t)
                turn(EB, ctx_t).then_inc(S("E_cTp"), 1)

            def e_kv(t):
                pe.wait_ge(S("E_cT"), t + 1)
                free("EB", "e_kv", t)
                product(EB[:], lambda c: cT[:, c, :], lambda c: ewkv[:, c, :]).then_inc(S("E_kvp"), 1)

            def e_xT(t):
                if isinstance(t, int) and t == 0:
                    pe.wait_ge(S("w_in"), 16 * WEIGHTS)
                pe.wait_ge(S("E_xn"), t + 1)
                free("EB", "e_xT", t)
                turn(EB, xn["E"]).then_inc(S("E_xTp"), 1)

            def e_q(t):
                pe.wait_ge(S("E_xT"), t + 1)
                free("EB", "e_q", t)
                product(EB[:, 0:D], lambda c: xTE[:, c, :], lambda c: ewq[:, c, :]).then_inc(S("E_qp"), 1)

            def et_aT(t):
                pe.wait_ge(S("E_att"), 4 * t + 4)
                free("EB", "et_aT", t)
                turn(EB, att).then_inc(S("E_aTp"), 1)

            def et_wo(t):
                pe.wait_ge(S("E_aT"), t + 1)
                free("EB", "et_wo", t)
                product(EB[:, 0:D], lambda c: attT[:, c, :], lambda c: ewo[:, c, :]).then_inc(S("E_wo"), 1)

            def f_zT(t):
                pe.wait_ge(S("F_xn"), 3 * t + 3)
                free("MI", "f_zT", t)
                turn(MI, xn["F"]).then_inc(S("F_zTp"), 1)

            def f_qkv(t):
                pe.wait_ge(S("F_x1"), 2 * t + 2)
                free("PJ", "f_qkv", t)
                projections("F", fwqk, 4)
                for s in range(2):
                    last = product(PJ[:, 1, s * D:(s + 1) * D], lambda c: twice("F", c, s), lambda c: fwv[:, c, :])
                last.then_inc(S("F_pj"), 1)

            def f_s(t):
                pe.wait_ge(S("F_kx"), KX * (t + 1))
                free("SS", "f_s", t)
                scores("F").then_inc(S("F_s"), 1)

            def ft_eT(t):
                pe.wait_ge(S("F_exp"), t + 1)
                free("SS", "ft_eT", t)
                weights_T("F").then_inc(S("F_eTp"), 1)

            def ft_av(t):
                pe.wait_ge(S("F_eT"), t + 1)
                pe.wait_ge(S("F_vb"), 2 * t + 2)
                free("MI", "ft_av", t)
                weighted_values("F", MI).then_inc(S("F_av"), 1)

            def ft_oT(t):
                pe.wait_ge(S("F_o"), t + 1)
                free("MI", "ft_oT", t)
                turn(MI, o["F"]).then_inc(S("F_oTp"), 1)

            def ft_at(t):
                pe.wait_ge(S("F_oT"), t + 1)
                free("MI", "ft_at", t)
                for m in range(DC):
                    last = product(MI[:, m * P:(m + 1) * P], lambda c: fwo[:, c, m * P:(m + 1) * P], lambda c: oT["F"][:, c, :])
                last.then_inc(S("F_atp"), 1)

            def ft_a(t):
                pe.wait_ge(S("F_at"), t + 1)
                pe.wait_ge(S("F_x2"), 2 * t + 2)
                free("MI", "ft_a", t)
                product(MI[0:R, 0:P], lambda c: fa[:, c, :], lambda c: atT[:, c, :])
                product(MI[0:R, P:2 * P], lambda c: fa[:, c, :], lambda c: x2T[:, c, bass.ds(t * P, P)]).then_inc(S("F_ap"), 1)

            def m_half(half):
                def piece(t):
                    pe.wait_ge(S("F_gm"), t + 1)
                    free("GA", f"m_{half}", t)
                    h = lambda c: x2T[:, c, bass.ds(t * P, P)]
                    for k in range(4):
                        units = slice((4 * half + k) * P, (4 * half + k + 1) * P)
                        bank = GA[:, k * P:(k + 1) * P]
                        for c in range(DC):
                            nc.tensor.matmul(bank, win[:, c, units], h(c), start=c == 0, stop=False)
                        last = nc.tensor.matmul(bank, fb[:, units], gmT[:], start=False, stop=True)
                    last.then_inc(S("M_g"), 1)
                    free("UA", f"m_{half}", t)
                    for k in range(4):
                        units = slice((4 * half + k) * P, (4 * half + k + 1) * P)
                        last = product(UA[:, k * P:(k + 1) * P], lambda c: wup[:, c, units], h)
                    last.then_inc(S("M_u"), 1)
                return piece

            def m_down(t):
                pe.wait_ge(S("M_hid"), 2 * t + 2)
                free("GA", "m_down", t)
                for k in range(FT):
                    last = nc.tensor.matmul(GA[:, 0:D], hid[:, k, :], wdn[:, k, :], start=k == 0, stop=k == FT - 1)
                last.then_inc(S("M_dn"), 1)

            pe.wait_ge(S("d_in"), 16 * D_WEIGHTS)
            pe.wait_ge(S("const"), 11)
            iterate(pe, [("M", m_half(0)), ("D", d_xT), ("Dt", d_eT), ("E", e_xT), ("Dt", d_av), ("D", d_qk), ("F", f_zT),
                         ("E", e_cT), ("Ft", ft_eT), ("E", e_q), ("Ft", ft_av), ("E", e_kv), ("F", f_qkv), ("Dt", d_oT),
                         ("M", m_half(1)), ("Dt", d_wo), ("Ft", ft_oT), ("D", d_v), ("Ft", ft_at), ("D", d_s),
                         ("Ft", ft_a), ("M", m_down), ("Et", et_aT), ("F", f_s), ("Et", et_wo)])

        @block.scalar
        def _(act):
            def leave(out, bank, filled, read, done):
                def piece(t):
                    wait_if(act, S(read), t)
                    act.wait_ge(S(filled), t + 1)
                    nc.scalar.activation(out[:], bank[:, 0:D].rearrange("p (c n) -> p c n", c=DC), ACT.Copy).then_inc(S(done), 1)
                return piece

            def d_xT(t):
                wait_if(act, S("D_pv"), t)
                act.wait_ge(S("D_xTp"), t + 1)
                nc.scalar.activation(xT["D"][:].rearrange("p c s r n -> p (c s) r n"),
                                     EB[:, 0:D].rearrange("p (s n) -> p s n", n=SEQ).unsqueeze(2).to_broadcast([P, 4, 2, SEQ]),
                                     ACT.Copy).then_inc(S("D_xT"), 1)

            def exponentials(k):
                def piece(t):
                    act.wait_ge(S(k + "_arg"), t + 1)
                    nc.scalar.activation(ex[k][:], ex[k][:], ACT.Exp).then_inc(S(k + "_exp"), 1)
                return piece

            def weights_T(k, other, ahead):
                def piece(t):
                    wait_if(act, S(k + "_av"), t)
                    wait_if(act, S(other + "_av"), cap(t + ahead))
                    act.wait_ge(S(k + "_eTp"), t + 1)
                    nc.scalar.activation(eT[:], SS[:].rearrange("p b (j n) -> p (b j) n", n=P), ACT.Copy).then_inc(S(k + "_eT"), 1)
                return piece

            def f_x1(t):
                if isinstance(t, int) and t == 0:
                    act.wait_ge(S("w_in"), 16 * WEIGHTS)
                wait_if(act, S("F_pj"), t)
                act.wait_ge(S("F_zTp"), t + 1)
                for c in range(DC):
                    nc.scalar.activation(xT["F"][:, c], MI[:, c * P:(c + 1) * P].rearrange("p (s n) -> p s n", n=SEQ).unsqueeze(2)
                                         .to_broadcast([P, 2, 2, SEQ]), ACT.Identity, scale=lnw[:, c:c + 1]).then_inc(S("F_x1"), 1)

            def f_x2(t):
                act.wait_ge(S("F_zTp"), t + 1)
                for c in range(DC):
                    nc.scalar.activation(x2T[:, c, bass.ds(t * P, P)], MI[:, c * P:(c + 1) * P], ACT.Identity,
                                         scale=lnw[:, DC + c:DC + c + 1]).then_inc(S("F_x2"), 1)

            def f_qk(t):
                wait_if(act, S("F_s"), t)
                act.wait_ge(S("F_pj"), t + 1)
                nc.scalar.activation(qk["F"][:, 0:DC, :], PJ[:, 0, 0:D].rearrange("p (m n) -> p m n", n=P), ACT.Copy).then_inc(S("F_qk"), 1)

            def spread_keys(k):
                def piece(t):
                    wait_if(act, S(k + "_s"), t)
                    act.wait_ge(S(k + "_qk"), t + 1)
                    for c in range(DC):
                        keys = qk["D"][:, 2 + c, :] if k == "D" else PJ[:, 0, (2 + c) * P:(3 + c) * P]
                        for h in range(G8):
                            nc.scalar.activation(kx[k][:, c, :, h, :], keys.rearrange("p (s n) -> p s n", n=SEQ), ACT.Identity,
                                                 scale=headmask[:, h:h + 1]).then_inc(S(k + "_kx"), 1)
                return piece

            def ft_mod(t):
                wait_if(act, S("F_gm"), t)
                act.wait_ge(S("F_ap"), t + 1)
                nc.scalar.activation(modT[:], MI[0:R, 0:P], ACT.Tanh).then_inc(S("F_mod"), 1)

            def m_tanh(half):
                def piece(t):
                    wait_if(act, S("M_dn"), t)
                    act.wait_ge(S("M_g"), 2 * t + half + 1)
                    nc.scalar.activation(hid[:, 4 * half:4 * half + 4, :], GA[:], ACT.Tanh, scale=0.5).then_inc(S("M_th"), 1)
                return piece

            def et_exp(t):
                act.wait_ge(S("E_sub"), t + 1)
                nc.scalar.activation(sco[:], sco[:], ACT.Exp).then_inc(S("E_exp"), 1)

            def et_keep(t):
                wait_if(act, S("E_pav"), 16 * t)
                act.wait_ge(S("E_kv"), t + 1)
                nc.scalar.activation(vE[:], kv[:, 1, :], ACT.Copy).then_inc(S("E_keep"), 1)

            act.wait_ge(S("d_in"), 16 * D_WEIGHTS)
            iterate(act, [("Ft", exponentials("F")), ("M", m_tanh(0)), ("D", d_xT), ("Dt", weights_T("D", "F", -4)),
                          ("E", leave(xTE, EB, "E_xTp", "E_qp", "E_xT")), ("Et", et_keep), ("F", f_x1), ("F", f_x2), ("Et", et_exp),
                          ("E", leave(cT, EB, "E_cTp", "E_kvp", "E_cT")), ("Ft", weights_T("F", "D", 5)), ("D", spread_keys("D")),
                          ("F", f_qk), ("F", spread_keys("F")), ("Dt", leave(oT["D"], EB, "D_oTp", "D_wo", "D_oT")), ("M", m_tanh(1)),
                          ("Ft", leave(oT["F"], MI, "F_oTp", "F_atp", "F_oT")), ("Ft", leave(atT, MI, "F_atp", "F_ap", "F_at")),
                          ("D", exponentials("D")), ("Ft", ft_mod), ("Et", leave(attT, EB, "E_aTp", "E_wo", "E_aT"))])

        @block.vector
        def _(dve):
            def row(t):
                return x_sb[:, tile(t), :].rearrange("p t d -> p (t d)")

            def statistics(k, before, per):
                def piece(t):
                    wait_if(dve, S(k + "_xn"), (3 if k == "F" else 1) * t)
                    if before:
                        dve.wait_ge(S(before), per * t + per)
                    nc.vector.memset(mark[:], 0.0)
                    nc.vector.bn_stats(st[k][:], row(t)).then_inc(S(k + "_st"), 1)
                    dve.wait_ge(S(k + "_st"), t + 1)
                    nc.vector.memset(mark[:], 0.0)
                    nc.vector.bn_aggr(mv[k][:], st[k][:]).then_inc(S(k + "_mv"), 1)
                    dve.wait_ge(S(k + "_mv"), t + 1)
                    nc.vector.tensor_scalar(ve[k][:, 0:1], mv[k][:, 1:2], LN_EPS, None, ALU.add).then_inc(S(k + "_ve"), 1)
                    if k == "F":
                        nc.vector.tensor_scalar(ve[k][:, 1:2], mv[k][:, 1:2], 1.0 + RMS_EPS, RMS_EPS * LN_EPS, ALU.mult,
                                                ALU.add).then_inc(S(k + "_ve"), 1)
                return piece

            def normalise(k):
                def piece(t):
                    wait_if(dve, S(k + "_xTp"), t)
                    dve.wait_ge(S(k + "_rs"), t + 1)
                    nc.vector.tensor_scalar(xn[k][:], row(t), mv[k][:, 0:1], rs[k][:, 0:1], ALU.subtract, ALU.mult).then_inc(S(k + "_xn"), 1)
                return piece

            def f_norm(t):
                wait_if(dve, S("F_zTp"), t)
                dve.wait_ge(S("F_rs"), t + 1)
                nc.vector.tensor_scalar(y[:], row(t), mv["F"][:, 0:1], rs["F"][:, 0:1], ALU.subtract, ALU.mult).then_inc(S("F_xn"), 1)
                nc.vector.tensor_scalar(xn["F"][:], row(t), mv["F"][:, 0:1], rs["F"][:, 1:2], ALU.subtract, ALU.mult).then_inc(S("F_xn"), 1)
                dve.wait_ge(S("F_xn"), 3 * t + 2)
                nc.vector.tensor_tensor(out=row(t), in0=row(t), in1=y[:], op=ALU.add).then_inc(S("F_xn"), 1)

            def d_rope(t):
                dve.wait_ge(S("D_pj"), t + 1)
                wait_if(dve, S("D_s"), t)
                wait_if(dve, S("D_kx"), KX * t)
                for i, to in enumerate((qk["D"], rt)):
                    nc.vector.tensor_tensor(out=to[:], in0=PJ[:, i, :].rearrange("p (m n) -> p m n", n=P),
                                            in1=rope[:, i, :].unsqueeze(1).to_broadcast([P, 4, P]), op=ALU.mult).then_inc(S("D_rt"), 1)
                dve.wait_ge(S("D_rt"), 2 * t + 2)
                nc.vector.tensor_tensor(out=qk["D"][:], in0=qk["D"][:], in1=rt[:], op=ALU.add).then_inc(S("D_qk"), 1)

            def d_vb(t):
                wait_if(dve, S("D_av"), t)
                dve.wait_ge(S("D_pv"), t + 1)
                for h in range(2):
                    rows = slice(h * SEQ, (h + 1) * SEQ)
                    to = vbd["D"][rows].rearrange("p s (v r) h a -> p (s v) r h a", r=2)[:, :, :, h, 0:HD]
                    src = EB[rows, 0:P].rearrange("p (g d) -> p g d", d=HD).unsqueeze(2).to_broadcast([SEQ, 2 * 4, 2, HD])
                    nc.vector.tensor_copy(to, src).then_inc(S("D_vb"), 1)

            def f_vb(t):
                wait_if(dve, S("F_av"), t)
                dve.wait_ge(S("F_pj"), t + 1)
                for h in range(2):
                    rows = slice(h * SEQ, (h + 1) * SEQ)
                    to = vbd["F"][rows].rearrange("p s j h a -> p (s j) h a")[:, :, h, 0:HD]
                    src = PJ[rows, 1, :].rearrange("p (j h d) -> p j h d", h=2, d=HD)[:, :, h, :]
                    nc.vector.tensor_copy(to, src).then_inc(S("F_vb"), 1)

            def arguments(k):
                def piece(t):
                    ss = SS[:].rearrange("p b (h n) -> p (b h) n", n=SEQ)
                    wait_if(dve, S(k + "_arg"), t)
                    dve.wait_ge(S(k + "_s"), t + 1)
                    nc.vector.reduce_max(hm[k][:, 0, :], ss, axis=AX).then_inc(S(k + "_max"), 1)
                    dve.wait_ge(S(k + "_max"), t + 1)
                    if k == "D":
                        nc.vector.scalar_tensor_tensor(out=hm[k][:, 1, :], in0=hm[k][:, 0, :], scalar=SC, in1=sink[:], op0=ALU.mult,
                                                       op1=ALU.add).then_inc(S("D_top"), 1)
                        dve.wait_ge(S("D_top"), t + 1)
                        nc.vector.tensor_tensor(out=hm[k][:, 2, :], in0=sink[:], in1=hm[k][:, 1, :], op=ALU.subtract).then_inc(S("D_shift"), 1)
                    else:
                        nc.vector.tensor_scalar(hm[k][:, 2, :], hm[k][:, 0, :], -SC, None, ALU.mult).then_inc(S("F_shift"), 1)
                    wait_if(dve, S(k + "_eTp"), t)
                    dve.wait_ge(S(k + "_shift"), t + 1)
                    nc.vector.scalar_tensor_tensor(out=ex[k][:], in0=ss, scalar=SC, in1=hm[k][:, 2, :].unsqueeze(2).to_broadcast([P, H, SEQ]),
                                                   op0=ALU.mult, op1=ALU.add).then_inc(S(k + "_arg"), 1)
                return piece

            def divide(k, bank):
                def piece(t):
                    av = bank[:, 0:H * AV].rearrange("p (h a) -> p h a", a=AV)
                    wait_if(dve, S(k + "_o"), t)
                    dve.wait_ge(S(k + "_av"), t + 1)
                    nc.vector.reciprocal(rec[k][:], av[:, :, HD]).then_inc(S(k + "_rec"), 1)
                    wait_if(dve, S(k + "_oTp"), t)
                    dve.wait_ge(S(k + "_rec"), t + 1)
                    nc.vector.tensor_tensor(out=o[k][:].rearrange("p (h d) -> p h d", d=HD), in0=av[:, :, 0:HD],
                                            in1=rec[k][:].unsqueeze(2).to_broadcast([P, H, HD]), op=ALU.mult).then_inc(S(k + "_o"), 1)
                return piece

            def d_x(t):
                dve.wait_ge(S("D_wo"), t + 1)
                nc.vector.tensor_tensor(out=row(t), in0=EB[:, 0:D], in1=row(t), op=ALU.add).then_inc(S("D_x"), 1)

            def e_kv(t):
                wait_if(dve, S("E_pqk"), H * t)
                wait_if(dve, S("E_keep"), t)
                dve.wait_ge(S("E_kvp"), t + 1)
                nc.vector.tensor_tensor(out=kv[:].rearrange("p k d -> p (k d)"), in0=EB[:], in1=ebkv[:], op=ALU.add).then_inc(S("E_kv"), 1)

            def e_q(t):
                if isinstance(t, int) and t == 0:
                    dve.wait_ge(S("w_in"), 16 * WEIGHTS)
                wait_if(dve, S("E_pqk"), H * t)
                dve.wait_ge(S("E_qp"), t + 1)
                nc.vector.tensor_tensor(out=q[:], in0=EB[:, 0:D], in1=ebq[:], op=ALU.add).then_inc(S("E_q"), 1)

            def et_scores(k):
                def piece(t):
                    wait_if(dve, S("E_pav"), H * t)
                    dve.wait_ge(S("E_pqk"), H * t + 4 * k + 4)
                    nc.vector.reduce_sum(sco[:, 4 * k:4 * k + 4, :], prod[:, 4 * k:4 * k + 4], axis=AX).then_inc(S("E_sc"), 1)
                return piece

            def et_shift(t):
                dve.wait_ge(S("E_sc"), 4 * t + 4)
                nc.vector.reduce_max(se[:, 0, :], sco[:], axis=AX).then_inc(S("E_max"), 1)
                dve.wait_ge(S("E_max"), t + 1)
                nc.vector.tensor_tensor(out=sco[:], in0=sco[:], in1=se[:, 0, :].unsqueeze(2).to_broadcast([P, H, H]),
                                        op=ALU.subtract).then_inc(S("E_sub"), 1)

            def et_weights(t):
                dve.wait_ge(S("E_exp"), t + 1)
                nc.vector.reduce_sum(se[:, 1, :], sco[:], axis=AX).then_inc(S("E_sum"), 1)
                dve.wait_ge(S("E_sum"), t + 1)
                nc.vector.reciprocal(se[:, 2, :], se[:, 1, :]).then_inc(S("E_rec"), 1)
                dve.wait_ge(S("E_rec"), t + 1)
                nc.vector.tensor_tensor(out=sco[:], in0=sco[:], in1=se[:, 2, :].unsqueeze(2).to_broadcast([P, H, H]),
                                        op=ALU.mult).then_inc(S("E_w"), 1)

            def et_values(k):
                def piece(t):
                    wait_if(dve, S("E_aTp"), t)
                    dve.wait_ge(S("E_pav"), H * t + 4 * k + 4)
                    nc.vector.reduce_sum(att[:].rearrange("p (h d) -> p h d", d=HD)[:, 4 * k:4 * k + 4, :], prod[:, 4 * k:4 * k + 4],
                                         axis=AX).then_inc(S("E_att"), 1)
                return piece

            def et_x(t):
                dve.wait_ge(S("E_wo"), t + 1)
                nc.vector.tensor_tensor(out=row(t), in0=EB[:, 0:D], in1=row(t), op=ALU.add).then_inc(S("E_x"), 1)
                dve.wait_ge(S("E_x"), 2 * t + 1)
                nc.vector.tensor_tensor(out=row(t), in0=row(t), in1=ebo[:], op=ALU.add).then_inc(S("E_x"), 1)

            def ft_gm(t):
                wait_if(dve, S("M_u"), 2 * t)
                dve.wait_ge(S("F_mod"), t + 1)
                nc.vector.scalar_tensor_tensor(out=gmT[:], in0=MI[0:R, P:2 * P], scalar=MOD_SCALE, in1=modT[:], op0=ALU.mult,
                                               op1=ALU.mult).then_inc(S("F_gm"), 1)

            def m_hidden(half):
                def piece(t):
                    part = hid[:, 4 * half:4 * half + 4, :].rearrange("p k n -> p (k n)")
                    dve.wait_ge(S("M_th"), 2 * t + half + 1)
                    nc.vector.scalar_tensor_tensor(out=part, in0=part, scalar=1.0, in1=GA[:], op0=ALU.add, op1=ALU.mult).then_inc(S("M_silu"), 1)
                    dve.wait_ge(S("M_u"), 2 * t + half + 1)
                    dve.wait_ge(S("M_silu"), 2 * t + half + 1)
                    nc.vector.tensor_tensor(out=part, in0=part, in1=UA[:], op=ALU.mult).then_inc(S("M_hid"), 1)
                return piece

            def m_x(t):
                dve.wait_ge(S("F_xn"), 3 * t + 3)
                dve.wait_ge(S("M_dn"), t + 1)
                nc.vector.scalar_tensor_tensor(out=row(t), in0=GA[:, 0:D], scalar=0.5, in1=row(t), op0=ALU.mult,
                                               op1=ALU.add).then_inc(S("M_x"), 1)

            dve.wait_ge(S("d_in"), 16 * D_WEIGHTS)
            dve.wait_ge(S("const"), 11)
            iterate(dve, [("Ft", arguments("F")), ("Dn", statistics("D", None, 0)), ("F", statistics("F", "E_x", 2)),
                          ("Et", et_scores(0)), ("Et", et_scores(1)), ("F", f_norm), ("Dt", divide("D", EB)), ("Et", et_scores(2)),
                          ("Et", et_scores(3)), ("Et", et_shift), ("D", d_rope), ("Et", et_weights), ("E", e_q),
                          ("Dn", normalise("D")), ("Ft", divide("F", MI)), ("M", m_hidden(0)), ("E", e_kv), ("F", f_vb),
                          ("M", m_hidden(1)), ("Dt", d_x), ("En", statistics("E", "D_x", 1)), ("D", d_vb), ("Et", et_values(0)),
                          ("Et", et_values(1)), ("Et", et_values(2)), ("Et", et_values(3)), ("D", arguments("D")),
                          ("En", normalise("E")), ("Ft", ft_gm), ("M", m_x), ("Et", et_x)])


def decoder(nc, a, x_in, out):
    with ExitStack() as ctx:
        x_sb = ctx.enter_context(nc.sbuf_tensor("x_sb", [P, TILES, D], F32))
        ident = ctx.enter_context(nc.sbuf_tensor("ident", [P, P], F32))
        x_loaded, masks_made = (ctx.enter_context(nc.semaphore(n)) for n in ("x_loaded", "masks_made"))

        held = []

        def new_sem(name):
            held.append(nc.alloc_semaphore(name=name))
            return held[-1]

        def clear_semaphores():
            nc.clear_and_free_semaphores(list(held))
            held.clear()
            nc.all_engine_barrier()

        with ExitStack() as first:
            tri = first.enter_context(nc.sbuf_tensor("tri", [P, P], F32))
            tri_strict, mask4 = (first.enter_context(nc.sbuf_tensor(n, [P, BT, P], F32)) for n in ("tri_strict", "mask4"))
            with nc.Block() as block:
                @block.sync
                def _(sp):
                    sp.dma_start(x_sb[:], x_in.rearrange("(t p) d -> p t d", p=P)).then_inc(x_loaded, 16)
                    sp.wait_ge(x_loaded, 16)

                @block.gpsimd
                def _(pool):
                    emit_masks(nc, pool, masks_made, ident, tri, tri_strict, mask4)

            linear_attention(nc, new_sem, x_sb, ident[:], tri[:], tri_strict[:], mask4[:], a["w_qk"], a["w_vg"], a["w_o"], a["w_beta"],
                             a["b_beta"], a["ln_cols"])
        clear_semaphores()
        wkv_and_experts(nc, new_sem, x_sb, ident[:], a["w_gate"], a["w_up"], a["w_down"], a["b_gate"], a["b_up"], a["b_down"],
                        a["w_router"], a["b_router"], a["ctx_in"], a["wu_cols"])
        clear_semaphores()
        layer_one(nc, new_sem, x_sb, ident[:], dict(a, out=out))


def head_tiles(w):
    rows, cols = w.shape
    return w.reshape(rows // P, P, cols // P, P).transpose(2, 1, 0, 3).reshape(cols // P, P, rows)


def attention_0_layout(np, i):
    heads = np.arange(H0 + 3) % H0
    by_channel = lambda a: a.reshape(H0, P, -1)
    qk = np.concatenate([head_tiles(i["L0_attn_Wq"]), head_tiles(i["L0_attn_Wk"]), by_channel(i["L0_attn_qconv_w"]),
                         by_channel(i["L0_attn_kconv_w"]), by_channel(i["L0_attn_qconv_b"]), by_channel(i["L0_attn_kconv_b"])], axis=2)
    vg = np.concatenate([head_tiles(i["L0_attn_Wv"]), head_tiles(i["L0_attn_Wg"])], axis=2)
    return {
        "w_qk": qk[heads], "w_vg": vg[heads], "w_o": i["L0_attn_Wo"].reshape(H0, P, D)[heads],
        "w_beta": i["L0_attn_Wb"].reshape(DC, P, H0).transpose(1, 0, 2),
        "b_beta": np.broadcast_to(i["L0_attn_bb"], (P, H0)),
        "ln_cols": np.stack([i["L0_attn_qn_w"], i["L0_attn_qn_b"], i["L0_attn_kn_w"], i["L0_attn_kn_b"]], axis=1),
    }


def experts_layout(np, i):
    gu, gub = i["L0_ffn_gate_up_proj"], i["L0_ffn_gate_up_proj_bias"]
    rows = lambda w: w.reshape(w.shape[0], DC, P, D).transpose(2, 0, 1, 3)
    cols = lambda v: v.reshape(-1, DC, P).transpose(2, 0, 1)
    return {
        "w_gate": rows(gu[:, :, 0::2]), "w_up": rows(gu[:, :, 1::2]), "w_down": rows(i["L0_ffn_down_proj"]),
        "b_gate": cols(gub[:, 0::2]), "b_up": cols(gub[:, 1::2]), "b_down": i["L0_ffn_down_proj_bias"],
        "w_router": i["L0_ffn_router_weight"].T.reshape(DC, P, -1).transpose(1, 0, 2),
        "b_router": np.broadcast_to(i["L0_ffn_router_bias"], (P, 8)),
        "ctx_in": i["ctx_2048"].reshape(TOK, D),
        "wu_cols": np.concatenate([i["L0_xattn_w"].reshape(DC, P).T, i["L0_xattn_u"].reshape(DC, P).T], axis=1),
    }


def layer_one_layout(np, i):
    heads, hd, kv_heads = 16, 16, 4
    half = hd // 2
    rows = lambda w: w.reshape(w.shape[0] // P, P, w.shape[1]).transpose(1, 0, 2)
    everywhere = lambda v: np.broadcast_to(v.reshape(1, -1), (P, v.size))
    columns = lambda v: v.reshape(DC, P).T
    h, f, j = (v.reshape(-1) for v in np.meshgrid(np.arange(heads), np.arange(2), np.arange(half), indexing="ij"))
    column = lambda head, f: head * hd + 2 * j + f
    wq, wk = i["L1_attn_wq"], i["L1_attn_wk"]
    shared = h // (heads // kv_heads)
    dwqk = np.concatenate([wq[:, column(h, f)], wk[:, column(shared, f)], wq[:, column(h, 1 - f)], wk[:, column(shared, 1 - f)]], axis=1)
    inv = 1.0 / np.float32(10000.0) ** (np.arange(half, dtype=np.float32) / half)
    angle = np.arange(SEQ, dtype=np.float32)[:, None] * inv.astype(np.float32)[None, :]
    place = np.arange(P) % SEQ
    channel = np.arange(P)
    cos, sin = (g(angle).astype(np.float32)[place][:, channel % half].T for g in (np.cos, np.sin))
    sign = np.where(channel % hd < half, -1.0, 1.0).astype(np.float32)[:, None]
    return {
        "dwqk": rows(dwqk), "dwv": rows(i["L1_attn_wv"]), "dwo": rows(i["L1_attn_wo"]),
        "rope": np.stack([cos, sign * sin], axis=1), "sink": everywhere(i["L1_attn_sink"]),
        "ewq": rows(i["L1_xattn_Wq"].T), "ewo": rows(i["L1_xattn_Wo"].T),
        "ewkv": rows(np.concatenate([i["L1_xattn_Wk"].T, i["L1_xattn_Wv"].T], axis=1)),
        "ebq": everywhere(i["L1_xattn_bq"]), "ebo": everywhere(i["L1_xattn_bo"]),
        "ebkv": everywhere(np.concatenate([i["L1_xattn_bk"], i["L1_xattn_bv"]])),
        "fwqk": rows(np.concatenate([i["L1_ffn_Wq"].T, i["L1_ffn_Wk"].T], axis=1)), "fwv": rows(i["L1_ffn_Wv"].T),
        "fwo": rows(i["L1_ffn_Wo"].T), "fa": rows(i["L1_ffn_A"]), "fb": i["L1_ffn_B"],
        "lnw": np.concatenate([columns(i["L1_ffn_ln1_w"]), columns(i["L1_ffn_ln2_w"])], axis=1),
        "headmask": (channel[:, None] // hd == np.arange(P // hd)[None, :]).astype(np.float32),
        "win": rows(i["L1_ffn_W_in_base"].T), "wup": rows(i["L1_ffn_W_up_base"].T), "wdn": rows(i["L1_ffn_W_down"].T),
    }


def kernel(**inputs):
    import numpy as _np
    import concourse.bacc as _bacc
    from concourse import mybir as _mybir
    from concourse.bass_utils import run_bass_kernel_spmd as _run

    laid = {"x_in": inputs["x"].reshape(TOK, D)}
    for layout in (attention_0_layout, experts_layout, layer_one_layout):
        laid.update(layout(_np, inputs))
    nc = _bacc.Bacc("TRN2", target_bir_lowering=False, num_devices=1)
    arrays, aps = {}, {}
    for name, a in laid.items():
        a = _np.ascontiguousarray(a)
        arrays[f"in_{name}_dram"] = a
        aps[name] = nc.dram_tensor(f"in_{name}_dram", a.shape, _mybir.dt.from_np(a.dtype), kind="ExternalInput").ap()
    out = nc.dram_tensor("out_0_dram", (TOK, D), _mybir.dt.float32, kind="ExternalOutput").ap()
    x_in = aps.pop("x_in")
    decoder(nc, aps, x_in, out)
    r = _run(nc, [arrays], core_ids=[0])
    return r.results[0]["out_0_dram"].reshape(SEQS, SEQ, D)
```
